# Optimizing a Trainium2 kernel written in Bass

```python
import numpy as np
import jax
import jax.numpy as jnp

def _softmax(x, axis=-1):
    return jax.nn.softmax(x, axis=axis)

def _gelu(x):
    return jax.nn.gelu(x, approximate=True)

def _silu(x):
    return jax.nn.silu(x)

def _sigmoid(x):
    return jax.nn.sigmoid(x)

def _layernorm(x, axis=-1, eps=1e-05):
    m = jnp.mean(x, axis=axis, keepdims=True)
    v = jnp.var(x, axis=axis, keepdims=True)
    return (x - m) / jnp.sqrt(v + eps)

def _scatter_add(tgt, idx, src, axis=0):
    return tgt.at[idx].add(src)

def _segment_sum(src, seg, n):
    return jax.ops.segment_sum(src, seg, n)
kernel_name = 'mk_xattn_ffn_d4_seqx_r8_509432'

def setup_inputs(seed: int=0):
    np.random.seed(seed)
    _w = jnp.asarray

    def _rec_inputs():
        import jax
        import jax.numpy as jnp
        _rk = jax.random.key(seed)
        x = -0.000125 + 0.9999 * jax.random.normal(jax.random.fold_in(_rk, 1), (4, 512, 128), jnp.float32)
        _lenS = 512 - jax.random.randint(jax.random.fold_in(_rk, 7), (4,), 0, max(1, 512 // 4) + 1, jnp.int32)
        _lenS2 = 77 - jax.random.randint(jax.random.fold_in(_rk, 8), (4,), 0, max(1, 77 // 4) + 1, jnp.int32)
        _ctx_1024P = jax.random.normal(jax.random.fold_in(_rk, 11), (4, 16, 128), jnp.float32)
        _ctx_1024c = jax.random.dirichlet(jax.random.fold_in(_rk, 511), 0.3 * jnp.ones((16,), jnp.float32), (4, 77))
        _ctx_1024t = jnp.einsum('bsk,bkd->bsd', _ctx_1024c, _ctx_1024P)
        _ctx_1024t = _ctx_1024t * jax.lax.rsqrt(jnp.mean(jnp.square(_ctx_1024t)) + 1e-12) * 0.953939
        ctx_1024 = -1.52775e-05 + 0.999936 * (_ctx_1024t + 0.3 * jax.random.normal(jax.random.fold_in(_rk, 611), (4, 77, 128), jnp.float32))
        _validS = jnp.arange(512)[None, :] < _lenS[:, None]
        _validS2 = jnp.arange(77)[None, :] < _lenS2[:, None]
        _causal = jnp.tril(jnp.ones((512, 512), dtype=bool))
        mask_BxS2_if1 = jnp.where(jnp.ones((4, 77), dtype=bool), 1, 0).astype(jnp.int32)
        mask_BxSxS2_ik1 = jnp.where(jnp.broadcast_to(_validS2[:, None, :], (4, 512, 77)), 1, 0).astype(jnp.int32)
        mask_Bx1xSxS2_ik1 = jnp.where(jnp.broadcast_to(_validS2[:, None, None, :], (4, 1, 512, 77)), 1, 0).astype(jnp.int32)
        return (x, ctx_1024, mask_BxS2_if1, mask_BxSxS2_ik1, mask_Bx1xSxS2_ik1)
    x, ctx_1024, mask_BxS2_if1, mask_BxSxS2_ik1, mask_Bx1xSxS2_ik1 = _rec_inputs()

    def _L0_xattn_setup():
        import jax, jax.numpy as jnp
        import numpy as np
        NEG = -10000.0
        key = jax.random.key(seed)
        k1, k2, k3 = jax.random.split(key, 3)
        B, L, D, H = (16, 256, 128, 128)
        x1 = jax.random.normal(k1, (B, L, D), dtype=jnp.float32)
        x2 = jax.random.normal(k2, (B, L, D), dtype=jnp.float32)
        x2_mask = jnp.ones((B, L), dtype=jnp.int64)
        W = jax.random.normal(k3, (H, D), dtype=jnp.float32) * (1.0 / np.sqrt(D))
        diagonal = jnp.ones((H,), dtype=jnp.float32)
        return {'x1': x1, 'x2': x2, 'x2_mask': x2_mask, 'W': W, 'diagonal': diagonal}
    _L0_xattn_all = _L0_xattn_setup()
    _L0_xattn_in = {k: v for k, v in _L0_xattn_all.items() if k in ('W', 'diagonal')}
    del _L0_xattn_all

    def _L0_ffn_setup():
        import jax, jax.numpy as jnp
        import numpy as np
        D_MODEL = 128
        MLP_DIM = 512
        N_EXPERTS = 8
        B, T = (4, 128)
        key = jax.random.key(seed)
        ks = jax.random.split(key, 7)
        scale_in = (1.0 / D_MODEL) ** 0.5
        scale_out = (1.0 / MLP_DIM) ** 0.5
        bound_g = (1.0 / D_MODEL) ** 0.5
        w_gate = jax.random.uniform(ks[0], (D_MODEL, N_EXPERTS), minval=-bound_g, maxval=bound_g, dtype=jnp.float32)
        b_gate = jax.random.uniform(ks[1], (N_EXPERTS,), minval=-bound_g, maxval=bound_g, dtype=jnp.float32)
        W1 = jax.random.uniform(ks[2], (N_EXPERTS, D_MODEL, MLP_DIM), minval=-scale_in, maxval=scale_in, dtype=jnp.float32)
        b1 = jnp.zeros((N_EXPERTS, MLP_DIM), dtype=jnp.float32)
        W2 = jax.random.uniform(ks[3], (N_EXPERTS, MLP_DIM, D_MODEL), minval=-scale_out, maxval=scale_out, dtype=jnp.float32)
        b2 = jnp.zeros((N_EXPERTS, D_MODEL), dtype=jnp.float32)
        x = jax.random.normal(ks[4], (B, T, D_MODEL), dtype=jnp.float32)
        return {'x': x, 'w_gate': w_gate, 'b_gate': b_gate, 'W1': W1, 'b1': b1, 'W2': W2, 'b2': b2}
    _L0_ffn_all = _L0_ffn_setup()
    _L0_ffn_in = {k: v for k, v in _L0_ffn_all.items() if k in ('w_gate', 'b_gate', 'W1', 'b1', 'W2', 'b2')}
    del _L0_ffn_all

    def _L1_xattn_setup():
        import jax, jax.numpy as jnp
        import numpy as np
        D_MODEL = 128
        N_HEADS = 16
        HEAD_DIM = D_MODEL // N_HEADS
        key = jax.random.key(seed)
        ks = jax.random.split(key, 10)
        B, NQ, S = (8, 64, 512)
        inv = 1.0 / np.sqrt(D_MODEL)
        inp = {'queries': jax.random.normal(ks[0], (B, NQ, D_MODEL), dtype=jnp.float32), 'context': jax.random.normal(ks[1], (B, S, D_MODEL), dtype=jnp.float32), 'wq': jax.random.normal(ks[2], (D_MODEL, D_MODEL), dtype=jnp.float32) * inv, 'bq': jnp.zeros((D_MODEL,), dtype=jnp.float32), 'wk': jax.random.normal(ks[3], (D_MODEL, D_MODEL), dtype=jnp.float32) * inv, 'bk': jnp.zeros((D_MODEL,), dtype=jnp.float32), 'wv': jax.random.normal(ks[4], (D_MODEL, D_MODEL), dtype=jnp.float32) * inv, 'bv': jnp.zeros((D_MODEL,), dtype=jnp.float32), 'wo': jax.random.normal(ks[5], (D_MODEL, D_MODEL), dtype=jnp.float32) * inv, 'bo': jnp.zeros((D_MODEL,), dtype=jnp.float32)}
        return inp
    _L1_xattn_all = _L1_xattn_setup()
    _L1_xattn_in = {k: v for k, v in _L1_xattn_all.items() if k in ('wq', 'bq', 'wk', 'bk', 'wv', 'bv', 'wo', 'bo')}
    del _L1_xattn_all

    def _L1_ffn_setup():
        import jax, jax.numpy as jnp
        import numpy as np
        BLOCK = 32
        W_BITS = 4
        ACT_BITS = 16

        def act_qdq(x):
            qmax = 2.0 ** (ACT_BITS - 1) - 1.0
            scale = jnp.maximum(jnp.max(jnp.abs(x)) / qmax, 1e-12)
            return jnp.clip(jnp.round(x / scale), -qmax - 1.0, qmax) * scale

        def fixed_qdq_u16(x):
            scale = 1.0 / 65536.0
            return jnp.clip(jnp.round(x / scale), 0.0, 65535.0) * scale

        def lpbq_dequant(w):
            O, I = w.shape
            qmax = 2.0 ** (W_BITS - 1) - 1.0
            wb = w.reshape(O, I // BLOCK, BLOCK)
            s = jnp.maximum(jnp.max(jnp.abs(wb), axis=-1, keepdims=True) / qmax, 1e-12)
            wq = jnp.clip(jnp.round(wb / s), -qmax - 1.0, qmax) * s
            return wq.reshape(O, I)
        key = jax.random.key(seed)
        k1, k2, k3, k4 = jax.random.split(key, 4)
        B, S, H, I = (2, 512, 128, 384)
        x = jax.random.normal(k1, (B, S, H), jnp.float32)
        w_gate = jax.random.normal(k2, (I, H), jnp.float32) * 0.02
        w_up = jax.random.normal(k3, (I, H), jnp.float32) * 0.02
        w_down = jax.random.normal(k4, (H, I), jnp.float32) * 0.02
        return {'x': x, 'w_gate': w_gate, 'w_up': w_up, 'w_down': w_down}
    _L1_ffn_all = _L1_ffn_setup()
    _L1_ffn_in = {k: v for k, v in _L1_ffn_all.items() if k in ('w_gate', 'w_up', 'w_down')}
    del _L1_ffn_all

    def _L2_xattn_setup():
        import jax, jax.numpy as jnp
        import numpy as np
        import math
        D_MODEL = 128
        N_HEAD = 16
        D_K = 64
        D_V = 64
        EPS = 1e-06

        def _layer_norm(x, gamma, beta, eps=EPS):
            mean = jnp.mean(x, axis=-1, keepdims=True)
            std = jnp.std(x, axis=-1, keepdims=True, ddof=1)
            return gamma * (x - mean) / (std + eps) + beta
        key = jax.random.key(seed)
        ks = jax.random.split(key, 10)
        B, S = (4, 256)
        inp = {'x_queries': jax.random.normal(ks[0], (B, S, D_MODEL), jnp.float32), 'x_keys': jax.random.normal(ks[1], (B, S, D_MODEL), jnp.float32), 'x_values': jax.random.normal(ks[2], (B, S, D_MODEL), jnp.float32), 'mask': jax.random.randint(ks[3], (B, S, S), 0, 2, jnp.int32), 'w_q': jax.random.normal(ks[4], (D_MODEL, N_HEAD * D_K), jnp.float32) * np.sqrt(2.0 / (D_MODEL + D_K)), 'w_k': jax.random.normal(ks[5], (D_MODEL, N_HEAD * D_K), jnp.float32) * np.sqrt(2.0 / (D_MODEL + D_K)), 'w_v': jax.random.normal(ks[6], (D_MODEL, N_HEAD * D_V), jnp.float32) * np.sqrt(2.0 / (D_MODEL + D_V)), 'w_0': jax.random.normal(ks[7], (N_HEAD * D_V, D_MODEL), jnp.float32) * np.sqrt(2.0 / (N_HEAD * D_V + D_MODEL)), 'gamma': jnp.ones((D_MODEL,), jnp.float32), 'beta': jnp.zeros((D_MODEL,), jnp.float32)}
        return inp
    _L2_xattn_all = _L2_xattn_setup()
    _L2_xattn_in = {k: v for k, v in _L2_xattn_all.items() if k in ('w_q', 'w_k', 'w_v', 'w_0', 'gamma', 'beta')}
    del _L2_xattn_all

    def _L2_ffn_setup():
        import jax, jax.numpy as jnp
        import numpy as np
        NUM_EXPERTS = 8
        TOP_K = 2
        CAP_RATIO = 1.25
        INIT_STD = 0.02
        key = jax.random.key(seed)
        k1, k2, k3, k4 = jax.random.split(key, 4)
        B, T, H, F = (4, 256, 128, 512)
        x = jax.random.normal(k1, (B, T, H), jnp.float32)
        router_w = jax.random.normal(k2, (NUM_EXPERTS, H), jnp.float32) * INIT_STD
        w1 = jax.random.normal(k3, (NUM_EXPERTS, H, F), jnp.float32) * INIT_STD
        w2 = jax.random.normal(k4, (NUM_EXPERTS, F, H), jnp.float32) * INIT_STD
        return {'x': x, 'router_w': router_w, 'w1': w1, 'w2': w2}
    _L2_ffn_all = _L2_ffn_setup()
    _L2_ffn_in = {k: v for k, v in _L2_ffn_all.items() if k in ('router_w', 'w1', 'w2')}
    del _L2_ffn_all

    def _L3_xattn_setup():
        import jax, jax.numpy as jnp
        import numpy as np
        HEADS = 16
        key = jax.random.key(seed)
        k1, k2, k3, k4, k5, k6 = jax.random.split(key, 6)
        N, L, E = (2, 256, 128)
        return {'values': jax.random.normal(k1, (N, L, E), dtype=jnp.float32), 'key': jax.random.normal(k2, (N, L, E), dtype=jnp.float32), 'query': jax.random.normal(k3, (N, L, E), dtype=jnp.float32), 'mask': jax.random.randint(k4, (N, 1, L, L), 0, 2, dtype=jnp.int32), 'W_out': jax.random.normal(k5, (E, E), dtype=jnp.float32) / np.sqrt(E), 'b_out': jax.random.normal(k6, (E,), dtype=jnp.float32) * 0.01}
    _L3_xattn_all = _L3_xattn_setup()
    _L3_xattn_in = {k: v for k, v in _L3_xattn_all.items() if k in ('W_out', 'b_out')}
    del _L3_xattn_all

    def _L3_ffn_setup():
        import jax, jax.numpy as jnp
        import numpy as np
        NUM_EXPERTS = 8
        TOP_K = 2
        DIM = 128
        HIDDEN = 512
        B, S = (2, 128)
        key = jax.random.key(seed)
        k_x, k_g, k_1, k_2, k_3 = jax.random.split(key, 5)
        s_d = 1.0 / np.sqrt(DIM)
        s_h = 1.0 / np.sqrt(HIDDEN)
        return {'x': jax.random.normal(k_x, (B, S, DIM), dtype=jnp.float32), 'gate_w': jax.random.normal(k_g, (NUM_EXPERTS, DIM), dtype=jnp.float32) * s_d, 'w1': jax.random.normal(k_1, (NUM_EXPERTS, HIDDEN, DIM), dtype=jnp.float32) * s_d, 'w2': jax.random.normal(k_2, (NUM_EXPERTS, DIM, HIDDEN), dtype=jnp.float32) * s_h, 'w3': jax.random.normal(k_3, (NUM_EXPERTS, HIDDEN, DIM), dtype=jnp.float32) * s_d}
    _L3_ffn_all = _L3_ffn_setup()
    _L3_ffn_in = {k: v for k, v in _L3_ffn_all.items() if k in ('gate_w', 'w1', 'w2', 'w3')}
    del _L3_ffn_all
    return {'x': x, 'ctx_1024': ctx_1024, 'mask_BxS2_if1': mask_BxS2_if1, 'mask_BxSxS2_ik1': mask_BxSxS2_ik1, 'mask_Bx1xSxS2_ik1': mask_Bx1xSxS2_ik1, 'L0_xattn_W': _L0_xattn_in['W'], 'L0_xattn_diagonal': _L0_xattn_in['diagonal'], 'L0_ffn_w_gate': _L0_ffn_in['w_gate'], 'L0_ffn_b_gate': _L0_ffn_in['b_gate'], 'L0_ffn_W1': _L0_ffn_in['W1'], 'L0_ffn_b1': _L0_ffn_in['b1'], 'L0_ffn_W2': _L0_ffn_in['W2'], 'L0_ffn_b2': _L0_ffn_in['b2'], 'L1_xattn_wq': _L1_xattn_in['wq'], 'L1_xattn_bq': _L1_xattn_in['bq'], 'L1_xattn_wk': _L1_xattn_in['wk'], 'L1_xattn_bk': _L1_xattn_in['bk'], 'L1_xattn_wv': _L1_xattn_in['wv'], 'L1_xattn_bv': _L1_xattn_in['bv'], 'L1_xattn_wo': _L1_xattn_in['wo'], 'L1_xattn_bo': _L1_xattn_in['bo'], 'L1_ffn_w_gate': _L1_ffn_in['w_gate'], 'L1_ffn_w_up': _L1_ffn_in['w_up'], 'L1_ffn_w_down': _L1_ffn_in['w_down'], 'L2_xattn_w_q': _L2_xattn_in['w_q'], 'L2_xattn_w_k': _L2_xattn_in['w_k'], 'L2_xattn_w_v': _L2_xattn_in['w_v'], 'L2_xattn_w_0': _L2_xattn_in['w_0'], 'L2_xattn_gamma': _L2_xattn_in['gamma'], 'L2_xattn_beta': _L2_xattn_in['beta'], 'L2_ffn_router_w': _L2_ffn_in['router_w'], 'L2_ffn_w1': _L2_ffn_in['w1'], 'L2_ffn_w2': _L2_ffn_in['w2'], 'L3_xattn_W_out': _L3_xattn_in['W_out'], 'L3_xattn_b_out': _L3_xattn_in['b_out'], 'L3_ffn_gate_w': _L3_ffn_in['gate_w'], 'L3_ffn_w1': _L3_ffn_in['w1'], 'L3_ffn_w2': _L3_ffn_in['w2'], 'L3_ffn_w3': _L3_ffn_in['w3']}

def reference(x, ctx_1024, mask_BxS2_if1, mask_BxSxS2_ik1, mask_Bx1xSxS2_ik1, L0_xattn_W, L0_xattn_diagonal, L0_ffn_w_gate, L0_ffn_b_gate, L0_ffn_W1, L0_ffn_b1, L0_ffn_W2, L0_ffn_b2, L1_xattn_wq, L1_xattn_bq, L1_xattn_wk, L1_xattn_bk, L1_xattn_wv, L1_xattn_bv, L1_xattn_wo, L1_xattn_bo, L1_ffn_w_gate, L1_ffn_w_up, L1_ffn_w_down, L2_xattn_w_q, L2_xattn_w_k, L2_xattn_w_v, L2_xattn_w_0, L2_xattn_gamma, L2_xattn_beta, L2_ffn_router_w, L2_ffn_w1, L2_ffn_w2, L3_xattn_W_out, L3_xattn_b_out, L3_ffn_gate_w, L3_ffn_w1, L3_ffn_w2, L3_ffn_w3):
    import jax
    import jax.numpy as jnp

    def _L0_xattn_ref(x1, x2, x2_mask, W, diagonal):
        import jax, jax.numpy as jnp
        import numpy as np
        NEG = -10000.0
        x1_rep = jax.nn.relu(jnp.einsum('bld,hd->blh', x1, W))
        x2_rep = jax.nn.relu(jnp.einsum('bld,hd->blh', x2, W))
        scores = jnp.einsum('bih,bjh->bij', x1_rep * diagonal, x2_rep)
        m = (1.0 - x2_mask.astype(scores.dtype)) * NEG
        alpha = jax.nn.softmax(scores + m[:, None, :], axis=-1)
        return jnp.einsum('bij,bjd->bid', alpha, x2)

    def _L0_ffn_ref(x, w_gate, b_gate, W1, b1, W2, b2):
        import jax, jax.numpy as jnp
        import numpy as np
        D_MODEL = 128
        MLP_DIM = 512
        N_EXPERTS = 8
        B, T = (4, 128)
        b, t, d = x.shape
        x_flat = x.reshape(b * t, d)
        logits = x_flat @ w_gate + b_gate
        probs = jax.nn.softmax(logits, axis=-1)
        route_p = jnp.max(probs, axis=-1)
        route_idx = jnp.argmax(probs, axis=-1)
        h = jnp.einsum('nd,edm->enm', x_flat, W1) + b1[:, None, :]
        h = jax.nn.relu(h)
        y = jnp.einsum('enm,emd->end', h, W2) + b2[:, None, :]
        n = b * t
        out = y[route_idx, jnp.arange(n)] * route_p[:, None]
        return out.reshape(b, t, d)

    def _L1_xattn_ref(queries, context, wq, bq, wk, bk, wv, bv, wo, bo):
        import jax, jax.numpy as jnp
        import numpy as np
        D_MODEL = 128
        N_HEADS = 16
        HEAD_DIM = D_MODEL // N_HEADS
        B, NQ, D = queries.shape
        S = context.shape[1]
        H, HD = (N_HEADS, HEAD_DIM)
        scale = HD ** (-0.5)
        q = queries @ wq.T + bq
        k = context @ wk.T + bk
        v = context @ wv.T + bv
        q = q.reshape(B, NQ, H, HD).transpose(0, 2, 1, 3)
        k = k.reshape(B, S, H, HD).transpose(0, 2, 1, 3)
        v = v.reshape(B, S, H, HD).transpose(0, 2, 1, 3)
        attn = jnp.einsum('bhnd,bhsd->bhns', q, k) * scale
        attn = jax.nn.softmax(attn, axis=-1)
        out = jnp.einsum('bhns,bhsd->bhnd', attn, v)
        out = out.transpose(0, 2, 1, 3).reshape(B, NQ, D)
        return out @ wo.T + bo

    def _L1_ffn_ref(x, w_gate, w_up, w_down):
        import jax, jax.numpy as jnp
        import numpy as np
        BLOCK = 32
        W_BITS = 4
        ACT_BITS = 16

        def act_qdq(x):
            qmax = 2.0 ** (ACT_BITS - 1) - 1.0
            scale = jnp.maximum(jnp.max(jnp.abs(x)) / qmax, 1e-12)
            return jnp.clip(jnp.round(x / scale), -qmax - 1.0, qmax) * scale

        def fixed_qdq_u16(x):
            scale = 1.0 / 65536.0
            return jnp.clip(jnp.round(x / scale), 0.0, 65535.0) * scale

        def lpbq_dequant(w):
            O, I = w.shape
            qmax = 2.0 ** (W_BITS - 1) - 1.0
            wb = w.reshape(O, I // BLOCK, BLOCK)
            s = jnp.maximum(jnp.max(jnp.abs(wb), axis=-1, keepdims=True) / qmax, 1e-12)
            wq = jnp.clip(jnp.round(wb / s), -qmax - 1.0, qmax) * s
            return wq.reshape(O, I)
        x = act_qdq(x)
        up = act_qdq(x @ lpbq_dequant(w_up).T)
        gate = act_qdq(x @ lpbq_dequant(w_gate).T)
        sig = fixed_qdq_u16(jax.nn.sigmoid(gate))
        gate = act_qdq(gate * sig)
        o = act_qdq(gate * up)
        return o @ lpbq_dequant(w_down).T

    def _L2_xattn_ref(x_queries, x_keys, x_values, mask, w_q, w_k, w_v, w_0, gamma, beta):
        import jax, jax.numpy as jnp
        import numpy as np
        import math
        D_MODEL = 128
        N_HEAD = 16
        D_K = 64
        D_V = 64
        EPS = 1e-06

        def _layer_norm(x, gamma, beta, eps=EPS):
            mean = jnp.mean(x, axis=-1, keepdims=True)
            std = jnp.std(x, axis=-1, keepdims=True, ddof=1)
            return gamma * (x - mean) / (std + eps) + beta
        B, Lq, _ = x_queries.shape
        residual = x_queries
        Q = (x_queries @ w_q).reshape(B, Lq, N_HEAD, D_K)
        K = (x_keys @ w_k).reshape(B, x_keys.shape[1], N_HEAD, D_K)
        V = (x_values @ w_v).reshape(B, x_values.shape[1], N_HEAD, D_V)
        scores = jnp.einsum('bqhd,bkhd->bhqk', Q, K) / math.sqrt(D_K)
        scores = jnp.where(mask[:, None, :, :] == 0, EPS, scores)
        attn = jax.nn.softmax(scores, axis=-1)
        out = jnp.einsum('bhqk,bkhd->bqhd', attn, V).reshape(B, Lq, N_HEAD * D_V)
        out = out @ w_0
        return _layer_norm(out + residual, gamma, beta)

    def _L2_ffn_ref(x, router_w, w1, w2):
        import jax, jax.numpy as jnp
        import numpy as np
        NUM_EXPERTS = 8
        TOP_K = 2
        CAP_RATIO = 1.25
        INIT_STD = 0.02
        B, T, H = x.shape
        E, K = (NUM_EXPERTS, TOP_K)
        xf = x.reshape(-1, H)
        N = xf.shape[0]
        P = N * K
        capacity = int(CAP_RATio * N * K / E) + 1 if False else int(CAP_RATIO * N * K / E) + 1
        logits = xf @ router_w.T
        probs = jax.nn.softmax(logits, axis=-1)
        k_probs, k_idx = jax.lax.top_k(probs, K)
        k_probs = k_probs / jnp.sum(k_probs, axis=-1, keepdims=True)
        flat_e = k_idx.reshape(-1)
        onehot = jax.nn.one_hot(flat_e, E, dtype=jnp.int32)
        rank = jnp.take_along_axis(jnp.cumsum(onehot, axis=0) - 1, flat_e[:, None], axis=1)[:, 0]
        keep = rank < capacity
        slot = jnp.minimum(rank, capacity - 1)
        token_id = jnp.arange(P) // K
        dispatched = jnp.where(keep[:, None], xf[token_id], 0.0)
        buf = jnp.zeros((E, capacity, H), x.dtype).at[flat_e, slot].add(dispatched)
        h = jax.nn.silu(jnp.einsum('ech,ehf->ecf', buf, w1))
        out_buf = jnp.einsum('ecf,efh->ech', h, w2)
        pair_out = out_buf[flat_e, slot] * keep[:, None].astype(x.dtype)
        combined = jnp.sum(pair_out.reshape(N, K, H) * k_probs[..., None], axis=1)
        return combined.reshape(B, T, H) + x

    def _L3_xattn_ref(values, key, query, mask, W_out, b_out):
        import jax, jax.numpy as jnp
        import numpy as np
        HEADS = 16
        N, Lq, E = query.shape
        Lk = key.shape[1]
        H = HEADS
        D = E // H
        q = query.reshape(N, Lq, H, D)
        k = key.reshape(N, Lk, H, D)
        v = values.reshape(N, Lk, H, D)
        energy = jnp.einsum('nqhd,nkhd->nhqk', q, k)
        energy = jnp.where(mask == 0, jnp.float32(-1e+20), energy)
        attn = jax.nn.softmax(energy / np.float32(np.sqrt(D)), axis=3)
        out = jnp.einsum('nhqk,nkhd->nqhd', attn, v).reshape(N, Lq, H * D)
        return out @ W_out.T + b_out

    def _L3_ffn_ref(x, gate_w, w1, w2, w3):
        import jax, jax.numpy as jnp
        import numpy as np
        NUM_EXPERTS = 8
        TOP_K = 2
        DIM = 128
        HIDDEN = 512
        B, S = (2, 128)
        orig_shape = x.shape
        xt = x.reshape(-1, orig_shape[-1])
        scores = xt @ gate_w.T
        top_vals, top_idx = jax.lax.top_k(scores, TOP_K)
        top_w = jax.nn.softmax(top_vals, axis=-1)
        combine = jnp.einsum('tke,tk->te', jax.nn.one_hot(top_idx, NUM_EXPERTS, dtype=xt.dtype), top_w)
        h = jax.nn.silu(jnp.einsum('td,ehd->eth', xt, w1)) * jnp.einsum('td,ehd->eth', xt, w3)
        ye = jnp.einsum('eth,edh->etd', h, w2)
        y = jnp.einsum('te,etd->td', combine, ye)
        return y.reshape(orig_shape)
    x = x + _L0_xattn_ref(_layernorm(x, axis=-1), ctx_1024, mask_BxS2_if1, L0_xattn_W, L0_xattn_diagonal)
    x = x + _L0_ffn_ref(_layernorm(x, axis=-1), L0_ffn_w_gate, L0_ffn_b_gate, L0_ffn_W1, L0_ffn_b1, L0_ffn_W2, L0_ffn_b2)
    x = x + _L1_xattn_ref(_layernorm(x, axis=-1), ctx_1024, L1_xattn_wq, L1_xattn_bq, L1_xattn_wk, L1_xattn_bk, L1_xattn_wv, L1_xattn_bv, L1_xattn_wo, L1_xattn_bo)
    x = x + _L1_ffn_ref(_layernorm(x, axis=-1), L1_ffn_w_gate, L1_ffn_w_up, L1_ffn_w_down)
    x = x + _L2_xattn_ref(_layernorm(x, axis=-1), ctx_1024, ctx_1024, mask_BxSxS2_ik1, L2_xattn_w_q, L2_xattn_w_k, L2_xattn_w_v, L2_xattn_w_0, L2_xattn_gamma, L2_xattn_beta)
    x = x + _L2_ffn_ref(_layernorm(x, axis=-1), L2_ffn_router_w, L2_ffn_w1, L2_ffn_w2)
    x = x + _L3_xattn_ref(ctx_1024, ctx_1024, _layernorm(x, axis=-1), mask_Bx1xSxS2_ik1, L3_xattn_W_out, L3_xattn_b_out)
    x = x + _L3_ffn_ref(_layernorm(x, axis=-1), L3_ffn_gate_w, L3_ffn_w1, L3_ffn_w2, L3_ffn_w3)
    return x

_drawn_inputs = setup_inputs


def setup_inputs(seed=0):
    import zlib

    import numpy as np

    out = dict(_drawn_inputs(seed))
    spreads = {'L0_xattn_diagonal': (1.0, 0.2),
     'L0_ffn_b1': (0.0, 0.8),
     'L0_ffn_b2': (0.0, 0.447),
     'L1_xattn_bq': (0.0, 0.408),
     'L1_xattn_bk': (0.0, 2.0),
     'L1_xattn_bv': (0.0, 0.1),
     'L1_xattn_bo': (0.0, 0.1),
     'L2_xattn_gamma': (1.0, 0.2),
     'L2_xattn_beta': (0.0, 0.308)}
    factors = {'L0_ffn_b_gate': 5.941,
     'L1_ffn_w_gate': 7.285,
     'L1_ffn_w_up': 7.394,
     'L1_ffn_w_down': 6.769,
     'L2_ffn_router_w': 5.678,
     'L2_ffn_w1': 4.767,
     'L2_ffn_w2': 4.731,
     'L3_xattn_b_out': 33.687}
    for name, (base, spread) in spreads.items():
        noise = np.random.default_rng([zlib.crc32(name.encode()), seed]).standard_normal(out[name].shape)
        drawn = base * np.exp(spread * noise) if base else spread * noise
        out[name] = jnp.asarray(drawn.astype(out[name].dtype))
    for name, factor in factors.items():
        out[name] = (out[name] * factor).astype(out[name].dtype)
    return out
```

```python
from contextlib import ExitStack

import numpy as np

import concourse.bass as bass
from concourse import mybir

F32 = mybir.dt.float32
BF16 = mybir.dt.bfloat16
I32 = mybir.dt.int32
U32 = mybir.dt.uint32
ALU = mybir.AluOpType
ACT = mybir.ActivationFunctionType
AX = mybir.AxisListType
RED = bass.bass_isa.ReduceOp

P = 128
D = 128
B, S, J = 4, 512, 77
N = B * S
NT = N // P
TB = NT // B
BANK = 512
H = 16
HD = D // H
HJ = H * J
QH = H // 4
QJ = QH * J
E = 8
F = 512
FC = F // P
LN_EPS = 1e-5
MASKED = -1e20
MAGIC = 1.5 * 2.0 ** 23

class Chunk:
    def __init__(self, at):
        self.at, self.width = at, min(P, HJ - at)
        self.row, self.h0 = at % J, at // J
        self.heads = (at + self.width - 1) // J - self.h0 + 1


CHUNKS = [Chunk(at) for at in range(0, HJ, P)]
NC = len(CHUNKS)
CH = max(c.heads for c in CHUNKS)
GROUPS = [range(g, min(g + 4, NC)) for g in range(0, NC, 4)]
NG = len(GROUPS)


class Machine:
    pass


def ge(eng, sem, value):
    if not (isinstance(value, int) and value <= 0):
        eng.wait_ge(sem, value)


class Chain:

    def __init__(self, sem):
        self.sem, self.n = sem, 0

    def __call__(self, ins):
        ins.then_inc(self.sem, 1)
        self.n = self.n + 1
        return self.n

    def wait(self, eng):
        ge(eng, self.sem, self.n)


class Fetch:

    def __init__(self, sem):
        self.sem, self.n = sem, 0

    def __call__(self, ins):
        ins.then_inc(self.sem, 16)
        self.n = self.n + 1

    def wait(self, eng):
        eng.wait_ge(self.sem, 16 * self.n)


def layer_norm(nc, m, k, loads=None):
    with nc.Block() as block:
        if loads is not None:
            @block.sync
            def _(sp):
                loads(sp)

        @block.vector
        def _(dve):
            for i in range(NT):
                m.dve(dve.bn_stats(m.stats[:, i, :], m.x[:, i, :]))
            m.dve.wait(dve)
            for i in range(NT):
                m.dve(dve.bn_aggr(m.mv[:, i, :], m.stats[:, i, :]))
            m.dve.wait(dve)
            dve.tensor_scalar(m.var[:, :], m.mv[:, :, 1], LN_EPS, None, ALU.add).then_inc(m.ln_var, 1)
            dve.wait_ge(m.ln_std, k + 1)
            m.dve(dve.reciprocal(m.rstd[:, :], m.std[:, :]))
            m.dve.wait(dve)
            m.dve(dve.scalar_tensor_tensor(m.nmr[:, :], m.mv[:, :, 0], -1.0, m.rstd[:, :], ALU.mult, ALU.mult))
            m.dve.wait(dve)
            for i in range(NT):
                dve.tensor_scalar(m.xn[:, i, :], m.x[:, i, :], m.rstd[:, i:i + 1], m.nmr[:, i:i + 1],
                                  ALU.mult, ALU.add).then_inc(m.ln_xn, 1)
            for q in (1, 3):
                dve.wait_ge(m.ln_turned, 4 * k + q + 1)
                dve.tensor_copy(m.xnT[:, q * BANK:(q + 1) * BANK], m.ps[q][:, :]).then_inc(m.ln_copied, 1)

        @block.scalar
        def _(act):
            act.wait_ge(m.ln_var, k + 1)
            act.activation(m.std[:, :], m.var[:, :], ACT.Sqrt).then_inc(m.ln_std, 1)
            for q in (0, 2):
                act.wait_ge(m.ln_turned, 4 * k + q + 1)
                act.copy(m.xnT[:, q * BANK:(q + 1) * BANK], m.ps[q][:, :]).then_inc(m.ln_copied, 1)

        @block.tensor
        def _(pe):
            for i in range(NT):
                pe.wait_ge(m.ln_xn, NT * k + i + 1)
                ins = pe.transpose(m.ps[i // 4][:, i % 4 * P:i % 4 * P + P], m.xn[:, i, :], m.ident[:, :])
                if i % 4 == 3:
                    ins.then_inc(m.ln_turned, 1)


def load(nc, m, a):
    with nc.Block() as block:
        @block.sync
        def _(sp):
            sp.dma_start(m.x[:, :, :], a["x"].rearrange("b (i p) d -> p (b i) d", p=P)).then_inc(m.loaded, 16)
            sp.dma_start(m.ident[:, :], a["ident"]).then_inc(m.loaded, 16)
            sp.dma_start(m.ctxT[:, :, :], a["ctxT"]).then_inc(m.loaded, 16)
            for r in range(3):
                sp.dma_start(m.ctxT3[:, :, r * J:(r + 1) * J], a["ctxT"]).then_inc(m.loaded, 16)
            for name, tile in m.given.items():
                sp.dma_start(tile[:, :], a[name]).then_inc(m.loaded, 16)
            sp.wait_ge(m.loaded, 16 * (6 + len(m.given)))

        @block.vector
        def _(dve):
            m.dve(dve.memset(m.ones1[:, :], 1.0))
            dve.wait_ge(m.loaded, 16 * (6 + len(m.given)))
            for name in m.narrow:
                m.dve(dve.tensor_copy(m.small[name][:, :], m.given[name][:, :]))
            m.dve.wait(dve)


def attention0(nc, m, a, sem, sb):
    yield None
    kT = sb("a0_kT", [P, B, J])
    ctxv = sb("a0_ctxv", [J, B, D + 1])
    madd = sb("a0_madd", [1, B * J])
    maski = sb("a0_maski", [1, B * J], I32)
    qT = sb("a0_qT", [P, N])
    pr = sb("a0_pr", [P, B, TB, J])
    prT = sb("a0_prT", [J, N])
    mx = sb("a0_mx", [P, B, TB])
    rden = sb("a0_rden", [P, NT])
    ctx_loaded, k_ready, k_done, bias_done, q_ready, q_done, s_ready, sub_done, exp_done, t_ready, t_done, o_ready, x_done = (
        sem("a0_" + n) for n in ("ctx_loaded", "k_ready", "k_done", "bias_done", "q_ready", "q_done", "s_ready", "sub_done",
                                 "exp_done", "t_ready", "t_done", "o_ready", "x_done"))

    with nc.Block() as block:
        @block.sync
        def _(sp):
            sp.dma_start(ctxv[:, :, 0:D], a["ctx"].rearrange("b j d -> j b d")).then_inc(ctx_loaded, 16)
            sp.dma_start(maski[:, :], a["mask0"].rearrange("b j -> (b j)").unsqueeze(0)).then_inc(ctx_loaded, 16)

        @block.tensor
        def _(pe):
            pe.matmul(m.ps[7][:, 0:B * J], m.w0T[:, :], m.ctxT[:, :, :], start=True, stop=True).then_inc(k_ready, 1)
            for s in range(B + 3):
                if s < B:
                    ge(pe, q_done, s - 1)
                    pe.matmul(m.ps[s % 2][:, :], m.w0T[:, :], m.xnT[:, s * S:(s + 1) * S],
                              start=True, stop=True).then_inc(q_ready, 1)
                if 1 <= s <= B:
                    b = s - 1
                    pe.wait_ge(q_done, b + 1)
                    if b == 0:
                        pe.wait_ge(k_done, 1)
                        pe.wait_ge(bias_done, 1)
                    ge(pe, sub_done, b - 1)
                    for t in range(TB):
                        o = m.ps[2 + b % 2][:, t * J:(t + 1) * J]
                        pe.matmul(o, qT[:, (b * TB + t) * P:(b * TB + t + 1) * P], kT[:, b, :], start=True, stop=False)
                        ins = pe.matmul(o, m.ones1[0:1, :], madd[:, b * J:(b + 1) * J], start=False, stop=True)
                    ins.then_inc(s_ready, 1)
                if 2 <= s <= B + 1:
                    b = s - 2
                    pe.wait_ge(exp_done, b + 1)
                    ge(pe, t_done, b - 1)
                    for t in range(TB):
                        ins = pe.transpose(m.ps[(4, 7)[b % 2]][0:J, t * P:(t + 1) * P], pr[:, b, t, :], m.ident[:, :])
                    ins.then_inc(t_ready, 1)
                if 3 <= s:
                    b = s - 3
                    pe.wait_ge(t_done, b + 1)
                    ge(pe, x_done, b)
                    if b == 0:
                        pe.wait_ge(ctx_loaded, 32)
                    for t in range(TB):
                        i = b * TB + t
                        ins = pe.matmul(m.ps[5 + t // 2][:, t % 2 * 129:t % 2 * 129 + 129], prT[:, i * P:(i + 1) * P],
                                        ctxv[:, b, :], start=True, stop=True)
                    ins.then_inc(o_ready, 1)

        @block.vector
        def _(dve):
            m.dve(dve.memset(ctxv[:, :, D:D + 1], 1.0))
            dve.wait_ge(k_ready, 1)
            dve.tensor_scalar(kT[:, :, :], m.ps[7][:, 0:B * J].rearrange("p (b j) -> p b j", b=B), 0.0, m.diag0[:, 0:1],
                              ALU.max, ALU.mult).then_inc(k_done, 1)
            dve.wait_ge(ctx_loaded, 32)
            dve.tensor_scalar(madd[:, :], maski[:, :], 10000.0, -10000.0, ALU.mult, ALU.add).then_inc(bias_done, 1)
            m.dve.wait(dve)
            for s in range(B + 3):
                if s < B:
                    dve.wait_ge(q_ready, s + 1)
                    dve.tensor_scalar(qT[:, s * S:(s + 1) * S], m.ps[s % 2][:, :], 0.0, None, ALU.max).then_inc(q_done, 1)
                if 1 <= s <= B:
                    b = s - 1
                    dve.wait_ge(s_ready, b + 1)
                    sc = m.ps[2 + b % 2][:, 0:TB * J].rearrange("p (t j) -> p t j", t=TB)
                    m.dve(dve.tensor_reduce(mx[:, b, :], sc, AX.X, ALU.max))
                    m.dve.wait(dve)
                    dve.tensor_tensor(pr[:, b, :, :], sc, mx[:, b, :].unsqueeze(2).broadcast_to([P, TB, J]),
                                      ALU.subtract).then_inc(sub_done, 1)
                if 3 <= s:
                    b = s - 3
                    dve.wait_ge(o_ready, b + 1)
                    for t in range(TB):
                        i = b * TB + t
                        m.dve(dve.reciprocal(rden[:, i:i + 1], m.ps[5 + t // 2][:, t % 2 * 129 + 128:t % 2 * 129 + 129]))
                    m.dve.wait(dve)
                    for t in range(TB):
                        i = b * TB + t
                        ins = dve.scalar_tensor_tensor(m.x[:, i, :], m.ps[5 + t // 2][:, t % 2 * 129:t % 2 * 129 + 128],
                                                       rden[:, i:i + 1], m.x[:, i, :], ALU.mult, ALU.add)
                        m.dve(ins)
                    m.dve.wait(dve)
                    dve.sem_inc(x_done, 1)

        @block.scalar
        def _(act):
            for s in range(1, B + 2):
                if s <= B:
                    b = s - 1
                    act.wait_ge(sub_done, b + 1)
                    act.activation(pr[:, b, :, :], pr[:, b, :, :], ACT.Exp).then_inc(exp_done, 1)
                if s >= 2:
                    b = s - 2
                    act.wait_ge(t_ready, b + 1)
                    act.copy(prT[:, b * S:(b + 1) * S], m.ps[(4, 7)[b % 2]][0:J, :]).then_inc(t_done, 1)


def moe(nc, m, a, sem, sb, name, blocks, topk, cap, biased, gated, act_fn, x_stage):
    G, k = blocks, topk
    Q = k * NT
    U = 8
    assert G % U == 0
    w1 = sb(name + "_w1", [P, E, F])
    w2 = sb(name + "_w2", [P, E, FC, D])
    w3 = sb(name + "_w3", [P, E, F]) if gated else None
    b1 = sb(name + "_b1", [P, E, F]) if biased else None
    b2 = sb(name + "_b2", [P, E, D]) if biased else None
    weights = [("w1", w1), ("w2", w2)] + ([("w3", w3)] if gated else []) + ([("b1", b1), ("b2", b2)] if biased else [])

    def loads(sp):
        for n, t in weights:
            dst = t[:, :, :, :].rearrange("p e c d -> p e (c d)") if n == "w2" else t[:, :, :]
            for half in (slice(0, E // 2), slice(E // 2, E)):
                m.fetch(sp.dma_start(dst[:, half, :], a[f"{name}_{n}"][half, :, :].rearrange("e p f -> p e f")))

    yield loads
    fetched = m.fetch.n

    (logits_ready, shifted, exped, sel_ready, rank_ready, slots_known, index_ready, index_done, table_ready, xn_out,
     xT_ready, xT_done, h_ready, h_act, h_done, hT_ready, hT_done, y_ready, y_done, gnow_done, snow_done, pool_pass) = (
        sem(f"{name}_{n}") for n in (
        "logits_ready", "shifted", "exped", "sel_ready", "rank_ready", "slots_known", "index_ready", "index_done",
        "table_ready", "xn_out", "xT_ready", "xT_done", "h_ready", "h_act", "h_done", "hT_ready", "hT_done",
        "y_ready", "y_done", "gnow_done", "snow_done", "pool_pass"))
    x_in, scattered = ([sem(f"{name}_{n}{sl}") for sl in range(U)] for n in ("x_in", "scattered"))
    back_in = [sem(f"{name}_back_in{q}") for q in range(B)]
    bt = lambda ap: ap.unsqueeze(1).broadcast_to([P, NT, E])
    be = lambda ap: ap.unsqueeze(2).broadcast_to([P, NT, E])
    wt = [sb(f"{name}_wt{i}", [P, NT]) for i in range(k)]
    btabi = sb(name + "_btabi", [1, G], I32)
    gidx = sb(name + "_gidx", [P, G], U32)
    sidx = sb(name + "_sidx", [P, G], U32)
    pairs_in, pairs_out = a["pairs_in"][0:Q * P, :], a[f"{name}_pairs_out"]

    with ExitStack() as inner:
        tp = lambda n, shape, dt=F32: inner.enter_context(nc.sbuf_tensor(f"{name}_{n}", shape, dt))
        lg, l2 = tp("lg", [P, NT, E]), tp("l2", [P, NT, E])
        tmp = [tp(f"tmp{i}", [P, NT, E]) for i in range(2)]
        oh = [tp(f"oh{i}", [P, NT, E]) for i in range(k)]
        top = [tp(f"top{i}", [P, NT]) for i in range(k)]
        low, den = tp("low", [P, NT]), tp("den", [P, NT])
        dif, ex = (tp(n, [P, NT, E] if k == 1 else [P, NT]) for n in ("dif", "ex"))
        sel = tp("sel", [P, NT, E], BF16)
        tot, run, over = (tp(n, [P, E, NT]) for n in ("tot", "run", "over"))
        rank, keep = tp("rank", [P, NT, E]), tp("keep", [P, NT, E])
        cnt, nblk, bend, base = (tp(n, [P, E]) for n in ("cnt", "nblk", "bend", "base"))
        pos = tp("pos", [P, k, NT])
        kept = tp("kept", [P, NT])
        div, mod = tp("div", [P, Q]), tp("mod", [P, Q])
        rowhot = tp("rowhot", [P, Q, P], BF16)
        blkhot = tp("blkhot", [P, Q, G], BF16)
        code = tp("code", [P, Q, 2, G], BF16)
        found, ffree = tp("found", [P, G]), tp("ffree", [P, G])
        cmpt, btab = tp("cmpt", [1, G, E]), tp("btab", [1, G])

        with nc.Block() as block:
            @block.sync
            def _(sp):
                for j in range(k):
                    sp.dma_start(pairs_in[j * N:(j + 1) * N, :].rearrange("(i p) d -> p i d", p=P), m.xn[:, :, :]).then_inc(xn_out, 16)
                sp.wait_ge(xn_out, 16 * k)

            @block.tensor
            def _(pe):
                for i in range(NT):
                    ins = pe.matmul(m.ps[0][:, i * E:(i + 1) * E], m.xnT[:, i * P:(i + 1) * P], m.small[name + "_router"][:, :],
                                    start=True, stop=True)
                ins.then_inc(logits_ready, 1)
                pe.wait_ge(sel_ready, 1)
                pe.matmul(m.ps[1][:, 0:P], m.tri[:, :], sel[:, :, :], start=True, stop=True)
                pe.matmul(m.ps[2][:, 0:P], m.onesb[:, :], sel[:, :, :], start=True, stop=True).then_inc(rank_ready, 1)
                for q in range(Q):
                    pe.wait_ge(slots_known, q // NT + 1)
                    ins = pe.matmul(m.ps[3][:, 0:2 * G], rowhot[:, q, :], code[:, q, :, :], start=(q == 0), stop=(q == Q - 1))
                ins.then_inc(index_ready, 1)

            @block.scalar
            def _(act):
                act.wait_ge(shifted, 1)
                sl = tuple([slice(None)] * len(dif.shape))
                act.activation(ex[sl], dif[sl], ACT.Exp).then_inc(exped, 1)

            @block.vector
            def _(dve):
                c = m.dve

                def step(ins):
                    c(ins)
                    c.wait(dve)

                dve.wait_ge(logits_ready, 1)
                logits = m.ps[0][:, 0:NT * E].rearrange("p (i e) -> p i e", e=E)
                if biased:
                    step(dve.tensor_tensor(lg[:, :, :], logits, bt(m.small[name + "_rbias"][:, :]), ALU.add))
                else:
                    step(dve.tensor_copy(lg[:, :, :], logits))
                src = lg
                for j in range(k):
                    step(dve.tensor_reduce(top[j][:, :], src[:, :, :], AX.X, ALU.max))
                    step(dve.tensor_tensor(tmp[0][:, :, :], src[:, :, :], be(top[j][:, :]), ALU.is_equal))
                    step(dve.scalar_tensor_tensor(tmp[1][:, :, :], tmp[0][:, :, :], -float(E), bt(m.iota8[:, :]), ALU.mult, ALU.add))
                    step(dve.tensor_reduce(low[:, :], tmp[1][:, :, :], AX.X, ALU.min))
                    step(dve.scalar_tensor_tensor(oh[j][:, :, :], bt(m.iota8[:, :]), -float(E), be(low[:, :]), ALU.add, ALU.is_equal))
                    if j + 1 < k:
                        step(dve.scalar_tensor_tensor(l2[:, :, :], oh[j][:, :, :], -1e30, lg[:, :, :], ALU.mult, ALU.add))
                        src = l2
                if k == 1:
                    dve.tensor_tensor(dif[:, :, :], lg[:, :, :], be(top[0][:, :]), ALU.subtract).then_inc(shifted, 1)
                    dve.tensor_copy(sel[:, :, :], oh[0][:, :, :]).then_inc(sel_ready, 1)
                    dve.wait_ge(exped, 1)
                    step(dve.tensor_reduce(den[:, :], ex[:, :, :], AX.X, ALU.add))
                    step(dve.reciprocal(wt[0][:, :], den[:, :]))
                else:
                    dve.tensor_tensor(dif[:, :], top[1][:, :], top[0][:, :], ALU.subtract).then_inc(shifted, 1)
                    dve.tensor_tensor(sel[:, :, :], oh[0][:, :, :], oh[1][:, :, :], ALU.add).then_inc(sel_ready, 1)
                    dve.wait_ge(exped, 1)
                    step(dve.tensor_scalar(den[:, :], ex[:, :], 1.0, None, ALU.add))
                    step(dve.reciprocal(wt[0][:, :], den[:, :]))
                    step(dve.tensor_tensor(wt[1][:, :], ex[:, :], wt[0][:, :], ALU.mult))
                dve.wait_ge(rank_ready, 1)
                step(dve.tensor_copy(tot[:, :, :], m.ps[2][:, 0:P].rearrange("p (i e) -> p e i", e=E)))
                step(dve.tensor_tensor_scan(run[:, :, :].rearrange("p e i -> p (e i)"), m.restart[:, :],
                                            tot[:, :, :].rearrange("p e i -> p (e i)"), 0.0, ALU.mult, ALU.add))
                step(dve.tensor_tensor(over[:, :, :], run[:, :, :], tot[:, :, :], ALU.subtract))
                step(dve.tensor_tensor(rank[:, :, :], m.ps[1][:, 0:P].rearrange("p (i e) -> p i e", e=E),
                                       over[:, :, :].rearrange("p e i -> p i e"), ALU.add))
                step(dve.tensor_scalar(cnt[:, :], run[:, :, NT - 1], float(cap if cap else N), None, ALU.min))
                step(dve.tensor_tensor(over[:, :, :], cnt[:, :].unsqueeze(2).broadcast_to([P, E, NT]),
                                       m.iota128[:, :].unsqueeze(1).broadcast_to([P, E, NT]), ALU.is_gt))
                step(dve.tensor_reduce(nblk[:, :], over[:, :, :], AX.X, ALU.add))
                step(dve.tensor_tensor_scan(bend[:, :], m.one8[:, :], nblk[:, :], 0.0, ALU.mult, ALU.add))
                step(dve.tensor_tensor(base[:, :], bend[:, :], nblk[:, :], ALU.subtract))
                if cap:
                    step(dve.tensor_scalar(keep[:, :, :], rank[:, :, :], float(cap), None, ALU.is_lt))
                step(dve.scalar_tensor_tensor(rank[:, :, :], bt(base[:, :]), float(P), rank[:, :, :], ALU.mult, ALU.add))
                for j in range(k):
                    step(dve.tensor_tensor(tmp[0][:, :, :], oh[j][:, :, :], rank[:, :, :], ALU.mult))
                    step(dve.tensor_reduce(pos[:, j, :], tmp[0][:, :, :], AX.X, ALU.add))
                    if cap:
                        step(dve.tensor_tensor(tmp[0][:, :, :], oh[j][:, :, :], keep[:, :, :], ALU.mult))
                        step(dve.tensor_reduce(kept[:, :], tmp[0][:, :, :], AX.X, ALU.add))
                        step(dve.tensor_tensor(wt[j][:, :], wt[j][:, :], kept[:, :], ALU.mult))
                        step(dve.tensor_scalar(kept[:, :], kept[:, :], -float(2 * G * P), float(2 * G * P), ALU.mult, ALU.add))
                        step(dve.tensor_tensor(pos[:, j, :], pos[:, j, :], kept[:, :], ALU.add))
                flat = pos[:, :, :].rearrange("p j i -> p (j i)")
                step(dve.tensor_scalar(div[:, :], flat, 1.0 / P, -63.5 / P, ALU.mult, ALU.add))
                step(dve.tensor_scalar(div[:, :], div[:, :], MAGIC, MAGIC, ALU.add, ALU.subtract))
                step(dve.scalar_tensor_tensor(mod[:, :], div[:, :], -float(P), flat, ALU.mult, ALU.add))
                for j in range(k):
                    own = slice(j * NT, (j + 1) * NT)
                    each = lambda t, n: t.unsqueeze(2).broadcast_to([P, NT, n])
                    row = lambda t, n: t.unsqueeze(1).broadcast_to([P, NT, n])
                    step(dve.tensor_tensor(blkhot[:, own, :], each(div[:, own], G), row(m.small["iotag"][:, 0:G], G), ALU.is_equal))
                    step(dve.tensor_tensor(code[:, own, 0, :], blkhot[:, own, :], each(m.small["tile1"][:, own], G), ALU.mult))
                    step(dve.tensor_scalar(code[:, own, 1, :], blkhot[:, own, :], m.small["part"][:, 0:1], None, ALU.mult))
                    dve.tensor_tensor(rowhot[:, own, :], each(mod[:, own], P), row(m.small["iotar"][:, :], P), ALU.is_equal).then_inc(slots_known, 1)
                step(dve.tensor_tensor(cmpt[:, :, :], m.small["iotag"][0:1, 0:G].unsqueeze(2).broadcast_to([1, G, E]),
                                       bend[0:1, :].unsqueeze(1).broadcast_to([1, G, E]), ALU.is_ge))
                step(dve.tensor_reduce(btab[:, :], cmpt[:, :, :], AX.X, ALU.add))
                dve.tensor_scalar(btabi[:, :], btab[:, :], float(E - 1), None, ALU.min).then_inc(table_ready, 1)
                dve.wait_ge(index_ready, 1)
                step(dve.tensor_copy(ffree[:, :], m.ps[3][:, G:2 * G]))
                step(dve.scalar_tensor_tensor(found[:, :], m.ps[3][:, 0:G], float(P), ffree[:, :], ALU.mult, ALU.add))
                step(dve.tensor_scalar(found[:, :], found[:, :], -float(P), None, ALU.add))
                step(dve.tensor_scalar(ffree[:, :], found[:, :], 0.0, float(2 * Q * P), ALU.is_lt, ALU.mult))
                dve.tensor_scalar(gidx[:, :], found[:, :], 0.0, None, ALU.max).then_inc(index_done, 1)
                dve.tensor_tensor(sidx[:, :], found[:, :], ffree[:, :], ALU.add).then_inc(index_done, 1)
                dve.wait_ge(index_done, 2)

    xb = sb(name + "_xb", [P, U, D])
    xT = sb(name + "_xT", [P, 2, P])
    hg = sb(name + "_hg", [P, 2, F]) if gated else None
    h = sb(name + "_h", [P, 2, F])
    hT = sb(name + "_hT", [P, 2, F])
    yb = sb(name + "_yb", [P, U, D])
    gnow, snow = (sb(f"{name}_{n}", [P, U], U32) for n in ("gnow", "snow"))
    IT = G // U
    LAG = U - 2

    def back(n, sl, by):
        if sl < by:
            n, sl = n - 1, sl + U
        if isinstance(n, int) and not 0 <= n < IT:
            return None
        return n, sl - by

    def loop(eng, body, tail):
        for sl in range(U):
            body(0, sl)
        with eng.Fori(1, IT) as n:
            for sl in range(U):
                body(n, sl)
        for sl in range(tail):
            body(IT, sl)

    with nc.Block() as block:
        @block.gpsimd
        def _(pool):
            def indices(nn, ss, table, now, done):
                g = nn * U + ss
                pool.sem_inc(pool_pass, 1)
                pool.tensor_copy(now[:, ss:ss + U // 2], table[:, bass.ds(g, U // 2)]).then_inc(done, 1)
                pool.wait_ge(done, 2 * nn + ss // (U // 2) + 1)
                pool.sem_inc(pool_pass, 1)

            def body(n, sl):
                if (at := back(n, sl, 0)):
                    g = at[0] * U + sl
                    if sl % (U // 2) == 0:
                        ge(pool, xT_ready, g - U // 2)
                        indices(n, sl, gidx, gnow, gnow_done)
                    else:
                        ge(pool, xT_ready, g + 1 - U)
                        pool.sem_inc(pool_pass, 1)
                    pool.indirect_dma_start(out=xb[:, sl, :], out_offset=None, in_=pairs_in,
                                            in_offset=bass.IndirectOffsetOnAxis(ap=gnow[:, sl:sl + 1], axis=0)).then_inc(x_in[sl], 16)
                if (at := back(n, sl, LAG)):
                    nn, ss = at
                    g = nn * U + ss
                    if ss % (U // 2) == 0:
                        for other in range(ss, ss + U // 2):
                            ge(pool, scattered[other], 16 * nn)
                        indices(nn, ss, sidx, snow, snow_done)
                    pool.wait_ge(y_done, g + 1)
                    pool.sem_inc(pool_pass, 1)
                    pool.indirect_dma_start(out=pairs_out, out_offset=bass.IndirectOffsetOnAxis(ap=snow[:, ss:ss + 1], axis=0),
                                            in_=yb[:, ss, :], in_offset=None, bounds_check=Q * P - 1,
                                            oob_is_err=False).then_inc(scattered[ss], 16)

            loop(pool, body, LAG)

        @block.tensor
        def _(pe):
            def body(n, sl):
                if (at := back(n, sl, 0)):
                    g = at[0] * U + sl
                    pe.wait_ge(x_in[sl], 16 * (n + 1))
                    ge(pe, xT_done, g)
                    pe.transpose(m.ps[0][:, 0:P], xb[:, sl, :], m.ident[:, :]).then_inc(xT_ready, 1)
                if (at := back(n, sl, 1)):
                    nn, ss = at
                    g = nn * U + ss
                    e = pe.value_load(btabi[0:1, bass.ds(g, 1)], min_val=0, max_val=E - 1)
                    pe.wait_ge(xT_done, g + 1)
                    ge(pe, h_done, g - 1)
                    for q, w in enumerate((w1, w3) if gated else (w1,)):
                        ins = pe.matmul(m.ps[1 + 2 * q + ss % 2][:, :], xT[:, ss % 2, :],
                                        w[:, bass.ds(e, 1), :].rearrange("p e f -> p (e f)"), start=True, stop=True)
                    ins.then_inc(h_ready, 1)
                if (at := back(n, sl, 2)):
                    nn, ss = at
                    g = nn * U + ss
                    pe.wait_ge(h_done, g + 1)
                    ge(pe, hT_done, g - 1)
                    for f in range(FC):
                        ins = pe.transpose(m.ps[5 + ss % 2][:, f * P:(f + 1) * P], h[:, ss % 2, f * P:(f + 1) * P], m.ident[:, :])
                    ins.then_inc(hT_ready, 1)
                if (at := back(n, sl, 3)):
                    nn, ss = at
                    g = nn * U + ss
                    e = pe.value_load(btabi[0:1, bass.ds(g, 1)], min_val=0, max_val=E - 1)
                    pe.wait_ge(hT_done, g + 1)
                    ge(pe, y_done, g)
                    for f in range(FC):
                        ins = pe.matmul(m.ps[7][:, 0:D], hT[:, ss % 2, f * P:(f + 1) * P],
                                        w2[:, bass.ds(e, 1), f, :].rearrange("p e d -> p (e d)"), start=(f == 0), stop=(f == FC - 1))
                    ins.then_inc(y_ready, 1)

            pe.wait_ge(m.fetch.sem, 16 * fetched)
            loop(pe, body, 3)

        @block.scalar
        def _(act):
            def body(n, sl):
                if act_fn is not None and (at := back(n, sl, 1)):
                    nn, ss = at
                    g = nn * U + ss
                    act.wait_ge(h_ready, g + 1)
                    if gated:
                        ge(act, h_done, g - 1)
                        act.activation(hg[:, ss % 2, :], m.ps[1 + ss % 2][:, :], act_fn).then_inc(h_act, 1)
                    else:
                        ge(act, hT_ready, g - 1)
                        act.activation(h[:, ss % 2, :], m.ps[1 + ss % 2][:, :], act_fn).then_inc(h_done, 1)
                if (gated or biased) and (at := back(n, sl, 2)):
                    nn, ss = at
                    g = nn * U + ss
                    act.wait_ge(hT_ready, g + 1)
                    ge(act, y_ready, g - 1)
                    if biased:
                        act.activation(hT[:, ss % 2, :], m.ps[5 + ss % 2][:, :], ACT.Relu).then_inc(hT_done, 1)
                    else:
                        act.copy(hT[:, ss % 2, :], m.ps[5 + ss % 2][:, :]).then_inc(hT_done, 1)

            loop(act, body, 2)

        @block.vector
        def _(dve):
            def body(n, sl):
                if (at := back(n, sl, 0)):
                    g = at[0] * U + sl
                    dve.wait_ge(xT_ready, g + 1)
                    ge(dve, h_ready, g - 1)
                    dve.tensor_copy(xT[:, sl % 2, :], m.ps[0][:, 0:P]).then_inc(xT_done, 1)
                if act_fn is None or gated:
                    if (at := back(n, sl, 1)):
                        nn, ss = at
                        g = nn * U + ss
                        if gated:
                            dve.wait_ge(h_act, g + 1)
                            ge(dve, hT_ready, g - 1)
                            dve.tensor_tensor(h[:, ss % 2, :], hg[:, ss % 2, :], m.ps[3 + ss % 2][:, :], ALU.mult).then_inc(h_done, 1)
                        else:
                            e = dve.value_load(btabi[0:1, bass.ds(g, 1)], min_val=0, max_val=E - 1)
                            dve.wait_ge(h_ready, g + 1)
                            ge(dve, hT_ready, g - 1)
                            dve.tensor_tensor(h[:, ss % 2, :], m.ps[1 + ss % 2][:, :],
                                              b1[:, bass.ds(e, 1), :].rearrange("p e f -> p (e f)"), ALU.add).then_inc(h_done, 1)
                elif (at := back(n, sl, 2)):
                    nn, ss = at
                    g = nn * U + ss
                    dve.wait_ge(hT_ready, g + 1)
                    ge(dve, y_ready, g - 1)
                    dve.tensor_copy(hT[:, ss % 2, :], m.ps[5 + ss % 2][:, :]).then_inc(hT_done, 1)
                if (at := back(n, sl, 3)):
                    nn, ss = at
                    g = nn * U + ss
                    if biased:
                        e = dve.value_load(btabi[0:1, bass.ds(g, 1)], min_val=0, max_val=E - 1)
                    dve.wait_ge(y_ready, g + 1)
                    ge(dve, scattered[ss], 16 * nn)
                    if biased:
                        dve.tensor_tensor(yb[:, ss, :], m.ps[7][:, 0:D],
                                          b2[:, bass.ds(e, 1), :].rearrange("p e d -> p (e d)"), ALU.add).then_inc(y_done, 1)
                    else:
                        dve.tensor_copy(yb[:, ss, :], m.ps[7][:, 0:D]).then_inc(y_done, 1)

            loop(dve, body, 3)

    got = sb(name + "_got", [P, Q, D])
    with nc.Block() as block:
        @block.sync
        def _(sp):
            for q in scattered:
                sp.wait_ge(q, 16 * IT)
            rows = pairs_out.rearrange("(q p) d -> p q d", p=P)
            for b in range(B):
                for j in range(k):
                    tiles = slice(j * NT + b * TB, j * NT + (b + 1) * TB)
                    sp.dma_start(got[:, tiles, :], rows[:, tiles, :]).then_inc(back_in[b], 16)

        @block.vector
        def _(dve):
            if x_stage:
                m.dve(dve.tensor_tensor(m.x[:, :, :], m.x[:, :, :], m.xn[:, :, :], ALU.add))
                m.dve.wait(dve)
            for b in range(B):
                dve.wait_ge(back_in[b], 16 * k)
                for j in range(k):
                    for i in range(b * TB, (b + 1) * TB):
                        m.dve(dve.scalar_tensor_tensor(m.x[:, i, :], got[:, j * NT + i, :], wt[j][:, i:i + 1], m.x[:, i, :],
                                                       ALU.mult, ALU.add))
                    m.dve.wait(dve)


def context_heads(nc, m, a, sem, sb, name, keys, values, projected, kbias, vbias):
    kT = sb(name + "_kT", [P, B, J]) if projected else m.ctxT
    kb = sb(name + "_kb", [P, B, H, J])
    vf = sb(name + "_vf", [P, B, NC, CH * (HD + 1)])
    k_ready, k_biased, kb_done, v_ready, zeroed = (
        sem(f"{name}_{n}") for n in ("k_ready", "k_biased", "kb_done", "v_ready", "zeroed"))
    with nc.Block() as block:
        @block.vector
        def _(dve):
            for b in range(B):
                dve.memset(m.ps[b][:, 0:NC * CH * HD], 0.0).then_inc(zeroed, 1)
            if projected:
                dve.wait_ge(k_ready, 1)
                dve.tensor_scalar(kT[:, :, :], m.ps[7][:, 0:B * J].rearrange("p (b j) -> p b j", b=B),
                                  kbias[:, 0:1], None, ALU.add).then_inc(k_biased, 1)
            for b in range(B):
                out = vf[:, b, :, :].rearrange("p c (h e) -> p (c h) e", e=HD + 1)
                mask = m.small["vmask"][:, :]
                dve.wait_ge(v_ready, b + 1)
                m.dve(dve.tensor_tensor(out[:, :, 0:HD], m.ps[b][:, 0:NC * CH * HD].rearrange("p (c e) -> p c e", e=HD),
                                        mask.unsqueeze(2).broadcast_to([P, NC * CH, HD]), ALU.mult))
                m.dve(dve.tensor_copy(out[:, :, HD], mask))
            m.dve.wait(dve)

        @block.gpsimd
        def _(pool):
            if projected:
                pool.wait_ge(k_biased, 1)
            for b in range(B):
                pool.tensor_tensor(kb[:, b, :, :], kT[:, b, :].unsqueeze(1).broadcast_to([P, H, J]),
                                   m.small["qmask"][:, :].unsqueeze(2).broadcast_to([P, H, J]), ALU.mult).then_inc(kb_done, 1)
            pool.wait_ge(kb_done, B)

        @block.tensor
        def _(pe):
            if projected:
                pe.matmul(m.ps[7][:, 0:B * J], keys[:, :], m.ctxT[:, :, :], start=True, stop=True).then_inc(k_ready, 1)
            for b in range(B):
                pe.wait_ge(zeroed, b + 1)
                for n, c in enumerate(CHUNKS):
                    o = m.ps[b][0:c.width, n * CH * HD:n * CH * HD + c.heads * HD]
                    cols = slice(c.h0 * HD, (c.h0 + c.heads) * HD)
                    ins = pe.matmul(o, m.ctxT3[:, b, c.row:c.row + c.width], values[:, cols], start=True, stop=not projected)
                    if projected:
                        ins = pe.matmul(o, m.ones1[0:1, 0:c.width], vbias[0:1, cols], start=False, stop=True)
                ins.then_inc(v_ready, 1)
    return kb, vf


def rotate(eng, body, lag):
    for t in range(TB):
        body(0, t)
    with eng.Fori(1, B) as b:
        for t in range(TB):
            body(b, t)
    for t in range(lag):
        body(B, t)


def due(b, t, by):
    while t < by:
        b, t = b - 1, t + TB
    if isinstance(b, int) and not 0 <= b < B:
        return None
    return b, t - by


def attention8(nc, m, a, sem, sb, name, scale, projected, masked):
    yield None
    if projected:
        keys, values, wo, bo = m.small["wkT"], m.small["wvT"], m.small["woT"], m.small["bo"]
        kb, vf = context_heads(nc, m, a, sem, sb, name, keys, values, True, m.small["bk"], m.small["bv"])
    else:
        wo, bo = m.small["woutT"], m.small["bout"]
        kb, vf = context_heads(nc, m, a, sem, sb, name, None, m.ident, False, None, None)
    (q_ready, q_done, s_ready, sub_done, exp_done, t_ready, t_done, pv_ready, o_done, oT_ready,
     oT_done, y_ready, x_done, max_done, rden_done, mask_in, pool_pass, mask_done) = (
        sem(f"{name}_{n}") for n in (
        "q_ready", "q_done", "s_ready", "sub_done", "exp_done", "t_ready", "t_done", "pv_ready",
        "o_done", "oT_ready", "oT_done", "y_ready", "x_done", "max_done", "rden_done", "mask_in",
        "pool_pass", "mask_done"))
    qT = sb(name + "_qT", [P, S])
    pr = sb(name + "_pr", [P, 2, HJ])
    prT = sb(name + "_prT", [P, 2, NC * P])
    mx = sb(name + "_mx", [P, 2, H])
    rden = sb(name + "_rden", [P, 2, H])
    o = sb(name + "_o", [P, 2, D])
    oT = sb(name + "_oT", [P, 2, P])
    if masked:
        maski = sb(name + "_maski", [P, NT, J], I32)
        madd = sb(name + "_madd", [P, NT, J], BF16)
    scores = [m.ps[i][:, 0:QJ] for i in range(4)]
    PV, OB = m.ps[6], m.ps[7]

    def tbank(g):
        return m.ps[4 + g % 2]

    with nc.Block() as block:
        if masked:
            @block.sync
            def _(sp):
                sp.dma_start(maski[:, :, :], a["mask3"].rearrange("b (i p) j -> p (b i) j", p=P)).then_inc(mask_in, 16)

        if not projected:
            @block.gpsimd
            def _(pool):
                def prepare(b):
                    ge(pool, s_ready, TB * b)
                    pool.sem_inc(pool_pass, 1)
                    pool.tensor_copy(qT[:, :], m.xnT[:, bass.ds(b * S, S)]).then_inc(q_done, 1)

                prepare(0)
                with pool.Fori(1, B) as b:
                    prepare(b)

        @block.tensor
        def _(pe):
            def project_q(b):
                ge(pe, x_done, TB * b - 3)
                pe.matmul(OB[:, :], m.small["wqT"][:, :], m.xnT[:, bass.ds(b * S, S)], start=True, stop=True).then_inc(q_ready, 1)

            def body(b, t):
                if (at := due(b, t, 0)):
                    i = at[0] * TB + at[1]
                    if t == 0:
                        if projected:
                            project_q(b)
                        pe.wait_ge(q_done, at[0] + 1)
                        if masked:
                            ge(pe, mask_done, 1)
                    ge(pe, sub_done, i)
                    for r in range(4):
                        ins = pe.matmul(scores[r], qT[:, t * P:(t + 1) * P],
                                        kb[:, bass.ds(at[0], 1), r * QH:(r + 1) * QH, :].rearrange("p b h j -> p (b h j)"),
                                        start=True, stop=not masked)
                    if masked:
                        for r in range(4):
                            ins = pe.matmul(scores[r], m.small["identb"][:, :],
                                            madd[:, bass.ds(i, 1), :].broadcast_to([P, QH, J]), start=False, stop=True)
                    ins.then_inc(s_ready, 1)
                if (at := due(b, t, 3)):
                    i = at[0] * TB + at[1]
                    pe.wait_ge(o_done, i + 1)
                    ge(pe, x_done, i)
                    pe.transpose(OB[:, 0:P], o[:, at[1] % 2, :], m.ident[:, :]).then_inc(oT_ready, 1)
                if (at := due(b, t, 2)):
                    i = at[0] * TB + at[1]
                    pe.wait_ge(t_done, NG * (i + 1))
                    ge(pe, o_done, i)
                    for n, c in enumerate(CHUNKS):
                        ins = pe.matmul(PV[:, c.h0 * 9:(c.h0 + c.heads) * 9], prT[0:c.width, at[1] % 2, n * P:(n + 1) * P],
                                        vf[0:c.width, bass.ds(at[0], 1), n, 0:c.heads * 9].rearrange("p b e -> p (b e)"),
                                        start=(n == 0), stop=(n == NC - 1), skip_group_check=True)
                    ins.then_inc(pv_ready, 1)
                if (at := due(b, t, 3)):
                    i = at[0] * TB + at[1]
                    pe.wait_ge(oT_done, i + 1)
                    pe.matmul(OB[:, P:P + D], oT[:, at[1] % 2, :], wo[:, :], start=True, stop=False)
                    pe.matmul(OB[:, P:P + D], m.ones1[0:1, :], bo[0:1, :], start=False, stop=True).then_inc(y_ready, 1)
                if (at := due(b, t, 1)):
                    i = at[0] * TB + at[1]
                    pe.wait_ge(exp_done, i + 1)
                    for g, group in enumerate(GROUPS):
                        ge(pe, t_done, NG * i + g - 1)
                        for n, ch in enumerate(group):
                            c = CHUNKS[ch]
                            ins = pe.transpose(m.ps[4 + (NG * at[1] + g) % 2][0:c.width, n * P:(n + 1) * P],
                                               pr[:, at[1] % 2, c.at:c.at + c.width], m.ident[:, :])
                        ins.then_inc(t_ready, 1)

            rotate(pe, body, 3)

        @block.vector
        def _(dve):
            if masked:
                dve.wait_ge(mask_in, 16)
                m.dve(dve.tensor_scalar(madd[:, :, :], maski[:, :, :], 0.0, MASKED, ALU.is_equal, ALU.mult))
                m.dve.wait(dve)
                dve.sem_inc(mask_done, 1)
            bank4 = m.all_banks[:, 0:4, 0:QJ].rearrange("p r (h j) -> p r h j", h=QH)

            def body(b, t):
                if (at := due(b, t, 0)):
                    i = at[0] * TB + at[1]
                    if projected and t == 0:
                        dve.wait_ge(q_ready, b + 1)
                        ge(dve, s_ready, TB * b)
                        dve.tensor_scalar(qT[:, :], OB[:, :], m.small["bq"][:, 0:1], None, ALU.add).then_inc(q_done, 1)
                    dve.wait_ge(s_ready, i + 1)
                    dve.tensor_reduce(mx[:, t % 2, :], bank4, AX.X, ALU.max).then_inc(max_done, 1)
                if (at := due(b, t, 3)):
                    i = at[0] * TB + at[1]
                    dve.wait_ge(oT_ready, i + 1)
                    dve.tensor_copy(oT[:, at[1] % 2, :], OB[:, 0:P]).then_inc(oT_done, 1)
                if (at := due(b, t, 0)):
                    i = at[0] * TB + at[1]
                    dve.wait_ge(max_done, i + 1)
                    ge(dve, t_ready, NG * (i - 1))
                    dve.tensor_tensor(pr[:, t % 2, :].rearrange("p (r h j) -> p r h j", r=4, h=QH), bank4,
                                      mx[:, t % 2, :].rearrange("p (r h) -> p r h", r=4).unsqueeze(3).broadcast_to([P, 4, QH, J]),
                                      ALU.subtract).then_inc(sub_done, 1)
                if (at := due(b, t, 2)):
                    i = at[0] * TB + at[1]
                    pv = PV[:, 0:H * 9].rearrange("p (h e) -> p h e", e=9)
                    dve.wait_ge(pv_ready, i + 1)
                    dve.reciprocal(rden[:, at[1] % 2, :], pv[:, :, HD]).then_inc(rden_done, 1)
                    dve.wait_ge(rden_done, i + 1)
                    dve.tensor_tensor(o[:, at[1] % 2, :].rearrange("p (h e) -> p h e", e=HD), pv[:, :, 0:HD],
                                      rden[:, at[1] % 2, :].unsqueeze(2).broadcast_to([P, H, HD]), ALU.mult).then_inc(o_done, 1)
                if (at := due(b, t, 3)):
                    i = at[0] * TB + at[1]
                    dve.wait_ge(y_ready, i + 1)
                    xi = m.x[:, bass.ds(i, 1), :].rearrange("p i d -> p (i d)")
                    dve.tensor_tensor(xi, xi, OB[:, P:P + D], ALU.add).then_inc(x_done, 1)

            rotate(dve, body, 3)

        @block.scalar
        def _(act):
            def body(b, t):
                if (at := due(b, t, 0)):
                    i = at[0] * TB + at[1]
                    act.wait_ge(sub_done, i + 1)
                    act.activation(pr[:, t % 2, :], pr[:, t % 2, :], ACT.Exp, scale=scale).then_inc(exp_done, 1)
                if (at := due(b, t, 1)):
                    i = at[0] * TB + at[1]
                    for g, group in enumerate(GROUPS):
                        act.wait_ge(t_ready, NG * i + g + 1)
                        if g == 0:
                            ge(act, pv_ready, i - 1)
                        bank = m.ps[4 + (NG * at[1] + g) % 2]
                        at0 = P * group[0]
                        if len(group) * P + at0 > HJ:
                            c = CHUNKS[group[-1]]
                            full = len(group) - 1
                            act.copy(prT[:, at[1] % 2, at0:at0 + full * P], bank[:, 0:full * P])
                            act.copy(prT[0:c.width, at[1] % 2, at0 + full * P:at0 + full * P + P],
                                     bank[0:c.width, full * P:full * P + P]).then_inc(t_done, 1)
                        else:
                            act.copy(prT[:, at[1] % 2, at0:at0 + len(group) * P], bank[:, 0:len(group) * P]).then_inc(t_done, 1)

            rotate(act, body, 1)


EPS2 = 1e-6
KH = 64
PAIRS = H // 2


def attention64(nc, m, a, sem, sb):
    yield None
    wk, wqT, wvT, w0 = (sb("a2_" + n, [P, PAIRS, P]) for n in ("wk", "wqT", "wvT", "w0"))
    gamma, beta = sb("a2_gamma", [P, D]), sb("a2_beta", [P, D])
    maski = sb("a2_maski", [P, NT, J], I32)
    G = sb("a2_G", [P, B, H, J])
    vwf = sb("a2_vwf", [P, B, NC, D])
    y = sb("a2_y", [P, NT, D])
    (w_in, mask_in, k_ready, k_done, g_ready, g_done, mm_ready, mm_done, vw_ready, vw_done, vw_back, q_done,
     s_ready, mask_applied, max_done, sub_done, exp_done, sum_done, rden_done, norm_done, t_ready, t_done,
     pv_ready, y_done, pool_pass, var_done, std_done) = (
        sem("a2_" + n) for n in (
        "w_in", "mask_in", "k_ready", "k_done", "g_ready", "g_done", "mm_ready", "mm_done", "vw_ready", "vw_done",
        "vw_back", "q_done", "s_ready", "mask_applied", "max_done", "sub_done", "exp_done", "sum_done",
        "rden_done", "norm_done", "t_ready", "t_done", "pv_ready", "y_done", "pool_pass", "var_done",
        "std_done"))
    vw_out = [sem(f"a2_vw_out{n}") for n in range(4)]
    m01 = sb("a2_m01", [P, NT, J])

    with ExitStack() as inner:
        tmp = lambda n, shape: inner.enter_context(nc.sbuf_tensor("a2_" + n, shape, F32))
        k2T, M, vw = tmp("k2T", [P, PAIRS, B * J]), tmp("M", [P, H * D]), tmp("vw", [J, B, H * D // 2])
        VH = H * D // 2 // BANK
        with nc.Block() as block:
            @block.sync
            def _(sp):
                for t, src in ((wk, a["a2_wk"]), (wqT, a["a2_wqT"]), (wvT, a["a2_wvT"]), (w0, a["a2_w0"])):
                    sp.dma_start(t[:, :, :], src).then_inc(w_in, 16)
                sp.dma_start(gamma[:, :], a["a2_gamma"]).then_inc(w_in, 16)
                sp.dma_start(beta[:, :], a["a2_beta"]).then_inc(w_in, 16)
                sp.dma_start(maski[:, :, :], a["mask2"].rearrange("b (i p) j -> p (b i) j", p=P)).then_inc(mask_in, 16)
                for n in range(2 * B):
                    b, half = n // 2, n % 2
                    sp.wait_ge(vw_done, VH * (n + 1))
                    sp.dma_start(a["vw"][b, half * H // 2:(half + 1) * H // 2, :, :].rearrange("h j d -> j h d"),
                                 vw[:, n % 4, :].rearrange("j (h d) -> j h d", d=D)).then_inc(vw_out[n % 4], 16)
                for q in vw_out:
                    sp.wait_ge(q, 16 * 2 * B // 4)
                rows = a["vw"].rearrange("b h j d -> b (h j) d")
                for b in range(B):
                    full = HJ // P
                    sp.dma_start(vwf[:, b, 0:full, :], rows[b, 0:full * P, :].rearrange("(c p) d -> p c d", p=P)).then_inc(vw_back, 16)
                    sp.dma_start(vwf[0:HJ - full * P, b, full, :], rows[b, full * P:, :]).then_inc(vw_back, 16)
                sp.wait_ge(vw_back, 16 * 2 * B)

            def g_pair(pe, c):
                pe.wait_ge(k_done, c + 1)
                ge(pe, g_done, 2 * c)
                for r in range(2):
                    rows = slice(KH * r, KH * r + KH)
                    pe.matmul(m.ps[2 + r][:, 0:B * J], wqT[rows, c, :], k2T[rows, c, :], start=True, stop=True).then_inc(g_ready, 1)

            @block.tensor
            def _(pe):
                pe.wait_ge(w_in, 96)
                for c in range(PAIRS):
                    ge(pe, k_done, c - 1)
                    pe.matmul(m.ps[c % 2][:, 0:B * J], wk[:, c, :], m.ctxT[:, :, :], start=True, stop=True).then_inc(k_ready, 1)
                    if c >= 1:
                        g_pair(pe, c - 1)
                g_pair(pe, PAIRS - 1)
                for c in range(PAIRS):
                    ge(pe, mm_done, 2 * (c - 1))
                    for r in range(2):
                        rows = slice(KH * r, KH * r + KH)
                        pe.matmul(m.ps[4 + 2 * (c % 2) + r][:, 0:D], wvT[rows, c, :], w0[rows, c, :],
                                  start=True, stop=True).then_inc(mm_ready, 1)
                pe.wait_ge(mm_done, 2 * PAIRS)
                for n in range(B * 2 * VH):
                    b, q = n // (2 * VH), n % (2 * VH)
                    ge(pe, vw_done, n - 1)
                    if n < 2:
                        pe.wait_ge(k_done, PAIRS)
                    pe.matmul(m.ps[n % 2][0:J, :], m.ctxT[:, b, :], M[:, q * BANK:(q + 1) * BANK], start=True, stop=True).then_inc(vw_ready, 1)

            @block.vector
            def _(dve):
                for c in range(PAIRS):
                    dve.wait_ge(k_ready, c + 1)
                    dve.tensor_scalar(k2T[:, c, :], m.ps[c % 2][:, 0:B * J], KH ** -0.5, None, ALU.mult).then_inc(k_done, 1)
                for c in range(PAIRS):
                    for r in range(2):
                        h = 2 * c + r
                        dve.wait_ge(mm_ready, h + 1)
                        dve.tensor_copy(M[:, h * D:(h + 1) * D], m.ps[4 + 2 * (c % 2) + r][:, 0:D]).then_inc(mm_done, 1)
                dve.wait_ge(mask_in, 16)
                m.dve(dve.tensor_scalar(m01[:, :, :], maski[:, :, :], 0.0, None, ALU.not_equal))
                m.dve.wait(dve)

            @block.scalar
            def _(act):
                for h in range(H):
                    act.wait_ge(g_ready, h + 1)
                    act.copy(G[:, :, h, :], m.ps[2 + h % 2][:, 0:B * J].rearrange("p (b j) -> p b j", b=B)).then_inc(g_done, 1)
                for n in range(B * 2 * VH):
                    half, q = n // VH, n % VH
                    act.wait_ge(vw_ready, n + 1)
                    if q == 0:
                        ge(act, vw_out[half % 4], 16 * (half // 4))
                    act.copy(vw[:, half % 4, q * BANK:(q + 1) * BANK], m.ps[n % 2][0:J, :]).then_inc(vw_done, 1)

    qT = sb("a2_qT", [P, S])
    SLOTS = 4
    pr = sb("a2_pr", [P, SLOTS, HJ])
    prT = sb("a2_prT", [P, 2, NC * P])
    mx, sm, rden = (sb("a2_" + n, [P, SLOTS, H]) for n in ("mx", "sm", "rden"))
    scores = [m.ps[i][:, 0:QJ] for i in range(4)]
    PV = m.ps[6]
    hj = lambda ap: ap.rearrange("p (h j) -> p h j", h=H)
    wide = lambda ap: ap.unsqueeze(2).broadcast_to([P, H, J])

    with nc.Block() as block:
        @block.gpsimd
        def _(pool):
            def body(b, t):
                if t == 0 and not (isinstance(b, int) and b == B):
                    ge(pool, s_ready, TB * b)
                    pool.sem_inc(pool_pass, 1)
                    pool.tensor_copy(qT[:, :], m.xnT[:, bass.ds(b * S, S)]).then_inc(q_done, 1)
                if (at := due(b, t, 1)):
                    i = at[0] * TB + at[1]
                    pool.wait_ge(rden_done, i + 1)
                    p = hj(pr[:, at[1], :])
                    pool.tensor_tensor(p, p, wide(rden[:, at[1], :]), ALU.mult).then_inc(norm_done, 1)

            rotate(pool, body, 1)

        @block.tensor
        def _(pe):
            def body(b, t):
                if (at := due(b, t, 0)):
                    i = at[0] * TB + at[1]
                    if t == 0:
                        pe.wait_ge(q_done, b + 1)
                    ge(pe, mask_applied, i)
                    for r in range(4):
                        pe.matmul(scores[r], qT[:, t * P:(t + 1) * P],
                                  G[:, bass.ds(b, 1), r * QH:(r + 1) * QH, :].rearrange("p b h j -> p (b h j)"), start=True, stop=False)
                    for r in range(4):
                        ins = pe.matmul(scores[r], m.small["ones3"][:, :], m.small["neps"][:, :], start=False, stop=True)
                    ins.then_inc(s_ready, 1)
                if (at := due(b, t, 3)):
                    i = at[0] * TB + at[1]
                    pe.wait_ge(t_done, NG * (i + 1))
                    ge(pe, y_done, i)
                    for n, c in enumerate(CHUNKS):
                        ins = pe.matmul(PV[:, 0:D], prT[0:c.width, at[1] % 2, n * P:(n + 1) * P],
                                        vwf[0:c.width, bass.ds(at[0], 1), n, :].rearrange("p b e -> p (b e)"),
                                        start=(n == 0), stop=(n == NC - 1))
                    ins.then_inc(pv_ready, 1)
                if (at := due(b, t, 2)):
                    i = at[0] * TB + at[1]
                    pe.wait_ge(norm_done, i + 1)
                    for g, group in enumerate(GROUPS):
                        ge(pe, t_done, NG * i + g - 1)
                        for n, ch in enumerate(group):
                            c = CHUNKS[ch]
                            ins = pe.transpose(m.ps[4 + (NG * at[1] + g) % 2][0:c.width, n * P:(n + 1) * P],
                                               pr[:, at[1], c.at:c.at + c.width], m.ident[:, :])
                        ins.then_inc(t_ready, 1)

            rotate(pe, body, 3)

        @block.vector
        def _(dve):
            bank4 = m.all_banks[:, 0:4, 0:QJ].rearrange("p r (h j) -> p r h j", h=QH)

            def body(b, t):
                if (at := due(b, t, 0)):
                    i = at[0] * TB + at[1]
                    p = hj(pr[:, t, :])
                    dve.wait_ge(s_ready, i + 1)
                    ge(dve, t_ready, NG * (i - 3))
                    dve.tensor_tensor(pr[:, t, :].rearrange("p (r h j) -> p r h j", r=4, h=QH), bank4,
                                      m01[:, bass.ds(i, 1), :].unsqueeze(1).broadcast_to([P, 4, QH, J]), ALU.mult).then_inc(mask_applied, 1)
                    dve.wait_ge(mask_applied, i + 1)
                    dve.tensor_reduce(mx[:, t, :], p, AX.X, ALU.max).then_inc(max_done, 1)
                    dve.wait_ge(max_done, i + 1)
                    dve.tensor_tensor(p, p, wide(mx[:, t, :]), ALU.subtract).then_inc(sub_done, 1)
                if (at := due(b, t, 1)):
                    i = at[0] * TB + at[1]
                    dve.wait_ge(exp_done, i + 1)
                    dve.tensor_reduce(sm[:, at[1], :], hj(pr[:, at[1], :]), AX.X, ALU.add).then_inc(sum_done, 1)
                    dve.wait_ge(sum_done, i + 1)
                    dve.reciprocal(rden[:, at[1], :], sm[:, at[1], :]).then_inc(rden_done, 1)
                if (at := due(b, t, 3)):
                    i = at[0] * TB + at[1]
                    dve.wait_ge(pv_ready, i + 1)
                    yi, xi = (z[:, bass.ds(i, 1), :].rearrange("p i d -> p (i d)") for z in (y, m.xn))
                    dve.tensor_tensor(yi, xi, PV[:, 0:D], ALU.add).then_inc(y_done, 1)

            rotate(dve, body, 3)

        @block.scalar
        def _(act):
            def body(b, t):
                if (at := due(b, t, 0)):
                    i = at[0] * TB + at[1]
                    act.wait_ge(sub_done, i + 1)
                    act.activation(pr[:, t, :], pr[:, t, :], ACT.Exp).then_inc(exp_done, 1)
                if (at := due(b, t, 2)):
                    i = at[0] * TB + at[1]
                    for g, group in enumerate(GROUPS):
                        act.wait_ge(t_ready, NG * i + g + 1)
                        if g == 0:
                            ge(act, pv_ready, i - 1)
                        bank = m.ps[4 + (NG * at[1] + g) % 2]
                        at0 = P * group[0]
                        if len(group) * P + at0 > HJ:
                            c = CHUNKS[group[-1]]
                            full = len(group) - 1
                            act.copy(prT[:, at[1] % 2, at0:at0 + full * P], bank[:, 0:full * P])
                            act.copy(prT[0:c.width, at[1] % 2, at0 + full * P:at0 + full * P + P],
                                     bank[0:c.width, full * P:full * P + P]).then_inc(t_done, 1)
                        else:
                            act.copy(prT[:, at[1] % 2, at0:at0 + len(group) * P], bank[:, 0:len(group) * P]).then_inc(t_done, 1)

            rotate(act, body, 2)

    with nc.Block() as block:
        @block.vector
        def _(dve):
            for i in range(NT):
                m.dve(dve.bn_stats(m.stats[:, i, :], y[:, i, :]))
            m.dve.wait(dve)
            for i in range(NT):
                m.dve(dve.bn_aggr(m.mv[:, i, :], m.stats[:, i, :]))
            m.dve.wait(dve)
            dve.tensor_scalar(m.var[:, :], m.mv[:, :, 1], D / (D - 1.0), None, ALU.mult).then_inc(var_done, 1)
            dve.wait_ge(std_done, 1)
            m.dve(dve.tensor_scalar(m.std[:, :], m.std[:, :], EPS2, None, ALU.add))
            m.dve.wait(dve)
            m.dve(dve.reciprocal(m.rstd[:, :], m.std[:, :]))
            m.dve.wait(dve)
            m.dve(dve.scalar_tensor_tensor(m.nmr[:, :], m.mv[:, :, 0], -1.0, m.rstd[:, :], ALU.mult, ALU.mult))
            m.dve.wait(dve)
            for i in range(NT):
                m.dve(dve.tensor_scalar(y[:, i, :], y[:, i, :], m.rstd[:, i:i + 1], m.nmr[:, i:i + 1], ALU.mult, ALU.add))
            m.dve.wait(dve)
            rows = lambda v: v[:, :].unsqueeze(1).broadcast_to([P, NT, D])
            m.dve(dve.tensor_tensor(y[:, :, :], y[:, :, :], rows(gamma), ALU.mult))
            m.dve(dve.tensor_tensor(m.x[:, :, :], m.x[:, :, :], rows(beta), ALU.add))
            m.dve.wait(dve)
            m.dve(dve.tensor_tensor(m.x[:, :, :], m.x[:, :, :], y[:, :, :], ALU.add))
            m.dve.wait(dve)

        @block.scalar
        def _(act):
            act.wait_ge(var_done, 1)
            act.activation(m.std[:, :], m.var[:, :], ACT.Sqrt).then_inc(std_done, 1)


HID = 384
HC = HID // P
QMAX = 2.0 ** 15 - 1
TINY = 1e-12


def ffn1(nc, m, a, sem, sb):
    yield None
    w = sb("f1_w", [P, 3 * HC, P])
    wT = sb("f1_wT", [P, 3 * HC, P])
    NBLK = 3 * HC * 4
    ws, winv = sb("f1_ws", [P, NBLK]), sb("f1_winv", [P, NBLK])
    up, gate, sig = (sb("f1_" + n, [P, HC, N]) for n in ("up", "gate", "sig"))
    (w_in, w_done, wT_ready, wT_done, most_ready, most_done, xq_done, mm_ready, mm_done, up_scaled, gate_done,
     sig_done, up_done, o_done, down_ready, x_done, scale_ready) = (
        sem("f1_" + n) for n in (
        "w_in", "w_done", "wT_ready", "wT_done", "most_ready", "most_done", "xq_done", "mm_ready", "mm_done",
        "up_scaled", "gate_done", "sig_done", "up_done", "o_done", "down_ready", "x_done", "scale_ready"))
    XQ, UP, GATE, G2, OUT = range(5)
    part = sb("f1_part", [P, 5, 12])
    most, over, sc, inv = (sb("f1_" + n, [P, 5]) for n in ("most", "over", "sc", "inv"))
    scug = sb("f1_scug", [P, 1])
    col = lambda t, q: t[:, q:q + 1]

    with nc.Block() as block:
        @block.sync
        def _(sp):
            sp.dma_start(w[:, 0:HC, :], a["f1_up"]).then_inc(w_in, 16)
            sp.dma_start(w[:, HC:2 * HC, :], a["f1_gate"]).then_inc(w_in, 16)
            sp.dma_start(w[:, 2 * HC:3 * HC, :], a["f1_down"]).then_inc(w_in, 16)

        @block.gpsimd
        def _(pool):
            for n, (q, count) in enumerate(((XQ, 1), (UP, 2), (G2, 1), (OUT, 1))):
                pool.wait_ge(most_ready, n + 1)
                pool.partition_all_reduce(over[:, q:q + count], most[:, q:q + count], P, RED.max).then_inc(most_done, 1)
                if n == 1:
                    pool.wait_ge(up_scaled, 1)
                    for c in range(HC):
                        pool.tensor_scalar(up[:, c, :], up[:, c, :], col(inv, UP), MAGIC, ALU.mult, ALU.add).then_inc(up_done, 1)

        @block.tensor
        def _(pe):
            pe.wait_ge(w_done, 1)
            for n in range(3 * HC):
                ins = pe.transpose(m.ps[n // 4][:, n % 4 * P:n % 4 * P + P], w[:, n, :], m.ident[:, :])
            ins.then_inc(wT_ready, 1)
            pe.wait_ge(xq_done, 1)
            pe.wait_ge(wT_done, 3)
            for n in range(8 * HC):
                q, mat = n // (2 * HC), n % (2 * HC)
                ge(pe, mm_done, n - 7)
                pe.matmul(m.ps[n % 8][:, :], wT[:, mat, :], m.xnT[:, q * BANK:(q + 1) * BANK], start=True, stop=True).then_inc(mm_ready, 1)
            pe.wait_ge(mm_done, 8 * HC)
            for i in range(NT):
                if i % 4 == 0:
                    pe.wait_ge(o_done, i // 4 + 1)
                for c in range(HC):
                    ins = pe.matmul(m.ps[i // 4][:, i % 4 * P:i % 4 * P + P], sig[:, c, i * P:(i + 1) * P], wT[:, 2 * HC + c, :],
                                    start=(c == 0), stop=(c == HC - 1))
                if i % 4 == 3:
                    ins.then_inc(down_ready, 1)

        @block.scalar
        def _(act):
            for n in range(8 * HC):
                q, mat = n // (2 * HC), n % (2 * HC)
                act.wait_ge(mm_ready, n + 1)
                act.copy((up, gate)[mat // HC][:, mat % HC, q * BANK:(q + 1) * BANK], m.ps[n % 8][:, :]).then_inc(mm_done, 1)
            for c in range(HC):
                act.wait_ge(gate_done, c + 1)
                act.activation(sig[:, c, :], gate[:, c, :], ACT.Sigmoid).then_inc(sig_done, 1)

        @block.vector
        def _(dve):
            def step(ins):
                m.dve(ins)
                m.dve.wait(dve)

            def scale(q, n, count=1):
                at = slice(q, q + count)
                dve.wait_ge(most_done, n)
                step(dve.tensor_scalar(sc[:, at], over[:, at], 1.0 / QMAX, TINY, ALU.mult, ALU.max))
                step(dve.reciprocal(inv[:, at], sc[:, at]))

            dve.wait_ge(w_in, 48)
            wb = w[:, :, :].rearrange("p n (k e) -> p (n k) e", e=32)
            wide = lambda t: t[:, :].unsqueeze(2).broadcast_to([P, NBLK, 32])
            step(dve.tensor_reduce(ws[:, :], wb, AX.X, ALU.max, apply_absolute_value=True))
            step(dve.tensor_scalar(ws[:, :], ws[:, :], 1.0 / 7, TINY, ALU.mult, ALU.max))
            step(dve.reciprocal(winv[:, :], ws[:, :]))
            step(dve.tensor_tensor(wb, wb, wide(winv), ALU.mult))
            step(dve.tensor_scalar(wb, wb, MAGIC, MAGIC, ALU.add, ALU.subtract))
            dve.tensor_tensor(wb, wb, wide(ws), ALU.mult).then_inc(w_done, 1)
            dve.tensor_reduce(col(most, XQ), m.xnT[:, :], AX.X, ALU.max, apply_absolute_value=True).then_inc(most_ready, 1)
            dve.wait_ge(wT_ready, 1)
            for n in range(0, 3 * HC, 4):
                k = min(4, 3 * HC - n)
                dve.tensor_copy(wT[:, n:n + k, :], m.ps[n // 4][:, 0:k * P].rearrange("p (n e) -> p n e", n=k)).then_inc(wT_done, 1)
            scale(XQ, 1)
            step(dve.tensor_scalar(m.xnT[:, :], m.xnT[:, :], col(inv, XQ), MAGIC, ALU.mult, ALU.add))
            dve.tensor_scalar(m.xnT[:, :], m.xnT[:, :], MAGIC, col(sc, XQ), ALU.subtract, ALU.mult).then_inc(xq_done, 1)
            for n in range(8 * HC):
                q, mat = n // (2 * HC), n % (2 * HC)
                dve.wait_ge(mm_done, n + 1)
                m.dve(dve.tensor_reduce(part[:, UP + mat // HC, q * HC + mat % HC:q * HC + mat % HC + 1],
                                        (up, gate)[mat // HC][:, mat % HC, q * BANK:(q + 1) * BANK], AX.X, ALU.max,
                                        apply_absolute_value=True))
            m.dve.wait(dve)
            dve.tensor_reduce(most[:, UP:UP + 2], part[:, UP:UP + 2, :], AX.X, ALU.max).then_inc(most_ready, 1)
            scale(UP, 2, 2)
            dve.sem_inc(up_scaled, 1)
            for c in range(HC):
                step(dve.tensor_scalar(gate[:, c, :], gate[:, c, :], col(inv, GATE), MAGIC, ALU.mult, ALU.add))
                dve.tensor_scalar(gate[:, c, :], gate[:, c, :], MAGIC, col(sc, GATE), ALU.subtract, ALU.mult).then_inc(gate_done, 1)
            for c in range(HC):
                dve.wait_ge(sig_done, c + 1)
                step(dve.tensor_scalar(sig[:, c, :], sig[:, c, :], 65536.0, MAGIC, ALU.mult, ALU.add))
                step(dve.tensor_scalar(sig[:, c, :], sig[:, c, :], MAGIC, 65535.0, ALU.subtract, ALU.min))
                step(dve.scalar_tensor_tensor(gate[:, c, :], sig[:, c, :], 1 / 65536.0, gate[:, c, :], ALU.mult, ALU.mult))
                step(dve.tensor_reduce(part[:, G2, c:c + 1], gate[:, c, :], AX.X, ALU.max, apply_absolute_value=True))
            dve.tensor_reduce(col(most, G2), part[:, G2, 0:HC], AX.X, ALU.max).then_inc(most_ready, 1)
            scale(G2, 3)
            for c in range(HC):
                step(dve.tensor_scalar(gate[:, c, :], gate[:, c, :], col(inv, G2), MAGIC, ALU.mult, ALU.add))
                step(dve.tensor_scalar(gate[:, c, :], gate[:, c, :], MAGIC, col(sc, G2), ALU.subtract, ALU.mult))
                dve.wait_ge(up_done, c + 1)
                step(dve.tensor_scalar(up[:, c, :], up[:, c, :], MAGIC, col(sc, UP), ALU.subtract, ALU.mult))
                step(dve.tensor_tensor(sig[:, c, :], gate[:, c, :], up[:, c, :], ALU.mult))
                step(dve.tensor_reduce(part[:, OUT, c:c + 1], sig[:, c, :], AX.X, ALU.max, apply_absolute_value=True))
            dve.tensor_reduce(col(most, OUT), part[:, OUT, 0:HC], AX.X, ALU.max).then_inc(most_ready, 1)
            scale(OUT, 4)
            for q in range(4):
                o = sig[:, :, q * BANK:(q + 1) * BANK]
                step(dve.tensor_scalar(o, o, col(inv, OUT), MAGIC, ALU.mult, ALU.add))
                dve.tensor_scalar(o, o, MAGIC, col(sc, OUT), ALU.subtract, ALU.mult).then_inc(o_done, 1)
            for q in range(4):
                dve.wait_ge(down_ready, q + 1)
                xq = m.x[:, 4 * q:4 * q + 4, :]
                m.dve(dve.tensor_tensor(xq, xq, m.ps[q][:, :].rearrange("p (t d) -> p t d", t=4), ALU.add))
            m.dve.wait(dve)


def build(nc, a, upto=8):
    with ExitStack() as ctx:
        def sem(name):
            return ctx.enter_context(nc.semaphore(name))

        def sb(name, shape, dt=F32):
            return ctx.enter_context(nc.sbuf_tensor(name, shape, dt))

        m = Machine()
        m.all_banks = ctx.enter_context(nc.psum_tensor("banks", [P, 8, BANK], F32))
        m.ps = [m.all_banks[:, i, :] for i in range(8)]
        m.x, m.xn = sb("x", [P, NT, D]), sb("xn", [P, NT, D])
        m.xnT = sb("xnT", [P, N])
        m.ident = sb("ident", [P, P])
        m.ctxT = sb("ctxT", [P, B, J])
        m.ctxT3 = sb("ctxT3", [P, B, 3 * J])
        m.ones1 = sb("ones1", [1, P])
        m.stats, m.mv = sb("stats", [P, NT, 6]), sb("mv", [P, NT, 2])
        m.var, m.std, m.rstd, m.nmr = (sb(n, [P, NT]) for n in ("var", "std", "rstd", "nmr"))
        m.small = {n: sb("c_" + n, list(shape), dt) for n, (shape, dt) in SMALL.items()}
        m.narrow = [n for n, (shape, dt) in SMALL.items() if dt == BF16]
        m.w0T, m.diag0 = m.small["w0T"], m.small["diag0"]
        m.tri, m.onesb, m.iota8, m.iota128 = (m.small[n] for n in ("tri", "onesb", "iota8", "iota128"))
        m.restart, m.one8 = m.small["restart"], m.small["one8"]
        m.dve = Chain(sem("dve_chain"))
        m.ln_var, m.ln_std, m.ln_xn, m.ln_turned, m.ln_copied = (sem("ln_" + n) for n in ("var", "std", "xn", "turned", "copied"))
        m.loaded = sem("loaded")
        m.fetch = Fetch(sem("fetched"))
        zeroed, stored = sem("zeroed"), sem("stored")
        zero = sb("zero", [P, D])

        with ExitStack() as inner:
            m.given = {n: inner.enter_context(nc.sbuf_tensor("g_" + n, list(shape), F32)) if n in m.narrow else m.small[n]
                       for n, (shape, dt) in SMALL.items()}
            load(nc, m, a)
        with nc.Block() as block:
            @block.gpsimd
            def _(pool):
                pool.memset(zero[:, :], 0.0).then_inc(zeroed, 1)

            @block.sync
            def _(sp):
                sp.wait_ge(zeroed, 1)
                sp.dma_start(a["m2_pairs_out"].rearrange("(q p) d -> p q d", p=P),
                             zero[:, :].unsqueeze(1).broadcast_to([P, 2 * NT, D])).then_inc(stored, 16)
                sp.wait_ge(stored, 16)

        def stage(number, f, **kw):
            own = []

            def own_sem(name):
                own.append(nc.alloc_semaphore(name=name))
                return own[-1]

            with ExitStack() as inner:
                steps = f(nc, m, a, own_sem, lambda name, shape, dt=F32: inner.enter_context(nc.sbuf_tensor(name, shape, dt)), **kw)
                loads = next(steps)
                layer_norm(nc, m, number, loads)
                for _ in steps:
                    pass
            nc.clear_and_free_semaphores(own)

        for number, (f, kw) in enumerate(STAGES[:upto]):
            stage(number, f, **kw)

        with nc.Block() as block:
            @block.sync
            def _(sp):
                sp.dma_start(a["out"].rearrange("b (i p) d -> p (b i) d", p=P), m.x[:, :, :]).then_inc(stored, 16)
                sp.wait_ge(stored, 32)


GMAX = 40
SMALL = dict(
    w0T=((P, P), F32), diag0=((P, 1), F32), m0_router=((P, E), F32), m0_rbias=((P, E), F32),
    m2_router=((P, E), F32), m3_router=((P, E), F32),
    wqT=((P, P), F32), wkT=((P, P), F32), wvT=((P, P), F32), woT=((P, P), F32), bq=((P, 1), F32), bk=((P, 1), F32),
    bv=((1, P), F32), bo=((1, P), F32), woutT=((P, P), F32), bout=((1, P), F32),
    vmask=((P, NC * CH), F32), qmask=((P, H), F32), identb=((P, P), BF16), ones3=((3, P), BF16), neps=((3, QJ), BF16),
    tri=((P, P), BF16), onesb=((P, P), BF16), iota8=((P, E), F32), iota128=((P, NT), F32), iotag=((P, GMAX), F32), iotar=((P, P), F32),
    tile1=((P, 2 * NT), F32), part=((P, 1), F32),
    restart=((P, E * NT), F32), one8=((P, E), F32),
)
STAGES = [
    (attention0, {}),
    (moe, dict(name="m0", blocks=24, topk=1, cap=0, biased=True, gated=False, act_fn=None, x_stage=False)),
    (attention8, dict(name="a1", scale=HD ** -0.5, projected=True, masked=False)),
    (ffn1, {}),
    (attention64, {}),
    (moe, dict(name="m2", blocks=GMAX, topk=2, cap=int(1.25 * N * 2 / E) + 1, biased=False, gated=False, act_fn=ACT.Silu, x_stage=True)),
    (attention8, dict(name="a3", scale=HD ** -0.5, projected=False, masked=True)),
    (moe, dict(name="m3", blocks=GMAX, topk=2, cap=0, biased=False, gated=True, act_fn=ACT.Silu, x_stage=False)),
]


def arrays(v):
    c = np.ascontiguousarray
    ctx = np.asarray(v["ctx_1024"])
    rows = lambda w, n: c(np.broadcast_to(w, (n,) + w.shape))
    chunked = lambda w: c(w.reshape(w.shape[0], FC, P, D).transpose(0, 2, 1, 3).reshape(w.shape[0], P, FC * D))
    pairs = lambda w: w.reshape(PAIRS, P, D).transpose(1, 0, 2)

    def vmask():
        k = np.zeros((P, NC, CH), np.float32)
        for n, ch in enumerate(CHUNKS):
            r = np.arange(ch.width)
            k[r, n, (ch.at + r) // J - ch.h0] = 1
        return k.reshape(P, NC * CH)

    def split3(value):
        parts, rest = [], np.float32(value)
        for _ in range(3):
            parts.append((np.array([rest]).view(np.uint32) & 0xffff0000).view(np.float32)[0])
            rest = np.float32(rest - parts[-1])
        return np.broadcast_to(np.array(parts, np.float32)[:, None], (3, QJ))

    o = dict(
        x=v["x"], ctx=ctx, ctxT=c(ctx.transpose(2, 0, 1)), mask0=v["mask_BxS2_if1"],
        w0T=c(v["L0_xattn_W"].T), diag0=c(v["L0_xattn_diagonal"].reshape(P, 1)),
        m0_router=v["L0_ffn_w_gate"], m0_rbias=rows(v["L0_ffn_b_gate"], P),
        m0_w1=v["L0_ffn_W1"], m0_w2=chunked(v["L0_ffn_W2"]),
        m0_b1=c(np.broadcast_to(v["L0_ffn_b1"][:, None, :], (E, P, F))),
        m0_b2=c(np.broadcast_to(v["L0_ffn_b2"][:, None, :], (E, P, D))),
        m2_router=c(v["L2_ffn_router_w"].T), m3_router=c(v["L3_ffn_gate_w"].T),
        wqT=c(v["L1_xattn_wq"].T), wkT=c(v["L1_xattn_wk"].T), wvT=c(v["L1_xattn_wv"].T), woT=c(v["L1_xattn_wo"].T),
        bq=v["L1_xattn_bq"][:, None], bk=v["L1_xattn_bk"][:, None], bv=v["L1_xattn_bv"][None], bo=v["L1_xattn_bo"][None],
        woutT=c(v["L3_xattn_W_out"].T), bout=v["L3_xattn_b_out"][None], mask3=v["mask_Bx1xSxS2_ik1"][:, 0],
        mask2=v["mask_BxSxS2_ik1"], a2_wk=v["L2_xattn_w_k"].reshape(D, PAIRS, P),
        a2_wqT=pairs(v["L2_xattn_w_q"].T), a2_wvT=pairs(v["L2_xattn_w_v"].T), a2_w0=pairs(v["L2_xattn_w_0"]),
        a2_gamma=rows(v["L2_xattn_gamma"], P), a2_beta=rows(v["L2_xattn_beta"], P),
        f1_up=v["L1_ffn_w_up"].reshape(HC, P, D).transpose(1, 0, 2), f1_gate=v["L1_ffn_w_gate"].reshape(HC, P, D).transpose(1, 0, 2),
        f1_down=v["L1_ffn_w_down"].reshape(P, HC, P),
        m2_w1=v["L2_ffn_w1"], m2_w2=chunked(v["L2_ffn_w2"]),
        m3_w1=c(v["L3_ffn_w1"].transpose(0, 2, 1)), m3_w3=c(v["L3_ffn_w3"].transpose(0, 2, 1)),
        m3_w2=chunked(v["L3_ffn_w2"].transpose(0, 2, 1)),
        vmask=vmask(), qmask=(np.arange(P)[:, None] // HD == np.arange(H)).astype(np.float32),
        identb=np.eye(P, dtype=np.float32), ones3=np.ones((3, P), np.float32), neps=split3(-EPS2),
        ident=np.eye(P, dtype=np.float32), tri=np.triu(np.ones((P, P), np.float32), 1), onesb=np.ones((P, P), np.float32),
        iota8=rows(np.arange(E, dtype=np.float32), P), iota128=rows(np.arange(NT, dtype=np.float32) * P, P),
        iotag=rows(np.arange(GMAX, dtype=np.float32), P), iotar=rows(np.arange(P, dtype=np.float32), P),
        tile1=rows(np.arange(1, 2 * NT + 1, dtype=np.float32), P), part=np.arange(P, dtype=np.float32)[:, None], restart=rows((np.arange(E * NT) % NT != 0).astype(np.float32), P),
        one8=np.ones((P, E), np.float32),
    )
    return {k: c(np.asarray(x)) for k, x in o.items()}


def kernel(**inputs):
    import concourse.bacc as bacc
    from concourse.bass_utils import run_bass_kernel_spmd

    nc = bacc.Bacc("TRN2", target_bir_lowering=False, num_devices=1)
    given = arrays({k: np.asarray(v) for k, v in inputs.items()})
    a = {k: nc.dram_tensor("in_" + k, v.shape, mybir.dt.from_np(v.dtype), kind="ExternalInput").ap() for k, v in given.items()}
    a["out"] = nc.dram_tensor("out", (B, S, D), F32, kind="ExternalOutput").ap()
    a["pairs_in"] = nc.dram_tensor("pairs_in", (2 * N, D), F32, kind="Internal").ap()
    a["vw"] = nc.dram_tensor("value_rows", (B, H, J, D), F32, kind="Internal").ap()
    for name, k in (("m0", 1), ("m2", 2), ("m3", 2)):
        a[name + "_pairs_out"] = nc.dram_tensor(name + "_pairs_out", (k * N, D), F32, kind="Internal").ap()
    build(nc, a, UPTO)
    result = run_bass_kernel_spmd(nc, [{"in_" + k: v for k, v in given.items()}], core_ids=[0])
    return result.results[0]["out"]


UPTO = 8
```

```python
from contextlib import ExitStack

import numpy as np

import concourse.bass as bass
from concourse import mybir

F32 = mybir.dt.float32
BF16 = mybir.dt.bfloat16
I32 = mybir.dt.int32
U32 = mybir.dt.uint32
ALU = mybir.AluOpType
ACT = mybir.ActivationFunctionType
AX = mybir.AxisListType
RED = bass.bass_isa.ReduceOp

P = 128
D = 128
B, S, J = 4, 512, 77
N = B * S
NT = N // P
TB = NT // B
BANK = 512
H = 16
HD = D // H
HJ = H * J
QH = H // 4
QJ = QH * J
E = 8
F = 512
FC = F // P
LN_EPS = 1e-5
MASKED = -1e20
MAGIC = 1.5 * 2.0 ** 23

CH = (P - 2) // J + 2


class Chunk:
    def __init__(self, at):
        self.at, self.width = at, min(P, HJ - at)
        self.row, self.h0 = at % J, min(at // J, H - CH)


CHUNKS = [Chunk(at) for at in range(0, HJ, P)]
NC = len(CHUNKS)
GROUPS = [range(g, min(g + 4, NC)) for g in range(0, NC, 4)]
NG = len(GROUPS)


class Machine:
    pass


def ge(eng, sem, value):
    if not (isinstance(value, int) and value <= 0):
        eng.wait_ge(sem, value)


class Chain:

    def __init__(self, sem):
        self.sem, self.n = sem, 0

    def __call__(self, ins):
        ins.then_inc(self.sem, 1)
        self.n = self.n + 1
        return self.n

    def wait(self, eng):
        ge(eng, self.sem, self.n)


class Fetch:

    def __init__(self, sem):
        self.sem, self.n = sem, 0

    def __call__(self, ins):
        ins.then_inc(self.sem, 16)
        self.n = self.n + 1

    def wait(self, eng):
        eng.wait_ge(self.sem, 16 * self.n)


def nothing(engine):
    pass


def layer_norm(nc, m, k, loads=nothing, pe_work=nothing, act_work=nothing, pool_work=nothing):
    with nc.Block() as block:
        if loads is not nothing:
            @block.sync
            def _(sp):
                loads(sp)

        if pool_work is not nothing:
            @block.gpsimd
            def _(pool):
                pool_work(pool)

        @block.vector
        def _(dve):
            for i in range(NT):
                if k == 0 and i % TB == 0:
                    dve.wait_ge(m.x_in[i // TB], 16)
                m.dve(dve.bn_stats(m.stats[:, i, :], m.x[:, i, :]))
            m.dve.wait(dve)
            for i in range(NT):
                m.dve(dve.bn_aggr(m.mv[:, i, :], m.stats[:, i, :]))
            m.dve.wait(dve)
            dve.tensor_scalar(m.var[:, :], m.mv[:, :, 1], LN_EPS, None, ALU.add).then_inc(m.ln_var, 1)
            dve.wait_ge(m.ln_std, k + 1)
            m.dve(dve.reciprocal(m.rstd[:, :], m.std[:, :]))
            m.dve.wait(dve)
            m.dve(dve.scalar_tensor_tensor(m.nmr[:, :], m.mv[:, :, 0], -1.0, m.rstd[:, :], ALU.mult, ALU.mult))
            m.dve.wait(dve)
            for i in range(NT):
                dve.tensor_scalar(m.xn[:, i, :], m.x[:, i, :], m.rstd[:, i:i + 1], m.nmr[:, i:i + 1],
                                  ALU.mult, ALU.add).then_inc(m.ln_xn, 1)
            for q in (1, 3):
                dve.wait_ge(m.ln_turned, 4 * k + q + 1)
                dve.tensor_copy(m.xnT[:, q * BANK:(q + 1) * BANK], m.ps[q][:, :]).then_inc(m.ln_copied, 1)

        @block.scalar
        def _(act):
            act.wait_ge(m.ln_var, k + 1)
            act.activation(m.std[:, :], m.var[:, :], ACT.Sqrt).then_inc(m.ln_std, 1)
            act_work(act)
            for q in (0, 2):
                act.wait_ge(m.ln_turned, 4 * k + q + 1)
                act.copy(m.xnT[:, q * BANK:(q + 1) * BANK], m.ps[q][:, :]).then_inc(m.ln_copied, 1)

        @block.tensor
        def _(pe):
            if k == 0:
                pe.wait_ge(m.early_in, 16)
            pe_work(pe)
            for i in range(NT):
                pe.wait_ge(m.ln_xn, NT * k + i + 1)
                ins = pe.transpose(m.ps[i // 4][:, i % 4 * P:i % 4 * P + P], m.xn[:, i, :], m.ident[:, :])
                if i % 4 == 3:
                    ins.then_inc(m.ln_turned, 1)


def first_loads(nc, m, a, sem):
    zeroed = sem("zeroed")

    def loads(sp):
        x = a["x"].rearrange("b (i p) d -> p b i d", p=P)
        for b in range(B):
            sp.dma_start(m.x[:, b * TB:(b + 1) * TB, :], x[:, b, :, :]).then_inc(m.x_in[b], 16)
            if b == 0:
                sp.dma_start(m.packs["early"][:, :], a["early"]).then_inc(m.early_in, 16)
        m.a0_loads(sp)
        m.fetch(sp.dma_start(m.packs["later"][:, :], a["later"]))
        m.fetch(sp.dma_start(m.packs["narrow"][:, :], a["narrow"]))
        sp.wait_ge(zeroed, 1)
        m.fetch(sp.dma_start(a["m2_pairs_out"].rearrange("(q p) d -> p q d", p=P), m.zero[:, :].unsqueeze(1).broadcast_to([P, 2 * NT, D])))

    def pool_work(pool):
        pool.memset(m.zero[:, :], 0.0).then_inc(zeroed, 1)
        pool.memset(m.xnT[:, N:N + P], 0.0).then_inc(zeroed, 1)
        pool.wait_ge(zeroed, 2)

    return loads, pool_work


def attention0(nc, m, a, sem, sb):
    kT = sb("a0_kT", [P, B, J])
    ctxv = sb("a0_ctxv", [J, B, D + 1])
    madd = sb("a0_madd", [1, B * J])
    maski = sb("a0_maski", [1, B * J], I32)
    ones1 = sb("a0_ones1", [1, P])
    qT = sb("a0_qT", [P, N])
    pr = sb("a0_pr", [P, B, TB, J])
    prT = sb("a0_prT", [J, N])
    mx = sb("a0_mx", [P, B, TB])
    rden = sb("a0_rden", [P, NT])
    ctx_loaded, k_ready, k_done, bias_done, q_ready, q_done, s_ready, sub_done, exp_done, t_ready, t_done, o_ready, x_done, narrowed = (
        sem("a0_" + n) for n in ("ctx_loaded", "k_ready", "k_done", "bias_done", "q_ready", "q_done", "s_ready", "sub_done",
                                 "exp_done", "t_ready", "t_done", "o_ready", "x_done", "narrowed"))

    def loads(sp):
        sp.dma_start(ctxv[:, :, 0:D], a["ctx"].rearrange("b j d -> j b d")).then_inc(ctx_loaded, 16)
        sp.dma_start(maski[:, :], a["mask0"].rearrange("b j -> (b j)").unsqueeze(0)).then_inc(ctx_loaded, 16)

    m.a0_loads = loads
    loads, pool_work = first_loads(nc, m, a, sem)
    yield loads, nothing, nothing, pool_work

    with nc.Block() as block:
        @block.sync
        def _(sp):
            m.fetch.wait(sp)

        @block.gpsimd
        def _(pool):
            m.fetch.wait(pool)
            pool.tensor_copy(m.narrow[:, :], m.packs["narrow"][:, :]).then_inc(narrowed, 1)
            pool.wait_ge(narrowed, 1)

        @block.tensor
        def _(pe):
            pe.matmul(m.ps[7][:, 0:B * J], m.w0T[:, :], m.ctxT[:, :, :], start=True, stop=True).then_inc(k_ready, 1)
            for s in range(B + 3):
                if s < B:
                    ge(pe, q_done, s - 1)
                    pe.matmul(m.ps[s % 2][:, :], m.w0T[:, :], m.xnT[:, s * S:(s + 1) * S],
                              start=True, stop=True).then_inc(q_ready, 1)
                if 1 <= s <= B:
                    b = s - 1
                    pe.wait_ge(q_done, b + 1)
                    if b == 0:
                        pe.wait_ge(k_done, 1)
                        pe.wait_ge(bias_done, 1)
                    ge(pe, sub_done, b - 1)
                    for t in range(TB):
                        o = m.ps[2 + b % 2][:, t * J:(t + 1) * J]
                        pe.matmul(o, qT[:, (b * TB + t) * P:(b * TB + t + 1) * P], kT[:, b, :], start=True, stop=False)
                        ins = pe.matmul(o, ones1[0:1, :], madd[:, b * J:(b + 1) * J], start=False, stop=True)
                    ins.then_inc(s_ready, 1)
                if 2 <= s <= B + 1:
                    b = s - 2
                    pe.wait_ge(exp_done, b + 1)
                    ge(pe, t_done, b - 1)
                    for t in range(TB):
                        ins = pe.transpose(m.ps[(4, 7)[b % 2]][0:J, t * P:(t + 1) * P], pr[:, b, t, :], m.ident[:, :])
                    ins.then_inc(t_ready, 1)
                if 3 <= s:
                    b = s - 3
                    pe.wait_ge(t_done, b + 1)
                    ge(pe, x_done, b)
                    if b == 0:
                        pe.wait_ge(ctx_loaded, 32)
                    for t in range(TB):
                        i = b * TB + t
                        ins = pe.matmul(m.ps[5 + t // 2][:, t % 2 * 129:t % 2 * 129 + 129], prT[:, i * P:(i + 1) * P],
                                        ctxv[:, b, :], start=True, stop=True)
                    ins.then_inc(o_ready, 1)

        @block.vector
        def _(dve):
            m.dve(dve.memset(ones1[:, :], 1.0))
            m.dve(dve.memset(ctxv[:, :, D:D + 1], 1.0))
            m.dve.wait(dve)
            dve.wait_ge(k_ready, 1)
            dve.tensor_scalar(kT[:, :, :], m.ps[7][:, 0:B * J].rearrange("p (b j) -> p b j", b=B), 0.0, m.diag0[:, 0:1],
                              ALU.max, ALU.mult).then_inc(k_done, 1)
            dve.wait_ge(ctx_loaded, 32)
            dve.tensor_scalar(madd[:, :], maski[:, :], 10000.0, -10000.0, ALU.mult, ALU.add).then_inc(bias_done, 1)
            for s in range(B + 3):
                if s < B:
                    dve.wait_ge(q_ready, s + 1)
                    dve.tensor_scalar(qT[:, s * S:(s + 1) * S], m.ps[s % 2][:, :], 0.0, None, ALU.max).then_inc(q_done, 1)
                if 1 <= s <= B:
                    b = s - 1
                    dve.wait_ge(s_ready, b + 1)
                    sc = m.ps[2 + b % 2][:, 0:TB * J].rearrange("p (t j) -> p t j", t=TB)
                    m.dve(dve.tensor_reduce(mx[:, b, :], sc, AX.X, ALU.max))
                    m.dve.wait(dve)
                    dve.tensor_tensor(pr[:, b, :, :], sc, mx[:, b, :].unsqueeze(2).broadcast_to([P, TB, J]),
                                      ALU.subtract).then_inc(sub_done, 1)
                if 3 <= s:
                    b = s - 3
                    dve.wait_ge(o_ready, b + 1)
                    for t in range(TB):
                        i = b * TB + t
                        m.dve(dve.reciprocal(rden[:, i:i + 1], m.ps[5 + t // 2][:, t % 2 * 129 + 128:t % 2 * 129 + 129]))
                    m.dve.wait(dve)
                    for t in range(TB):
                        i = b * TB + t
                        ins = dve.scalar_tensor_tensor(m.x[:, i, :], m.ps[5 + t // 2][:, t % 2 * 129:t % 2 * 129 + 128],
                                                       rden[:, i:i + 1], m.x[:, i, :], ALU.mult, ALU.add)
                        m.dve(ins)
                    m.dve.wait(dve)
                    dve.sem_inc(x_done, 1)

        @block.scalar
        def _(act):
            for s in range(1, B + 2):
                if s <= B:
                    b = s - 1
                    act.wait_ge(sub_done, b + 1)
                    act.activation(pr[:, b, :, :], pr[:, b, :, :], ACT.Exp).then_inc(exp_done, 1)
                if s >= 2:
                    b = s - 2
                    act.wait_ge(t_ready, b + 1)
                    act.copy(prT[:, b * S:(b + 1) * S], m.ps[(4, 7)[b % 2]][0:J, :]).then_inc(t_done, 1)


def moe(nc, m, a, sem, sb, name, blocks, topk, cap, biased, gated, act_fn, x_stage):
    G, k = blocks, topk
    Q = k * NT
    U = 8
    assert G % U == 0
    w1 = sb(name + "_w1", [P, E, F])
    w2 = sb(name + "_w2", [P, E, FC, D])
    w3 = sb(name + "_w3", [P, E, F]) if gated else None
    b1 = sb(name + "_b1", [P, E, F]) if biased else None
    b2 = sb(name + "_b2", [P, E, D]) if biased else None
    weights = [("w1", w1), ("w2", w2)] + ([("w3", w3)] if gated else []) + ([("b1", b1), ("b2", b2)] if biased else [])

    def loads(sp):
        for n, t in weights:
            dst = t[:, :, :, :].rearrange("p e c d -> p e (c d)") if n == "w2" else t[:, :, :]
            for half in (slice(0, E // 2), slice(E // 2, E)):
                m.fetch(sp.dma_start(dst[:, half, :], a[f"{name}_{n}"][half, :, :].rearrange("e p f -> p e f")))

    (logits_ready, shifted, exped, sel_ready, rank_ready, slots_known, index_ready, index_done, table_ready, xn_out,
     xT_ready, xT_done, h_ready, h_act, h_done, hT_ready, hT_done, y_ready, y_done, gnow_done, snow_done, pool_pass) = (
        sem(f"{name}_{n}") for n in (
        "logits_ready", "shifted", "exped", "sel_ready", "rank_ready", "slots_known", "index_ready", "index_done",
        "table_ready", "xn_out", "xT_ready", "xT_done", "h_ready", "h_act", "h_done", "hT_ready", "hT_done",
        "y_ready", "y_done", "gnow_done", "snow_done", "pool_pass"))
    x_in, scattered = ([sem(f"{name}_{n}{sl}") for sl in range(U)] for n in ("x_in", "scattered"))
    back_in = [sem(f"{name}_back_in{q}") for q in range(B)]
    bt = lambda ap: ap.unsqueeze(1).broadcast_to([P, NT, E])
    be = lambda ap: ap.unsqueeze(2).broadcast_to([P, NT, E])
    wt = [sb(f"{name}_wt{i}", [P, NT]) for i in range(k)]
    btabi = sb(name + "_btabi", [1, G], I32)
    gidx = sb(name + "_gidx", [P, G], U32)
    sidx = sb(name + "_sidx", [P, G], U32)
    yield (loads,)
    fetched = m.fetch.n

    pairs_in, pairs_out = a["pairs_in"][0:Q * P, :], a[f"{name}_pairs_out"]

    with ExitStack() as inner:
        tp = lambda n, shape, dt=F32: inner.enter_context(nc.sbuf_tensor(f"{name}_{n}", shape, dt))
        lg, l2 = tp("lg", [P, NT, E]), tp("l2", [P, NT, E])
        tmp = [tp(f"tmp{i}", [P, NT, E]) for i in range(2)]
        oh = [tp(f"oh{i}", [P, NT, E]) for i in range(k)]
        top = [tp(f"top{i}", [P, NT]) for i in range(k)]
        low, den = tp("low", [P, NT]), tp("den", [P, NT])
        dif, ex = (tp(n, [P, NT, E] if k == 1 else [P, NT]) for n in ("dif", "ex"))
        sel = tp("sel", [P, NT, E], BF16)
        tot, run, over = (tp(n, [P, E, NT]) for n in ("tot", "run", "over"))
        rank, keep = tp("rank", [P, NT, E]), tp("keep", [P, NT, E])
        cnt, nblk, bend, base = (tp(n, [P, E]) for n in ("cnt", "nblk", "bend", "base"))
        pos = tp("pos", [P, k, NT])
        kept = tp("kept", [P, NT])
        div, mod = tp("div", [P, Q]), tp("mod", [P, Q])
        rowhot = tp("rowhot", [P, Q, P], BF16)
        blkhot = tp("blkhot", [P, Q, G], BF16)
        code = tp("code", [P, Q, 2, G], BF16)
        found, ffree = tp("found", [P, G]), tp("ffree", [P, G])
        cmpt, btab = tp("cmpt", [1, G, E]), tp("btab", [1, G])

        with nc.Block() as block:
            @block.sync
            def _(sp):
                for j in range(k):
                    sp.dma_start(pairs_in[j * N:(j + 1) * N, :].rearrange("(i p) d -> p i d", p=P), m.xn[:, :, :]).then_inc(xn_out, 16)
                sp.wait_ge(xn_out, 16 * k)

            @block.tensor
            def _(pe):
                for i in range(NT):
                    ins = pe.matmul(m.ps[0][:, i * E:(i + 1) * E], m.xnT[:, i * P:(i + 1) * P], m.small[name + "_router"][:, :],
                                    start=True, stop=True)
                ins.then_inc(logits_ready, 1)
                pe.wait_ge(sel_ready, 1)
                pe.matmul(m.ps[1][:, 0:P], m.tri[:, :], sel[:, :, :], start=True, stop=True)
                pe.matmul(m.ps[2][:, 0:P], m.onesb[:, :], sel[:, :, :], start=True, stop=True).then_inc(rank_ready, 1)
                for q in range(Q):
                    pe.wait_ge(slots_known, q // NT + 1)
                    ins = pe.matmul(m.ps[3][:, 0:2 * G], rowhot[:, q, :], code[:, q, :, :], start=(q == 0), stop=(q == Q - 1))
                ins.then_inc(index_ready, 1)

            @block.scalar
            def _(act):
                act.wait_ge(shifted, 1)
                sl = tuple([slice(None)] * len(dif.shape))
                act.activation(ex[sl], dif[sl], ACT.Exp).then_inc(exped, 1)

            @block.vector
            def _(dve):
                c = m.dve

                def step(ins):
                    c(ins)
                    c.wait(dve)

                dve.wait_ge(logits_ready, 1)
                logits = m.ps[0][:, 0:NT * E].rearrange("p (i e) -> p i e", e=E)
                if biased:
                    step(dve.tensor_tensor(lg[:, :, :], logits, bt(m.small[name + "_rbias"][:, :]), ALU.add))
                else:
                    step(dve.tensor_copy(lg[:, :, :], logits))
                src = lg
                for j in range(k):
                    step(dve.tensor_reduce(top[j][:, :], src[:, :, :], AX.X, ALU.max))
                    step(dve.tensor_tensor(tmp[0][:, :, :], src[:, :, :], be(top[j][:, :]), ALU.is_equal))
                    step(dve.scalar_tensor_tensor(tmp[1][:, :, :], tmp[0][:, :, :], -float(E), bt(m.iota8[:, :]), ALU.mult, ALU.add))
                    step(dve.tensor_reduce(low[:, :], tmp[1][:, :, :], AX.X, ALU.min))
                    step(dve.scalar_tensor_tensor(oh[j][:, :, :], bt(m.iota8[:, :]), -float(E), be(low[:, :]), ALU.add, ALU.is_equal))
                    if j + 1 < k:
                        step(dve.scalar_tensor_tensor(l2[:, :, :], oh[j][:, :, :], -1e30, lg[:, :, :], ALU.mult, ALU.add))
                        src = l2
                if k == 1:
                    dve.tensor_tensor(dif[:, :, :], lg[:, :, :], be(top[0][:, :]), ALU.subtract).then_inc(shifted, 1)
                    dve.tensor_copy(sel[:, :, :], oh[0][:, :, :]).then_inc(sel_ready, 1)
                    dve.wait_ge(exped, 1)
                    step(dve.tensor_reduce(den[:, :], ex[:, :, :], AX.X, ALU.add))
                    step(dve.reciprocal(wt[0][:, :], den[:, :]))
                else:
                    dve.tensor_tensor(dif[:, :], top[1][:, :], top[0][:, :], ALU.subtract).then_inc(shifted, 1)
                    dve.tensor_tensor(sel[:, :, :], oh[0][:, :, :], oh[1][:, :, :], ALU.add).then_inc(sel_ready, 1)
                    dve.wait_ge(exped, 1)
                    step(dve.tensor_scalar(den[:, :], ex[:, :], 1.0, None, ALU.add))
                    step(dve.reciprocal(wt[0][:, :], den[:, :]))
                    step(dve.tensor_tensor(wt[1][:, :], ex[:, :], wt[0][:, :], ALU.mult))
                dve.wait_ge(rank_ready, 1)
                step(dve.tensor_copy(tot[:, :, :], m.ps[2][:, 0:P].rearrange("p (i e) -> p e i", e=E)))
                step(dve.tensor_tensor_scan(run[:, :, :].rearrange("p e i -> p (e i)"), m.restart[:, :],
                                            tot[:, :, :].rearrange("p e i -> p (e i)"), 0.0, ALU.mult, ALU.add))
                step(dve.tensor_tensor(over[:, :, :], run[:, :, :], tot[:, :, :], ALU.subtract))
                step(dve.tensor_tensor(rank[:, :, :], m.ps[1][:, 0:P].rearrange("p (i e) -> p i e", e=E),
                                       over[:, :, :].rearrange("p e i -> p i e"), ALU.add))
                step(dve.tensor_scalar(cnt[:, :], run[:, :, NT - 1], float(cap if cap else N), None, ALU.min))
                step(dve.tensor_tensor(over[:, :, :], cnt[:, :].unsqueeze(2).broadcast_to([P, E, NT]),
                                       m.iota128[:, :].unsqueeze(1).broadcast_to([P, E, NT]), ALU.is_gt))
                step(dve.tensor_reduce(nblk[:, :], over[:, :, :], AX.X, ALU.add))
                step(dve.tensor_tensor_scan(bend[:, :], m.one8[:, :], nblk[:, :], 0.0, ALU.mult, ALU.add))
                step(dve.tensor_tensor(base[:, :], bend[:, :], nblk[:, :], ALU.subtract))
                if cap:
                    step(dve.tensor_scalar(keep[:, :, :], rank[:, :, :], float(cap), None, ALU.is_lt))
                step(dve.scalar_tensor_tensor(rank[:, :, :], bt(base[:, :]), float(P), rank[:, :, :], ALU.mult, ALU.add))
                for j in range(k):
                    step(dve.tensor_tensor(tmp[0][:, :, :], oh[j][:, :, :], rank[:, :, :], ALU.mult))
                    step(dve.tensor_reduce(pos[:, j, :], tmp[0][:, :, :], AX.X, ALU.add))
                    if cap:
                        step(dve.tensor_tensor(tmp[0][:, :, :], oh[j][:, :, :], keep[:, :, :], ALU.mult))
                        step(dve.tensor_reduce(kept[:, :], tmp[0][:, :, :], AX.X, ALU.add))
                        step(dve.tensor_tensor(wt[j][:, :], wt[j][:, :], kept[:, :], ALU.mult))
                        step(dve.tensor_scalar(kept[:, :], kept[:, :], -float(2 * G * P), float(2 * G * P), ALU.mult, ALU.add))
                        step(dve.tensor_tensor(pos[:, j, :], pos[:, j, :], kept[:, :], ALU.add))
                flat = pos[:, :, :].rearrange("p j i -> p (j i)")
                step(dve.tensor_scalar(div[:, :], flat, 1.0 / P, -63.5 / P, ALU.mult, ALU.add))
                step(dve.tensor_scalar(div[:, :], div[:, :], MAGIC, MAGIC, ALU.add, ALU.subtract))
                step(dve.scalar_tensor_tensor(mod[:, :], div[:, :], -float(P), flat, ALU.mult, ALU.add))
                for j in range(k):
                    own = slice(j * NT, (j + 1) * NT)
                    each = lambda t, n: t.unsqueeze(2).broadcast_to([P, NT, n])
                    row = lambda t, n: t.unsqueeze(1).broadcast_to([P, NT, n])
                    step(dve.tensor_tensor(blkhot[:, own, :], each(div[:, own], G), row(m.small["iotag"][:, 0:G], G), ALU.is_equal))
                    step(dve.tensor_tensor(code[:, own, 0, :], blkhot[:, own, :], each(m.small["tile1"][:, own], G), ALU.mult))
                    step(dve.tensor_scalar(code[:, own, 1, :], blkhot[:, own, :], m.small["part"][:, 0:1], None, ALU.mult))
                    dve.tensor_tensor(rowhot[:, own, :], each(mod[:, own], P), row(m.small["iotar"][:, :], P), ALU.is_equal).then_inc(slots_known, 1)
                step(dve.tensor_tensor(cmpt[:, :, :], m.small["iotag"][0:1, 0:G].unsqueeze(2).broadcast_to([1, G, E]),
                                       bend[0:1, :].unsqueeze(1).broadcast_to([1, G, E]), ALU.is_ge))
                step(dve.tensor_reduce(btab[:, :], cmpt[:, :, :], AX.X, ALU.add))
                dve.tensor_scalar(btabi[:, :], btab[:, :], float(E - 1), None, ALU.min).then_inc(table_ready, 1)
                dve.wait_ge(index_ready, 1)
                step(dve.tensor_copy(ffree[:, :], m.ps[3][:, G:2 * G]))
                step(dve.scalar_tensor_tensor(found[:, :], m.ps[3][:, 0:G], float(P), ffree[:, :], ALU.mult, ALU.add))
                step(dve.tensor_scalar(found[:, :], found[:, :], -float(P), None, ALU.add))
                step(dve.tensor_scalar(ffree[:, :], found[:, :], 0.0, float(2 * Q * P), ALU.is_lt, ALU.mult))
                dve.tensor_scalar(gidx[:, :], found[:, :], 0.0, None, ALU.max).then_inc(index_done, 1)
                dve.tensor_tensor(sidx[:, :], found[:, :], ffree[:, :], ALU.add).then_inc(index_done, 1)
                dve.wait_ge(index_done, 2)

    xb = sb(name + "_xb", [P, U, D])
    xT = sb(name + "_xT", [P, 2, P])
    hg = sb(name + "_hg", [P, 2, F]) if gated else None
    h = sb(name + "_h", [P, 2, F])
    hT = sb(name + "_hT", [P, 2, F])
    yb = sb(name + "_yb", [P, U, D])
    gnow, snow = (sb(f"{name}_{n}", [P, U], U32) for n in ("gnow", "snow"))
    IT = G // U
    LAG = U - 2

    def back(n, sl, by):
        if sl < by:
            n, sl = n - 1, sl + U
        if isinstance(n, int) and not 0 <= n < IT:
            return None
        return n, sl - by

    def loop(eng, body, tail):
        for sl in range(U):
            body(0, sl)
        with eng.Fori(1, IT) as n:
            for sl in range(U):
                body(n, sl)
        for sl in range(tail):
            body(IT, sl)

    with nc.Block() as block:
        @block.gpsimd
        def _(pool):
            def indices(nn, ss, table, now, done):
                g = nn * U + ss
                pool.sem_inc(pool_pass, 1)
                pool.tensor_copy(now[:, ss:ss + U // 2], table[:, bass.ds(g, U // 2)]).then_inc(done, 1)
                pool.wait_ge(done, 2 * nn + ss // (U // 2) + 1)
                pool.sem_inc(pool_pass, 1)

            def body(n, sl):
                if (at := back(n, sl, 0)):
                    g = at[0] * U + sl
                    if sl % (U // 2) == 0:
                        ge(pool, xT_ready, g - U // 2)
                        indices(n, sl, gidx, gnow, gnow_done)
                    else:
                        ge(pool, xT_ready, g + 1 - U)
                        pool.sem_inc(pool_pass, 1)
                    pool.indirect_dma_start(out=xb[:, sl, :], out_offset=None, in_=pairs_in,
                                            in_offset=bass.IndirectOffsetOnAxis(ap=gnow[:, sl:sl + 1], axis=0)).then_inc(x_in[sl], 16)
                if (at := back(n, sl, LAG)):
                    nn, ss = at
                    g = nn * U + ss
                    if ss % (U // 2) == 0:
                        for other in range(ss, ss + U // 2):
                            ge(pool, scattered[other], 16 * nn)
                        indices(nn, ss, sidx, snow, snow_done)
                    pool.wait_ge(y_done, g + 1)
                    pool.sem_inc(pool_pass, 1)
                    pool.indirect_dma_start(out=pairs_out, out_offset=bass.IndirectOffsetOnAxis(ap=snow[:, ss:ss + 1], axis=0),
                                            in_=yb[:, ss, :], in_offset=None, bounds_check=Q * P - 1,
                                            oob_is_err=False).then_inc(scattered[ss], 16)

            loop(pool, body, LAG)

        @block.tensor
        def _(pe):
            def body(n, sl):
                if (at := back(n, sl, 0)):
                    g = at[0] * U + sl
                    pe.wait_ge(x_in[sl], 16 * (n + 1))
                    ge(pe, xT_done, g)
                    pe.transpose(m.ps[0][:, 0:P], xb[:, sl, :], m.ident[:, :]).then_inc(xT_ready, 1)
                if (at := back(n, sl, 1)):
                    nn, ss = at
                    g = nn * U + ss
                    e = pe.value_load(btabi[0:1, bass.ds(g, 1)], min_val=0, max_val=E - 1)
                    pe.wait_ge(xT_done, g + 1)
                    ge(pe, h_done, g - 1)
                    for q, w in enumerate((w1, w3) if gated else (w1,)):
                        ins = pe.matmul(m.ps[1 + 2 * q + ss % 2][:, :], xT[:, ss % 2, :],
                                        w[:, bass.ds(e, 1), :].rearrange("p e f -> p (e f)"), start=True, stop=True)
                    ins.then_inc(h_ready, 1)
                if (at := back(n, sl, 2)):
                    nn, ss = at
                    g = nn * U + ss
                    pe.wait_ge(h_done, g + 1)
                    ge(pe, hT_done, g - 1)
                    for f in range(FC):
                        ins = pe.transpose(m.ps[5 + ss % 2][:, f * P:(f + 1) * P], h[:, ss % 2, f * P:(f + 1) * P], m.ident[:, :])
                    ins.then_inc(hT_ready, 1)
                if (at := back(n, sl, 3)):
                    nn, ss = at
                    g = nn * U + ss
                    e = pe.value_load(btabi[0:1, bass.ds(g, 1)], min_val=0, max_val=E - 1)
                    pe.wait_ge(hT_done, g + 1)
                    ge(pe, y_done, g)
                    for f in range(FC):
                        ins = pe.matmul(m.ps[7][:, 0:D], hT[:, ss % 2, f * P:(f + 1) * P],
                                        w2[:, bass.ds(e, 1), f, :].rearrange("p e d -> p (e d)"), start=(f == 0), stop=(f == FC - 1))
                    ins.then_inc(y_ready, 1)

            pe.wait_ge(m.fetch.sem, 16 * fetched)
            loop(pe, body, 3)

        @block.scalar
        def _(act):
            def body(n, sl):
                if act_fn is not None and (at := back(n, sl, 1)):
                    nn, ss = at
                    g = nn * U + ss
                    act.wait_ge(h_ready, g + 1)
                    if gated:
                        ge(act, h_done, g - 1)
                        act.activation(hg[:, ss % 2, :], m.ps[1 + ss % 2][:, :], act_fn).then_inc(h_act, 1)
                    else:
                        ge(act, hT_ready, g - 1)
                        act.activation(h[:, ss % 2, :], m.ps[1 + ss % 2][:, :], act_fn).then_inc(h_done, 1)
                if (gated or biased) and (at := back(n, sl, 2)):
                    nn, ss = at
                    g = nn * U + ss
                    act.wait_ge(hT_ready, g + 1)
                    ge(act, y_ready, g - 1)
                    if biased:
                        act.activation(hT[:, ss % 2, :], m.ps[5 + ss % 2][:, :], ACT.Relu).then_inc(hT_done, 1)
                    else:
                        act.copy(hT[:, ss % 2, :], m.ps[5 + ss % 2][:, :]).then_inc(hT_done, 1)

            loop(act, body, 2)

        @block.vector
        def _(dve):
            def body(n, sl):
                if (at := back(n, sl, 0)):
                    g = at[0] * U + sl
                    dve.wait_ge(xT_ready, g + 1)
                    ge(dve, h_ready, g - 1)
                    dve.tensor_copy(xT[:, sl % 2, :], m.ps[0][:, 0:P]).then_inc(xT_done, 1)
                if act_fn is None or gated:
                    if (at := back(n, sl, 1)):
                        nn, ss = at
                        g = nn * U + ss
                        if gated:
                            dve.wait_ge(h_act, g + 1)
                            ge(dve, hT_ready, g - 1)
                            dve.tensor_tensor(h[:, ss % 2, :], hg[:, ss % 2, :], m.ps[3 + ss % 2][:, :], ALU.mult).then_inc(h_done, 1)
                        else:
                            e = dve.value_load(btabi[0:1, bass.ds(g, 1)], min_val=0, max_val=E - 1)
                            dve.wait_ge(h_ready, g + 1)
                            ge(dve, hT_ready, g - 1)
                            dve.tensor_tensor(h[:, ss % 2, :], m.ps[1 + ss % 2][:, :],
                                              b1[:, bass.ds(e, 1), :].rearrange("p e f -> p (e f)"), ALU.add).then_inc(h_done, 1)
                elif (at := back(n, sl, 2)):
                    nn, ss = at
                    g = nn * U + ss
                    dve.wait_ge(hT_ready, g + 1)
                    ge(dve, y_ready, g - 1)
                    dve.tensor_copy(hT[:, ss % 2, :], m.ps[5 + ss % 2][:, :]).then_inc(hT_done, 1)
                if (at := back(n, sl, 3)):
                    nn, ss = at
                    g = nn * U + ss
                    if biased:
                        e = dve.value_load(btabi[0:1, bass.ds(g, 1)], min_val=0, max_val=E - 1)
                    dve.wait_ge(y_ready, g + 1)
                    ge(dve, scattered[ss], 16 * nn)
                    if biased:
                        dve.tensor_tensor(yb[:, ss, :], m.ps[7][:, 0:D],
                                          b2[:, bass.ds(e, 1), :].rearrange("p e d -> p (e d)"), ALU.add).then_inc(y_done, 1)
                    else:
                        dve.tensor_copy(yb[:, ss, :], m.ps[7][:, 0:D]).then_inc(y_done, 1)

            loop(dve, body, 3)

    got = sb(name + "_got", [P, Q, D])
    with nc.Block() as block:
        @block.sync
        def _(sp):
            for q in scattered:
                sp.wait_ge(q, 16 * IT)
            rows = pairs_out.rearrange("(q p) d -> p q d", p=P)
            for b in range(B):
                for j in range(k):
                    tiles = slice(j * NT + b * TB, j * NT + (b + 1) * TB)
                    sp.dma_start(got[:, tiles, :], rows[:, tiles, :]).then_inc(back_in[b], 16)

        @block.vector
        def _(dve):
            if x_stage:
                m.dve(dve.tensor_tensor(m.x[:, :, :], m.x[:, :, :], m.xn[:, :, :], ALU.add))
                m.dve.wait(dve)
            for b in range(B):
                dve.wait_ge(back_in[b], 16 * k)
                for j in range(k):
                    for i in range(b * TB, (b + 1) * TB):
                        m.dve(dve.scalar_tensor_tensor(m.x[:, i, :], got[:, j * NT + i, :], wt[j][:, i:i + 1], m.x[:, i, :],
                                                       ALU.mult, ALU.add))
                    m.dve.wait(dve)


def context_heads(m, sem, sb, name, keys, kbias, values, vbias):
    kT = sb(name + "_kT", [P, B, J]) if keys is not None else m.ctxT
    kb = sb(name + "_kb", [P, B, H, J])
    vf = sb(name + "_vf", [P, B, NC, CH * (HD + 1)])
    vraw = sb(name + "_vraw", [P, B, NC * CH * HD])
    k_ready, k_done, kb_done, v_ready, v_copied, v_biased, vf_done = (
        sem(f"{name}_{n}") for n in ("k_ready", "k_done", "kb_done", "v_ready", "v_copied", "v_biased", "vf_done"))

    def pe_work(pe):
        if keys is not None:
            pe.matmul(m.ps[6][:, 0:B * J], keys[:, :], m.ctxT[:, :, :], start=True, stop=True).then_inc(k_ready, 1)
        for b in range(B):
            ge(pe, v_copied, b - 1)
            for n, c in enumerate(CHUNKS):
                ins = pe.matmul(m.ps[4 + b % 2][:, n * CH * HD:(n + 1) * CH * HD], m.ctxT3[:, b, c.row:c.row + P],
                                values[:, c.h0 * HD:(c.h0 + CH) * HD], start=True, stop=True)
            ins.then_inc(v_ready, 1)

    def act_work(act):
        if keys is not None:
            act.wait_ge(k_ready, 1)
            act.copy(kT[:, :, :], m.ps[6][:, 0:B * J].rearrange("p (b j) -> p b j", b=B)).then_inc(k_done, 1)
        for b in range(B):
            act.wait_ge(v_ready, b + 1)
            act.copy(vraw[:, b, :], m.ps[4 + b % 2][:, 0:NC * CH * HD]).then_inc(v_copied, 1)

    def pool_work(pool):
        if keys is not None:
            pool.wait_ge(k_done, 1)
            pool.tensor_scalar(kT[:, :, :], kT[:, :, :], kbias[:, 0:1], None, ALU.add).then_inc(k_done, 1)
            pool.wait_ge(k_done, 2)
        mask = m.small["vmask"][:, :]
        for b in range(B):
            pool.tensor_tensor(kb[:, b, :, :], kT[:, b, :].unsqueeze(1).broadcast_to([P, H, J]),
                               m.small["qmask"][:, :].unsqueeze(2).broadcast_to([P, H, J]), ALU.mult).then_inc(kb_done, 1)
            out = vf[:, b, :, :].rearrange("p c (h e) -> p (c h) e", e=HD + 1)
            pool.wait_ge(v_copied, b + 1)
            if vbias is not None:
                pool.tensor_tensor(vraw[:, b, :], vraw[:, b, :], vbias[:, :], ALU.add).then_inc(v_biased, 1)
                pool.wait_ge(v_biased, b + 1)
            pool.tensor_tensor(out[:, :, 0:HD], vraw[:, b, :].rearrange("p (c e) -> p c e", e=HD),
                               mask.unsqueeze(2).broadcast_to([P, NC * CH, HD]), ALU.mult).then_inc(vf_done, 1)
            pool.tensor_copy(out[:, :, HD], mask).then_inc(vf_done, 1)
        pool.wait_ge(kb_done, B)
        pool.wait_ge(vf_done, 2 * B)

    return kb, vf, pe_work, act_work, pool_work


LATE = NG - 1


def rotate(eng, body, lag):
    for t in range(TB):
        body(0, t)
    with eng.Fori(1, B) as b:
        for t in range(TB):
            body(b, t)
    for t in range(lag):
        body(B, t)


def due(b, t, by):
    while t < by:
        b, t = b - 1, t + TB
    if isinstance(b, int) and not 0 <= b < B:
        return None
    return b, t - by


def turn_queries(m, pool, b, t, qT, s_ready, q_done, pool_pass):
    ge(pool, s_ready, b * TB + t - 2)
    pool.sem_inc(pool_pass, 1)
    at = (t + 1) % TB * P
    pool.tensor_copy(qT[:, at:at + P], m.xnT[:, bass.ds(b * S + (t + 1) * P, P)]).then_inc(q_done, 1)


def attention8(nc, m, a, sem, sb, name, scale, projected, masked):
    if projected:
        kb, vf, pe_work, act_work, pool_work = context_heads(m, sem, sb, name, m.small["wkT"], m.small["bk"], m.small["wvT"], m.small["bv"])
        wo, bo = m.small["woT"], m.small["bo"]
    else:
        kb, vf, pe_work, act_work, pool_work = context_heads(m, sem, sb, name, None, None, m.ident, None)
        wo, bo = m.small["woutT"], m.small["bout"]
    (q_ready, q_biased, q_done, s_ready, sub_done, exp_done, t_ready, t_done, pv_ready, o_done, oT_ready,
     oT_done, y_ready, x_biased, x_done, max_done, rden_done, pool_pass, mask_done) = (
        sem(f"{name}_{n}") for n in (
        "q_ready", "q_biased", "q_done", "s_ready", "sub_done", "exp_done", "t_ready", "t_done", "pv_ready",
        "o_done", "oT_ready", "oT_done", "y_ready", "x_biased", "x_done", "max_done", "rden_done", "pool_pass", "mask_done"))
    qT = sb(name + "_qT", [P, S])
    pr = sb(name + "_pr", [P, 2, HJ])
    prT = sb(name + "_prT", [P, 2, NC * P])
    mx = sb(name + "_mx", [P, 2, H])
    rden = sb(name + "_rden", [P, 2, H])
    o = sb(name + "_o", [P, 2, D])
    oT = sb(name + "_oT", [P, 2, P])
    if masked:
        maski = sb(name + "_maski", [P, NT, J], I32)
        madd = sb(name + "_madd", [P, NT, J], BF16)
    scores = [m.ps[i][:, 0:QJ] for i in range(4)]
    PV, OB = m.ps[6], m.ps[7]
    def loads(sp):
        if masked:
            m.fetch(sp.dma_start(maski[:, :, :], a["mask3"].rearrange("b (i p) j -> p (b i) j", p=P)))

    def pool_part(pool):
        if masked:
            m.fetch.wait(pool)
            pool.tensor_scalar(madd[:, :, :], maski[:, :, :], 0.0, MASKED, ALU.is_equal, ALU.mult).then_inc(mask_done, 1)
            pool.wait_ge(mask_done, 1)
        pool_work(pool)

    yield loads, pe_work, act_work, pool_part

    with nc.Block() as block:
        @block.gpsimd
        def _(pool):
            if projected:
                pool.wait_ge(q_biased, 1)
            pool.tensor_copy(qT[:, 0:P], m.xnT[:, 0:P]).then_inc(q_done, 1)
            if projected:
                pool.wait_ge(q_biased, 2)
            for t in range(TB):
                turn_queries(m, pool, 0, t, qT, s_ready, q_done, pool_pass)
                if t == 0:
                    pool.tensor_tensor(m.x[:, :, :], m.x[:, :, :], bo[:, :].unsqueeze(1).broadcast_to([P, NT, D]), ALU.add).then_inc(x_biased, 1)
            if projected:
                pool.wait_ge(q_biased, B)
            with pool.Fori(1, B) as b:
                for t in range(TB):
                    turn_queries(m, pool, b, t, qT, s_ready, q_done, pool_pass)

        @block.tensor
        def _(pe):
            def body(b, t):
                if (at := due(b, t, 0)):
                    i = at[0] * TB + at[1]
                    pe.wait_ge(q_done, i + 1)
                    ge(pe, sub_done, i)
                    for r in range(4):
                        ins = pe.matmul(scores[r], qT[:, t * P:(t + 1) * P],
                                        kb[:, bass.ds(at[0], 1), r * QH:(r + 1) * QH, :].rearrange("p b h j -> p (b h j)"),
                                        start=True, stop=not masked)
                    if masked:
                        for r in range(4):
                            ins = pe.matmul(scores[r], m.small["identb"][:, :],
                                            madd[:, bass.ds(i, 1), :].broadcast_to([P, QH, J]), start=False, stop=True)
                    ins.then_inc(s_ready, 1)

                def turn(groups):
                    if (at := due(b, t, 1)):
                        i = at[0] * TB + at[1]
                        if 0 in groups:
                            pe.wait_ge(exp_done, i + 1)
                        for g in groups:
                            ge(pe, t_done, NG * i + g - 1)
                            for n, ch in enumerate(GROUPS[g]):
                                c = CHUNKS[ch]
                                ins = pe.transpose(m.ps[4 + (NG * at[1] + g) % 2][0:c.width, n * P:(n + 1) * P],
                                                   pr[:, at[1] % 2, c.at:c.at + c.width], m.ident[:, :])
                            ins.then_inc(t_ready, 1)

                turn(range(LATE))
                if (at := due(b, t, 3)):
                    i = at[0] * TB + at[1]
                    pe.wait_ge(o_done, i + 1)
                    ge(pe, x_done, i)
                    pe.transpose(OB[:, 0:P], o[:, at[1] % 2, :], m.ident[:, :]).then_inc(oT_ready, 1)
                if (at := due(b, t, 2)):
                    i = at[0] * TB + at[1]
                    pe.wait_ge(t_done, NG * (i + 1))
                    ge(pe, o_done, i)
                    for n, c in enumerate(CHUNKS):
                        ins = pe.matmul(PV[:, c.h0 * 9:(c.h0 + CH) * 9], prT[0:c.width, at[1] % 2, n * P:(n + 1) * P],
                                        vf[0:c.width, bass.ds(at[0], 1), n, :].rearrange("p b e -> p (b e)"),
                                        start=(n == 0), stop=(n == NC - 1), skip_group_check=True)
                    ins.then_inc(pv_ready, 1)
                turn([LATE])
                if (at := due(b, t, 3)):
                    i = at[0] * TB + at[1]
                    pe.wait_ge(oT_done, i + 1)
                    pe.matmul(OB[:, P:P + D], oT[:, at[1] % 2, :], wo[:, :], start=True, stop=True).then_inc(y_ready, 1)

            if projected:
                for b in range(B):
                    pe.matmul(m.ps[b][:, :], m.small["wqT"][:, :], m.xnT[:, b * S:(b + 1) * S], start=True, stop=True).then_inc(q_ready, 1)
                pe.wait_ge(q_biased, B)
            rotate(pe, body, 3)

        @block.vector
        def _(dve):
            if projected:
                for b in range(B):
                    dve.wait_ge(q_ready, b + 1)
                    dve.tensor_scalar(m.xnT[:, b * S:(b + 1) * S], m.ps[b][:, :], m.small["bq"][:, 0:1], None, ALU.add).then_inc(q_biased, 1)
            bank4 = m.all_banks[:, 0:4, 0:QJ].rearrange("p r (h j) -> p r h j", h=QH)

            def body(b, t):
                if (at := due(b, t, 0)):
                    i = at[0] * TB + at[1]
                    dve.wait_ge(s_ready, i + 1)
                    dve.tensor_reduce(mx[:, t % 2, :], bank4, AX.X, ALU.max).then_inc(max_done, 1)
                    dve.wait_ge(max_done, i + 1)
                    ge(dve, t_ready, NG * (i - 1))
                    dve.tensor_tensor(pr[:, t % 2, :].rearrange("p (r h j) -> p r h j", r=4, h=QH), bank4,
                                      mx[:, t % 2, :].rearrange("p (r h) -> p r h", r=4).unsqueeze(3).broadcast_to([P, 4, QH, J]),
                                      ALU.subtract).then_inc(sub_done, 1)
                if (at := due(b, t, 3)):
                    i = at[0] * TB + at[1]
                    dve.wait_ge(oT_ready, i + 1)
                    dve.tensor_copy(oT[:, at[1] % 2, :], OB[:, 0:P]).then_inc(oT_done, 1)
                if (at := due(b, t, 2)):
                    i = at[0] * TB + at[1]
                    pv = PV[:, 0:H * 9].rearrange("p (h e) -> p h e", e=9)
                    dve.wait_ge(pv_ready, i + 1)
                    dve.reciprocal(rden[:, at[1] % 2, :], pv[:, :, HD]).then_inc(rden_done, 1)
                    dve.wait_ge(rden_done, i + 1)
                    dve.tensor_tensor(o[:, at[1] % 2, :].rearrange("p (h e) -> p h e", e=HD), pv[:, :, 0:HD],
                                      rden[:, at[1] % 2, :].unsqueeze(2).broadcast_to([P, H, HD]), ALU.mult).then_inc(o_done, 1)
                if (at := due(b, t, 3)):
                    i = at[0] * TB + at[1]
                    dve.wait_ge(y_ready, i + 1)
                    if isinstance(i, int) and i == 0:
                        dve.wait_ge(x_biased, 1)
                    xi = m.x[:, bass.ds(i, 1), :].rearrange("p i d -> p (i d)")
                    dve.tensor_tensor(xi, xi, OB[:, P:P + D], ALU.add).then_inc(x_done, 1)

            rotate(dve, body, 3)

        @block.scalar
        def _(act):
            def body(b, t):
                def copy(groups):
                    if (at := due(b, t, 1)):
                        i = at[0] * TB + at[1]
                        for g in groups:
                            group = GROUPS[g]
                            act.wait_ge(t_ready, NG * i + g + 1)
                            if g == 0:
                                ge(act, pv_ready, i - 1)
                            bank, at0 = m.ps[4 + (NG * at[1] + g) % 2], P * group[0]
                            full = sum(CHUNKS[ch].width == P for ch in group)
                            ins = act.copy(prT[:, at[1] % 2, at0:at0 + full * P], bank[:, 0:full * P])
                            if full < len(group):
                                width = CHUNKS[group[-1]].width
                                ins = act.copy(prT[0:width, at[1] % 2, at0 + full * P:at0 + full * P + P],
                                               bank[0:width, full * P:full * P + P])
                            ins.then_inc(t_done, 1)

                copy(range(LATE))
                if (at := due(b, t, 0)):
                    i = at[0] * TB + at[1]
                    act.wait_ge(sub_done, i + 1)
                    act.activation(pr[:, t % 2, :], pr[:, t % 2, :], ACT.Exp, scale=scale).then_inc(exp_done, 1)
                copy([LATE])

            rotate(act, body, 1)


VW_SLOTS = 2
VH = H * D // 2 // BANK
EPS2 = 1e-6
KH = 64
PAIRS = H // 2


class Context64:

    def __init__(self, nc, a, sem, sb):
        self.a = a
        self.G = sb("a2_G", [P, B, H, J])
        self.vwf = sb("a2_vwf", [P, B, NC, D])
        self.names = ("w_in", "k_ready", "k_done", "g_ready", "g_done", "mm_ready", "mm_done", "vw_ready", "vw_done", "vw_back", "zeroed")
        self.s = {n: sem("a2_" + n) for n in self.names}
        self.vw_out = [sem(f"a2_vw_out{n}") for n in range(VW_SLOTS)]

    def take(self, sb):
        self.wk, self.wqT, self.wvT = (sb("a2_" + n, [P, PAIRS, P]) for n in ("wk", "wqT", "wvT"))
        self.w0 = sb("a2_w0", [P, H, D])
        self.k2T = sb("a2_k2T", [P, 4, B * J])
        self.M = sb("a2_M", [P, H * D])
        self.vw = sb("a2_vw", [J, VW_SLOTS, H * D // 2])

    def loads(self, sp):
        for t, n in ((self.wk, "wk"), (self.wqT, "wqT"), (self.wvT, "wvT"), (self.w0, "w0")):
            sp.dma_start(t[:, :, :], self.a["a2_" + n]).then_inc(self.s["w_in"], 16)

    def pool_zeros(self, pool):
        pool.memset(self.k2T[:, :, :], 0.0).then_inc(self.s["zeroed"], 1)
        pool.wait_ge(self.s["zeroed"], 1)

    def sp_work(self, sp):
        s, vw_in = self.s, self.a["vw"]
        for n in range(2 * B):
            b, half = n // 2, n % 2
            sp.wait_ge(s["vw_done"], VH * (n + 1))
            sp.dma_start(vw_in[b, half * H // 2:(half + 1) * H // 2, :, :].rearrange("h j d -> j h d"),
                         self.vw[:, n % VW_SLOTS, :].rearrange("j (h d) -> j h d", d=D)).then_inc(self.vw_out[n % VW_SLOTS], 16)
        for q in self.vw_out:
            sp.wait_ge(q, 16 * 2 * B // VW_SLOTS)
        rows, full = vw_in.rearrange("b h j d -> b (h j) d"), HJ // P
        for b in range(B):
            sp.dma_start(self.vwf[:, b, 0:full, :], rows[b, 0:full * P, :].rearrange("(c p) d -> p c d", p=P)).then_inc(s["vw_back"], 16)
            sp.dma_start(self.vwf[0:HJ - full * P, b, full, :], rows[b, full * P:, :]).then_inc(s["vw_back"], 16)
        sp.wait_ge(s["vw_back"], 16 * 2 * B)

    def pe_work(self, pe, m):
        s = self.s

        def g_pair(c):
            pe.wait_ge(s["k_done"], 2 * (c + 1))
            for r in range(2):
                ge(pe, s["g_done"], 2 * c + r - 1)
                pe.matmul(m.ps[6 + r][:, 0:B * J], self.wqT[:, c, :], self.k2T[:, (2 * c + r) % 4, :], start=True, stop=True).then_inc(s["g_ready"], 1)

        pe.wait_ge(s["w_in"], 64)
        for c in range(PAIRS):
            ge(pe, s["k_done"], 2 * (c - 1))
            pe.matmul(m.ps[4 + c % 2][:, 0:B * J], self.wk[:, c, :], m.ctxT[:, :, :], start=True, stop=True).then_inc(s["k_ready"], 1)
            if c >= 1:
                g_pair(c - 1)
        g_pair(PAIRS - 1)
        for h in range(H):
            if h == 0:
                pe.wait_ge(s["g_done"], H)
            ge(pe, s["mm_done"], h - 3)
            pe.matmul(m.ps[4 + h % 4][:, 0:D], self.wvT[:, h // 2, :], self.w0[:, h, :], start=True, stop=True).then_inc(s["mm_ready"], 1)
        pe.wait_ge(s["mm_done"], H)
        for n in range(B * 2 * VH):
            b, q = n // (2 * VH), n % (2 * VH)
            ge(pe, s["vw_done"], n - 3)
            pe.matmul(m.ps[4 + n % 4][0:J, :], m.ctxT[:, b, :], self.M[:, q * BANK:(q + 1) * BANK], start=True, stop=True).then_inc(s["vw_ready"], 1)

    def act_keys(self, act, m):
        s = self.s
        for c in range(PAIRS + 1):
            if c < PAIRS:
                act.wait_ge(s["k_ready"], c + 1)
                for r in range(2):
                    rows = slice(KH * r, KH * r + KH)
                    act.activation(self.k2T[rows, (2 * c + r) % 4, :], m.ps[4 + c % 2][rows, 0:B * J], ACT.Copy, scale=KH ** -0.5).then_inc(s["k_done"], 1)
            if c:
                for h in (2 * c - 2, 2 * c - 1):
                    act.wait_ge(s["g_ready"], h + 1)
                    act.copy(self.G[:, :, h, :], m.ps[6 + h % 2][:, 0:B * J].rearrange("p (b j) -> p b j", b=B)).then_inc(s["g_done"], 1)

    def act_values(self, act, m):
        s = self.s
        for h in range(H):
            act.wait_ge(s["mm_ready"], h + 1)
            act.copy(self.M[:, h * D:(h + 1) * D], m.ps[4 + h % 4][:, 0:D]).then_inc(s["mm_done"], 1)
        act.wait_ge(s["mm_done"], H)
        for n in range(B * 2 * VH):
            half, q = n // VH, n % VH
            act.wait_ge(s["vw_ready"], n + 1)
            if q == 0:
                ge(act, self.vw_out[half % VW_SLOTS], 16 * (half // VW_SLOTS))
            act.copy(self.vw[:, half % VW_SLOTS, q * BANK:(q + 1) * BANK], m.ps[4 + n % 4][0:J, :]).then_inc(s["vw_done"], 1)


def attention64(nc, m, a, sem, sb):
    G, vwf = m.context64.G, m.context64.vwf
    gamma, beta = sb("a2_gamma", [P, D]), sb("a2_beta", [P, D])
    maski = sb("a2_maski", [P, NT, J], I32)
    m01 = sb("a2_m01", [P, NT, J])
    y = sb("a2_y", [P, NT, D])
    (mask_done, q_done, s_ready, mask_applied, max_done, sub_done, exp_done, sum_done, rden_done, norm_done, t_ready,
     t_done, pv_ready, y_done, pool_pass, var_done, std_done) = (
        sem("a2_" + n) for n in (
        "mask_done", "q_done", "s_ready", "mask_applied", "max_done", "sub_done", "exp_done", "sum_done",
        "rden_done", "norm_done", "t_ready", "t_done", "pv_ready", "y_done", "pool_pass", "var_done", "std_done"))

    def loads(sp):
        m.fetch(sp.dma_start(maski[:, :, :], a["mask2"].rearrange("b (i p) j -> p (b i) j", p=P)))
        m.fetch(sp.dma_start(gamma[:, :], a["a2_gamma"]))
        m.fetch(sp.dma_start(beta[:, :], a["a2_beta"]))

    def pool_work(pool):
        m.fetch.wait(pool)
        pool.tensor_scalar(m01[:, :, :], maski[:, :, :], 0.0, -1.0, ALU.is_equal, ALU.mult).then_inc(mask_done, 1)
        pool.wait_ge(mask_done, 1)
        pool.tensor_scalar(m01[:, :, :], m01[:, :, :], 1.0, None, ALU.add).then_inc(mask_done, 1)
        pool.wait_ge(mask_done, 2)

    yield loads, nothing, nothing, pool_work

    qT = sb("a2_qT", [P, S])
    SLOTS = 4
    pr = sb("a2_pr", [P, SLOTS, HJ])
    prT = sb("a2_prT", [P, 2, NC * P])
    mx, sm, rden = (sb("a2_" + n, [P, SLOTS, H]) for n in ("mx", "sm", "rden"))
    scores = [m.ps[i][:, 0:QJ] for i in range(4)]
    PV = m.ps[6]
    hj = lambda ap: ap.rearrange("p (h j) -> p h j", h=H)
    wide = lambda ap: ap.unsqueeze(2).broadcast_to([P, H, J])

    with nc.Block() as block:
        @block.gpsimd
        def _(pool):
            def body(b, t):
                if (at := due(b, t, 2)):
                    i = at[0] * TB + at[1]
                    pool.wait_ge(rden_done, i + 1)
                    p = hj(pr[:, at[1], :])
                    pool.tensor_tensor(p, p, wide(rden[:, at[1], :]), ALU.mult).then_inc(norm_done, 1)
                if (at := due(b, t, 0)):
                    turn_queries(m, pool, b, t, qT, s_ready, q_done, pool_pass)
                    i = at[0] * TB + at[1]
                    p = hj(pr[:, at[1], :])
                    pool.wait_ge(max_done, i + 1)
                    pool.tensor_tensor(p, p, wide(mx[:, at[1], :]), ALU.subtract).then_inc(sub_done, 1)

            pool.tensor_copy(qT[:, 0:P], m.xnT[:, 0:P]).then_inc(q_done, 1)
            rotate(pool, body, 2)

        @block.tensor
        def _(pe):
            def turn(at, groups):
                i = at[0] * TB + at[1]
                if 0 in groups:
                    pe.wait_ge(norm_done, i + 1)
                for g in groups:
                    ge(pe, t_done, NG * i + g - 1)
                    for n, ch in enumerate(GROUPS[g]):
                        c = CHUNKS[ch]
                        ins = pe.transpose(m.ps[4 + (NG * at[1] + g) % 2][0:c.width, n * P:(n + 1) * P],
                                           pr[:, at[1], c.at:c.at + c.width], m.ident[:, :])
                    ins.then_inc(t_ready, 1)

            def body(b, t):
                if (at := due(b, t, 3)):
                    turn(at, [LATE])
                if (at := due(b, t, 0)):
                    i = at[0] * TB + at[1]
                    pe.wait_ge(q_done, i + 1)
                    ge(pe, mask_applied, i)
                    for r in range(4):
                        ins = pe.matmul(scores[r], qT[:, t * P:(t + 1) * P],
                                        G[:, bass.ds(b, 1), r * QH:(r + 1) * QH, :].rearrange("p b h j -> p (b h j)"), start=True, stop=True)
                    ins.then_inc(s_ready, 1)
                if (at := due(b, t, 3)):
                    i = at[0] * TB + at[1]
                    pe.wait_ge(t_done, NG * (i + 1))
                    ge(pe, y_done, i)
                    for n, c in enumerate(CHUNKS):
                        ins = pe.matmul(PV[:, 0:D], prT[0:c.width, at[1] % 2, n * P:(n + 1) * P],
                                        vwf[0:c.width, bass.ds(at[0], 1), n, :].rearrange("p b e -> p (b e)"),
                                        start=(n == 0), stop=(n == NC - 1))
                    ins.then_inc(pv_ready, 1)
                if (at := due(b, t, 2)):
                    turn(at, range(LATE))

            rotate(pe, body, 3)

        @block.vector
        def _(dve):
            def body(b, t):
                if (at := due(b, t, 0)):
                    i = at[0] * TB + at[1]
                    p = hj(pr[:, t, :])
                    dve.wait_ge(s_ready, i + 1)
                    ge(dve, t_ready, NG * (i - 3))
                    for r in range(4):
                        ins = dve.scalar_tensor_tensor(p[:, r * QH:(r + 1) * QH, :], scores[r].rearrange("p (h j) -> p h j", h=QH),
                                                       -EPS2, m01[:, bass.ds(i, 1), :].broadcast_to([P, QH, J]), ALU.add, ALU.mult)
                    ins.then_inc(mask_applied, 1)
                    dve.wait_ge(mask_applied, i + 1)
                    dve.tensor_reduce(mx[:, t, :], p, AX.X, ALU.max).then_inc(max_done, 1)
                if (at := due(b, t, 1)):
                    i = at[0] * TB + at[1]
                    dve.wait_ge(exp_done, i + 1)
                    dve.tensor_reduce(sm[:, at[1], :], hj(pr[:, at[1], :]), AX.X, ALU.add).then_inc(sum_done, 1)
                    dve.wait_ge(sum_done, i + 1)
                    dve.reciprocal(rden[:, at[1], :], sm[:, at[1], :]).then_inc(rden_done, 1)
                if (at := due(b, t, 3)):
                    i = at[0] * TB + at[1]
                    dve.wait_ge(pv_ready, i + 1)
                    yi, xi = (z[:, bass.ds(i, 1), :].rearrange("p i d -> p (i d)") for z in (y, m.xn))
                    dve.tensor_tensor(yi, xi, PV[:, 0:D], ALU.add).then_inc(y_done, 1)

            rotate(dve, body, 3)

        @block.scalar
        def _(act):
            def copy(at, groups):
                i = at[0] * TB + at[1]
                for g in groups:
                    group = GROUPS[g]
                    act.wait_ge(t_ready, NG * i + g + 1)
                    if g == 0:
                        ge(act, pv_ready, i - 1)
                    bank, at0 = m.ps[4 + (NG * at[1] + g) % 2], P * group[0]
                    full = sum(CHUNKS[ch].width == P for ch in group)
                    ins = act.copy(prT[:, at[1] % 2, at0:at0 + full * P], bank[:, 0:full * P])
                    if full < len(group):
                        width = CHUNKS[group[-1]].width
                        ins = act.copy(prT[0:width, at[1] % 2, at0 + full * P:at0 + full * P + P],
                                       bank[0:width, full * P:full * P + P])
                    ins.then_inc(t_done, 1)

            def body(b, t):
                if (at := due(b, t, 3)):
                    copy(at, [LATE])
                if (at := due(b, t, 1)):
                    i = at[0] * TB + at[1]
                    act.wait_ge(sub_done, i + 1)
                    act.activation(pr[:, at[1], :], pr[:, at[1], :], ACT.Exp).then_inc(exp_done, 1)
                if (at := due(b, t, 2)):
                    copy(at, range(LATE))

            rotate(act, body, 3)

    with nc.Block() as block:
        @block.vector
        def _(dve):
            for i in range(NT):
                m.dve(dve.bn_stats(m.stats[:, i, :], y[:, i, :]))
            m.dve.wait(dve)
            for i in range(NT):
                m.dve(dve.bn_aggr(m.mv[:, i, :], m.stats[:, i, :]))
            m.dve.wait(dve)
            dve.tensor_scalar(m.var[:, :], m.mv[:, :, 1], D / (D - 1.0), None, ALU.mult).then_inc(var_done, 1)
            dve.wait_ge(std_done, 1)
            m.dve(dve.tensor_scalar(m.std[:, :], m.std[:, :], EPS2, None, ALU.add))
            m.dve.wait(dve)
            m.dve(dve.reciprocal(m.rstd[:, :], m.std[:, :]))
            m.dve.wait(dve)
            m.dve(dve.scalar_tensor_tensor(m.nmr[:, :], m.mv[:, :, 0], -1.0, m.rstd[:, :], ALU.mult, ALU.mult))
            m.dve.wait(dve)
            for i in range(NT):
                m.dve(dve.tensor_scalar(y[:, i, :], y[:, i, :], m.rstd[:, i:i + 1], m.nmr[:, i:i + 1], ALU.mult, ALU.add))
            m.dve.wait(dve)
            rows = lambda v: v[:, :].unsqueeze(1).broadcast_to([P, NT, D])
            m.dve(dve.tensor_tensor(y[:, :, :], y[:, :, :], rows(gamma), ALU.mult))
            m.dve(dve.tensor_tensor(m.x[:, :, :], m.x[:, :, :], rows(beta), ALU.add))
            m.dve.wait(dve)
            m.dve(dve.tensor_tensor(m.x[:, :, :], m.x[:, :, :], y[:, :, :], ALU.add))
            m.dve.wait(dve)

        @block.scalar
        def _(act):
            act.wait_ge(var_done, 1)
            act.activation(m.std[:, :], m.var[:, :], ACT.Sqrt).then_inc(std_done, 1)


HID = 384
HC = HID // P
QMAX = 2.0 ** 15 - 1
TINY = 1e-12


def ffn1(nc, m, a, sem, sb):
    w = sb("f1_w", [P, 3 * HC, P])
    wT = sb("f1_wT", [P, 3 * HC, P])
    NBLK = 3 * HC * 4
    ws, winv = sb("f1_ws", [P, NBLK]), sb("f1_winv", [P, NBLK])
    up, gate, sig = (sb("f1_" + n, [P, HC, N]) for n in ("up", "gate", "sig"))
    (w_in, w_done, wT_ready, wT_done, most_ready, most_done, xq_done, mm_ready, mm_done, scaled, rounded, gate_done,
     sig_ready, sig_rounded, up_rounded, up_done, o_done, down_ready) = (
        sem("f1_" + n) for n in (
        "w_in", "w_done", "wT_ready", "wT_done", "most_ready", "most_done", "xq_done", "mm_ready", "mm_done",
        "scaled", "rounded", "gate_done", "sig_ready", "sig_rounded", "up_rounded", "up_done", "o_done", "down_ready"))
    XQ, UP, GATE, G2, OUT = range(5)
    part = sb("f1_part", [P, 5, 12])
    most, over, sc, inv = (sb("f1_" + n, [P, 5]) for n in ("most", "over", "sc", "inv"))
    scug = sb("f1_scug", [P, 1])
    col = lambda t, q: t[:, q:q + 1]
    m.context64.take(sb)

    def loads(sp):
        for n, part_name in enumerate(("f1_up", "f1_gate", "f1_down")):
            sp.dma_start(w[:, n * HC:(n + 1) * HC, :], a[part_name]).then_inc(w_in, 16)
        m.context64.loads(sp)

    yield loads, nothing, nothing, m.context64.pool_zeros

    with nc.Block() as block:
        @block.sync
        def _(sp):
            m.context64.sp_work(sp)

        @block.gpsimd
        def _(pool):
            for n, (q, count) in enumerate(((XQ, 1), (UP, 2), (G2, 1), (OUT, 1))):
                pool.wait_ge(most_ready, n + 1)
                pool.partition_all_reduce(over[:, q:q + count], most[:, q:q + count], P, RED.max).then_inc(most_done, 1)
                if n == 1:
                    pool.wait_ge(scaled, 1)
                    for c in range(HC):
                        pool.tensor_scalar(up[:, c, :], up[:, c, :], col(inv, UP), MAGIC, ALU.mult, ALU.add).then_inc(up_rounded, 1)
                    for c in range(HC):
                        pool.wait_ge(up_rounded, c + 1)
                        pool.tensor_scalar(up[:, c, :], up[:, c, :], 1.0, -MAGIC, ALU.mult, ALU.add).then_inc(up_rounded, 1)
                        pool.wait_ge(up_rounded, HC + c + 1)
                        pool.tensor_scalar(up[:, c, :], up[:, c, :], col(sc, UP), 0.0, ALU.mult, ALU.add).then_inc(up_done, 1)

        @block.tensor
        def _(pe):
            pe.wait_ge(w_done, 1)
            for n in range(3 * HC):
                ins = pe.transpose(m.ps[n // 4][:, n % 4 * P:n % 4 * P + P], w[:, n, :], m.ident[:, :])
            ins.then_inc(wT_ready, 1)
            pe.wait_ge(xq_done, 1)
            pe.wait_ge(wT_done, 3)
            for n in range(8 * HC):
                q, mat = n // (2 * HC), n % (2 * HC)
                ge(pe, mm_done, n - 7)
                pe.matmul(m.ps[n % 8][:, :], wT[:, mat, :], m.xnT[:, q * BANK:(q + 1) * BANK], start=True, stop=True).then_inc(mm_ready, 1)
            pe.wait_ge(mm_done, 8 * HC)
            m.context64.pe_work(pe, m)
            for i in range(NT):
                if i % 4 == 0:
                    pe.wait_ge(o_done, i // 4 + 1)
                for c in range(HC):
                    ins = pe.matmul(m.ps[i // 4][:, i % 4 * P:i % 4 * P + P], sig[:, c, i * P:(i + 1) * P], wT[:, 2 * HC + c, :],
                                    start=(c == 0), stop=(c == HC - 1))
                if i % 4 == 3:
                    ins.then_inc(down_ready, 1)

        @block.scalar
        def _(act):
            for n in range(8 * HC):
                q, mat = n // (2 * HC), n % (2 * HC)
                act.wait_ge(mm_ready, n + 1)
                act.copy((up, gate)[mat // HC][:, mat % HC, q * BANK:(q + 1) * BANK], m.ps[n % 8][:, :]).then_inc(mm_done, 1)
            act.wait_ge(scaled, 1)
            for c in range(HC):
                act.activation(gate[:, c, :], gate[:, c, :], ACT.Copy, scale=col(inv, GATE), bias=MAGIC).then_inc(rounded, 1)
            for c in range(HC):
                act.wait_ge(gate_done, c + 1)
                act.activation(sig[:, c, :], gate[:, c, :], ACT.Sigmoid).then_inc(sig_ready, 1)
                act.wait_ge(sig_ready, c + 1)
                act.activation(sig[:, c, :], sig[:, c, :], ACT.Copy, scale=65536.0, bias=MAGIC).then_inc(sig_rounded, 1)
            m.context64.act_keys(act, m)
            act.wait_ge(scaled, 2)
            for c in range(HC):
                act.activation(gate[:, c, :], gate[:, c, :], ACT.Copy, scale=col(inv, G2), bias=MAGIC).then_inc(rounded, 1)
            m.context64.act_values(act, m)
            act.wait_ge(scaled, 3)
            for q in range(4):
                o = sig[:, :, q * BANK:(q + 1) * BANK]
                act.activation(o, o, ACT.Copy, scale=col(inv, OUT), bias=MAGIC).then_inc(rounded, 1)

        @block.vector
        def _(dve):
            def step(ins):
                m.dve(ins)
                m.dve.wait(dve)

            def scale(q, n, count=1):
                at = slice(q, q + count)
                dve.wait_ge(most_done, n)
                step(dve.tensor_scalar(sc[:, at], over[:, at], 1.0 / QMAX, TINY, ALU.mult, ALU.max))
                step(dve.reciprocal(inv[:, at], sc[:, at]))

            dve.wait_ge(w_in, 48)
            wb = w[:, :, :].rearrange("p n (k e) -> p (n k) e", e=32)
            wide = lambda t: t[:, :].unsqueeze(2).broadcast_to([P, NBLK, 32])
            step(dve.tensor_reduce(ws[:, :], wb, AX.X, ALU.max, apply_absolute_value=True))
            step(dve.tensor_scalar(ws[:, :], ws[:, :], 1.0 / 7, TINY, ALU.mult, ALU.max))
            step(dve.reciprocal(winv[:, :], ws[:, :]))
            step(dve.tensor_tensor(wb, wb, wide(winv), ALU.mult))
            step(dve.tensor_scalar(wb, wb, MAGIC, MAGIC, ALU.add, ALU.subtract))
            dve.tensor_tensor(wb, wb, wide(ws), ALU.mult).then_inc(w_done, 1)
            dve.tensor_reduce(col(most, XQ), m.xnT[:, 0:N], AX.X, ALU.max, apply_absolute_value=True).then_inc(most_ready, 1)
            dve.wait_ge(wT_ready, 1)
            for n in range(0, 3 * HC, 4):
                k = min(4, 3 * HC - n)
                dve.tensor_copy(wT[:, n:n + k, :], m.ps[n // 4][:, 0:k * P].rearrange("p (n e) -> p n e", n=k)).then_inc(wT_done, 1)
            scale(XQ, 1)
            step(dve.tensor_scalar(m.xnT[:, 0:N], m.xnT[:, 0:N], col(inv, XQ), MAGIC, ALU.mult, ALU.add))
            dve.tensor_scalar(m.xnT[:, 0:N], m.xnT[:, 0:N], MAGIC, col(sc, XQ), ALU.subtract, ALU.mult).then_inc(xq_done, 1)
            for n in range(8 * HC):
                q, mat = n // (2 * HC), n % (2 * HC)
                dve.wait_ge(mm_done, n + 1)
                m.dve(dve.tensor_reduce(part[:, UP + mat // HC, q * HC + mat % HC:q * HC + mat % HC + 1],
                                        (up, gate)[mat // HC][:, mat % HC, q * BANK:(q + 1) * BANK], AX.X, ALU.max,
                                        apply_absolute_value=True))
            m.dve.wait(dve)
            dve.tensor_reduce(most[:, UP:UP + 2], part[:, UP:UP + 2, :], AX.X, ALU.max).then_inc(most_ready, 1)
            scale(UP, 2, 2)
            dve.sem_inc(scaled, 1)
            for c in range(HC):
                dve.wait_ge(rounded, c + 1)
                dve.tensor_scalar(gate[:, c, :], gate[:, c, :], MAGIC, col(sc, GATE), ALU.subtract, ALU.mult).then_inc(gate_done, 1)
            for c in range(HC):
                dve.wait_ge(sig_rounded, c + 1)
                step(dve.tensor_scalar(sig[:, c, :], sig[:, c, :], MAGIC, 65535.0, ALU.subtract, ALU.min))
                step(dve.scalar_tensor_tensor(gate[:, c, :], sig[:, c, :], 1 / 65536.0, gate[:, c, :], ALU.mult, ALU.mult))
                step(dve.tensor_reduce(part[:, G2, c:c + 1], gate[:, c, :], AX.X, ALU.max, apply_absolute_value=True))
            dve.tensor_reduce(col(most, G2), part[:, G2, 0:HC], AX.X, ALU.max).then_inc(most_ready, 1)
            scale(G2, 3)
            dve.sem_inc(scaled, 1)
            for c in range(HC):
                dve.wait_ge(rounded, HC + c + 1)
                step(dve.tensor_scalar(gate[:, c, :], gate[:, c, :], MAGIC, col(sc, G2), ALU.subtract, ALU.mult))
                dve.wait_ge(up_done, c + 1)
                step(dve.tensor_tensor(sig[:, c, :], gate[:, c, :], up[:, c, :], ALU.mult))
                step(dve.tensor_reduce(part[:, OUT, c:c + 1], sig[:, c, :], AX.X, ALU.max, apply_absolute_value=True))
            dve.tensor_reduce(col(most, OUT), part[:, OUT, 0:HC], AX.X, ALU.max).then_inc(most_ready, 1)
            scale(OUT, 4)
            dve.sem_inc(scaled, 1)
            for q in range(4):
                o = sig[:, :, q * BANK:(q + 1) * BANK]
                dve.wait_ge(rounded, 2 * HC + q + 1)
                dve.tensor_scalar(o, o, MAGIC, col(sc, OUT), ALU.subtract, ALU.mult).then_inc(o_done, 1)
            for q in range(4):
                dve.wait_ge(down_ready, q + 1)
                xq = m.x[:, 4 * q:4 * q + 4, :]
                m.dve(dve.tensor_tensor(xq, xq, m.ps[q][:, :].rearrange("p (t d) -> p t d", t=4), ALU.add))
            m.dve.wait(dve)


def build(nc, a, upto=8):
    with ExitStack() as ctx:
        def sem(name):
            return ctx.enter_context(nc.semaphore(name))

        def sb(name, shape, dt=F32):
            return ctx.enter_context(nc.sbuf_tensor(name, shape, dt))

        m = Machine()
        m.all_banks = ctx.enter_context(nc.psum_tensor("banks", [P, 8, BANK], F32))
        m.ps = [m.all_banks[:, i, :] for i in range(8)]
        m.x, m.xn = sb("x", [P, NT, D]), sb("xn", [P, NT, D])
        m.xnT = sb("xnT", [P, N + P])
        m.packs = {n: sb(n, [P, sum(width for _, width in parts)]) for n, parts in PACKS.items()}
        m.narrow = sb("narrow_b", [P, sum(width for _, width in PACKS["narrow"])], BF16)
        m.small = {}
        for pack, parts in PACKS.items():
            at = 0
            for n, width in parts:
                m.small[n] = (m.narrow if pack == "narrow" else m.packs[pack])[:, at:at + width]
                at += width
        m.ctxT = m.small["ctxT"].rearrange("p (b j) -> p b j", b=B)
        m.ctxT3 = m.small["ctxT3"].rearrange("p (b j) -> p b j", b=B)
        m.ident, m.w0T, m.diag0, m.tri, m.onesb, m.iota8, m.iota128, m.restart, m.one8 = (
            m.small[n] for n in ("ident", "w0T", "diag0", "tri", "onesb", "iota8", "iota128", "restart", "one8"))
        m.zero = sb("zero", [P, D])
        m.stats, m.mv = sb("stats", [P, NT, 6]), sb("mv", [P, NT, 2])
        m.var, m.std, m.rstd, m.nmr = (sb(n, [P, NT]) for n in ("var", "std", "rstd", "nmr"))
        m.dve = Chain(sem("dve_chain"))
        m.ln_var, m.ln_std, m.ln_xn, m.ln_turned, m.ln_copied = (sem("ln_" + n) for n in ("var", "std", "xn", "turned", "copied"))
        m.x_in, m.early_in, stored = [sem(f"x_in{b}") for b in range(B)], sem("early_in"), sem("stored")
        m.fetch = Fetch(sem("fetched"))
        m.context64 = Context64(nc, a, sem, sb)

        used = []

        def stage(number, f, **kw):
            own = []

            def own_sem(name):
                own.append(nc.alloc_semaphore(name=name))
                return own[-1]

            with ExitStack() as inner:
                steps = f(nc, m, a, own_sem, lambda name, shape, dt=F32: inner.enter_context(nc.sbuf_tensor(name, shape, dt)), **kw)
                layer_norm(nc, m, number, *next(steps))
                if used:
                    nc.clear_and_free_semaphores(used)
                for _ in steps:
                    pass
            return own

        for number, (f, kw) in enumerate(STAGES[:upto]):
            used = stage(number, f, **kw)

        with nc.Block() as block:
            @block.sync
            def _(sp):
                sp.dma_start(a["out"].rearrange("b (i p) d -> p (b i) d", p=P), m.x[:, :, :]).then_inc(stored, 16)
                sp.wait_ge(stored, 16)


GMAX = 40
PACKS = dict(
    early=[("ident", P), ("w0T", P), ("diag0", 1), ("ctxT", B * J)],
    later=[("ctxT3", 3 * B * J), ("m0_router", E), ("m0_rbias", E), ("m2_router", E), ("m3_router", E), ("wqT", P), ("wkT", P),
           ("wvT", P), ("woT", P), ("bq", 1), ("bk", 1), ("bv", NC * CH * HD), ("bo", P), ("woutT", P), ("bout", P),
           ("vmask", NC * CH), ("qmask", H), ("iota8", E), ("iota128", NT), ("iotag", GMAX), ("iotar", P), ("tile1", 2 * NT),
           ("part", 1), ("restart", E * NT), ("one8", E)],
    narrow=[("identb", P), ("tri", P), ("onesb", P)],
)
STAGES = [
    (attention0, {}),
    (moe, dict(name="m0", blocks=24, topk=1, cap=0, biased=True, gated=False, act_fn=None, x_stage=False)),
    (attention8, dict(name="a1", scale=HD ** -0.5, projected=True, masked=False)),
    (ffn1, {}),
    (attention64, {}),
    (moe, dict(name="m2", blocks=GMAX, topk=2, cap=int(1.25 * N * 2 / E) + 1, biased=False, gated=False, act_fn=ACT.Silu, x_stage=True)),
    (attention8, dict(name="a3", scale=HD ** -0.5, projected=False, masked=True)),
    (moe, dict(name="m3", blocks=GMAX, topk=2, cap=0, biased=False, gated=True, act_fn=ACT.Silu, x_stage=False)),
]


def arrays(v):
    c = np.ascontiguousarray
    ctx = np.asarray(v["ctx_1024"])
    rows = lambda w, n: c(np.broadcast_to(w, (n,) + w.shape))
    chunked = lambda w: c(w.reshape(w.shape[0], FC, P, D).transpose(0, 2, 1, 3).reshape(w.shape[0], P, FC * D))
    pairs = lambda w: w.reshape(PAIRS, P, D).transpose(1, 0, 2)

    def apart(w):
        z = np.zeros((PAIRS, 2, KH, 2, D), w.dtype)
        for r in range(2):
            z[:, r, :, r, :] = w.reshape(PAIRS, 2, KH, D)[:, r]
        return z.reshape(PAIRS, P, 2, D).transpose(1, 0, 2, 3).reshape(P, H, D)

    def vmask():
        k = np.zeros((P, NC, CH), np.float32)
        for n, ch in enumerate(CHUNKS):
            r = np.arange(ch.width)
            k[r, n, (ch.at + r) // J - ch.h0] = 1
        return k.reshape(P, NC * CH)

    o = dict(
        x=v["x"], ctx=ctx, ctxT=ctx.transpose(2, 0, 1), ctxT3=np.tile(ctx.transpose(2, 0, 1), (1, 1, 3)), mask0=v["mask_BxS2_if1"],
        w0T=c(v["L0_xattn_W"].T), diag0=c(v["L0_xattn_diagonal"].reshape(P, 1)),
        m0_router=v["L0_ffn_w_gate"], m0_rbias=rows(v["L0_ffn_b_gate"], P),
        m0_w1=v["L0_ffn_W1"], m0_w2=chunked(v["L0_ffn_W2"]),
        m0_b1=c(np.broadcast_to(v["L0_ffn_b1"][:, None, :], (E, P, F))),
        m0_b2=c(np.broadcast_to(v["L0_ffn_b2"][:, None, :], (E, P, D))),
        m2_router=c(v["L2_ffn_router_w"].T), m3_router=c(v["L3_ffn_gate_w"].T),
        wqT=c(v["L1_xattn_wq"].T), wkT=c(v["L1_xattn_wk"].T), wvT=c(v["L1_xattn_wv"].T), woT=c(v["L1_xattn_wo"].T),
        bq=v["L1_xattn_bq"][:, None], bk=v["L1_xattn_bk"][:, None], bv=rows(np.concatenate([v["L1_xattn_bv"][c.h0 * HD:(c.h0 + CH) * HD] for c in CHUNKS]), P), bo=rows(v["L1_xattn_bo"], P),
        woutT=c(v["L3_xattn_W_out"].T), bout=rows(v["L3_xattn_b_out"], P), mask3=v["mask_Bx1xSxS2_ik1"][:, 0],
        mask2=v["mask_BxSxS2_ik1"], a2_wk=v["L2_xattn_w_k"].reshape(D, PAIRS, P),
        a2_wqT=pairs(v["L2_xattn_w_q"].T), a2_wvT=pairs(v["L2_xattn_w_v"].T), a2_w0=apart(v["L2_xattn_w_0"]),
        a2_gamma=rows(v["L2_xattn_gamma"], P), a2_beta=rows(v["L2_xattn_beta"], P),
        f1_up=v["L1_ffn_w_up"].reshape(HC, P, D).transpose(1, 0, 2), f1_gate=v["L1_ffn_w_gate"].reshape(HC, P, D).transpose(1, 0, 2),
        f1_down=v["L1_ffn_w_down"].reshape(P, HC, P),
        m2_w1=v["L2_ffn_w1"], m2_w2=chunked(v["L2_ffn_w2"]),
        m3_w1=c(v["L3_ffn_w1"].transpose(0, 2, 1)), m3_w3=c(v["L3_ffn_w3"].transpose(0, 2, 1)),
        m3_w2=chunked(v["L3_ffn_w2"].transpose(0, 2, 1)),
        vmask=vmask(), qmask=(np.arange(P)[:, None] // HD == np.arange(H)).astype(np.float32),
        identb=np.eye(P, dtype=np.float32),
        ident=np.eye(P, dtype=np.float32), tri=np.triu(np.ones((P, P), np.float32), 1), onesb=np.ones((P, P), np.float32),
        iota8=rows(np.arange(E, dtype=np.float32), P), iota128=rows(np.arange(NT, dtype=np.float32) * P, P),
        iotag=rows(np.arange(GMAX, dtype=np.float32), P), iotar=rows(np.arange(P, dtype=np.float32), P),
        tile1=rows(np.arange(1, 2 * NT + 1, dtype=np.float32), P), part=np.arange(P, dtype=np.float32)[:, None], restart=rows((np.arange(E * NT) % NT != 0).astype(np.float32), P),
        one8=np.ones((P, E), np.float32),
    )
    for pack, parts in PACKS.items():
        o[pack] = np.concatenate([np.asarray(o.pop(n)).reshape(P, width) for n, width in parts], axis=1)
    return {k: c(np.asarray(x)) for k, x in o.items()}


def kernel(**inputs):
    import concourse.bacc as bacc
    from concourse.bass_utils import run_bass_kernel_spmd

    nc = bacc.Bacc("TRN2", target_bir_lowering=False, num_devices=1)
    given = arrays({k: np.asarray(v) for k, v in inputs.items()})
    a = {k: nc.dram_tensor("in_" + k, v.shape, mybir.dt.from_np(v.dtype), kind="ExternalInput").ap() for k, v in given.items()}
    a["out"] = nc.dram_tensor("out", (B, S, D), F32, kind="ExternalOutput").ap()
    a["pairs_in"] = nc.dram_tensor("pairs_in", (2 * N, D), F32, kind="Internal").ap()
    a["vw"] = nc.dram_tensor("value_rows", (B, H, J, D), F32, kind="Internal").ap()
    for name, k in (("m0", 1), ("m2", 2), ("m3", 2)):
        a[name + "_pairs_out"] = nc.dram_tensor(name + "_pairs_out", (k * N, D), F32, kind="Internal").ap()
    build(nc, a, UPTO)
    result = run_bass_kernel_spmd(nc, [{"in_" + k: v for k, v in given.items()}], core_ids=[0])
    return result.results[0]["out"]


UPTO = 8
```

```python
from contextlib import ExitStack

import numpy as np

import concourse.bass as bass
from concourse import mybir

F32 = mybir.dt.float32
BF16 = mybir.dt.bfloat16
I32 = mybir.dt.int32
U32 = mybir.dt.uint32
ALU = mybir.AluOpType
ACT = mybir.ActivationFunctionType
AX = mybir.AxisListType
RED = bass.bass_isa.ReduceOp

P = 128
D = 128
B, S, J = 4, 512, 77
N = B * S
NT = N // P
TB = NT // B
BANK = 512
H = 16
HD = D // H
HJ = H * J
QH = H // 4
QJ = QH * J
E = 8
F = 512
FC = F // P
LN_EPS = 1e-5
MASKED = -1e20
MAGIC = 1.5 * 2.0 ** 23

CH = (P - 2) // J + 2


class Chunk:
    def __init__(self, at):
        self.at, self.width = at, min(P, HJ - at)
        self.row, self.h0 = at % J, min(at // J, H - CH)


CHUNKS = [Chunk(at) for at in range(0, HJ, P)]
NC = len(CHUNKS)
GROUPS = [range(g, min(g + 4, NC)) for g in range(0, NC, 4)]
NG = len(GROUPS)


def keep_warm(pe, m, bank, count):
    for _ in range(count):
        pe.matmul(m.ps[bank][:, :], m.onesb[:, :], m.onesb[:, :].unsqueeze(1).broadcast_to([P, BANK // P, P]), start=True, stop=True)


LN_WARM = 12
TILE_WARM = 6


class Machine:
    pass


def ge(eng, sem, value):
    if not (isinstance(value, int) and value <= 0):
        eng.wait_ge(sem, value)


class Chain:

    def __init__(self, sem):
        self.sem, self.n = sem, 0

    def __call__(self, ins):
        ins.then_inc(self.sem, 1)
        self.n = self.n + 1
        return self.n

    def wait(self, eng):
        ge(eng, self.sem, self.n)


class Fetch:

    def __init__(self, sem):
        self.sem, self.n = sem, 0

    def __call__(self, ins):
        ins.then_inc(self.sem, 16)
        self.n = self.n + 1

    def wait(self, eng):
        eng.wait_ge(self.sem, 16 * self.n)


def nothing(engine):
    pass


DVE_TILES = [i for i in range(NT) if i % 2 == 0 or i % 8 == 7]
ACT_TILES = [i for i in range(NT) if i not in DVE_TILES]


def layer_norm(nc, m, k, loads=nothing, pe_work=nothing, act_work=nothing, pool_work=nothing, pe_batch=None):
    with nc.Block() as block:
        if loads is not nothing:
            @block.sync
            def _(sp):
                loads(sp)

        if pool_work is not nothing:
            @block.gpsimd
            def _(pool):
                pool_work(pool)

        @block.vector
        def _(dve):
            for i in range(NT) if not m.have_stats else ():
                if k == 0 and i % TB == 0:
                    dve.wait_ge(m.x_in[i // TB], 16)
                m.dve(dve.bn_stats(m.stats[:, i, :], m.x[:, i, :]))
            m.have_stats = False
            m.dve.wait(dve)
            for i in range(NT):
                m.dve(dve.bn_aggr(m.mv[:, i, :], m.stats[:, i, :]))
            m.dve.wait(dve)
            dve.tensor_scalar(m.var[:, :], m.mv[:, :, 1], LN_EPS, None, ALU.add).then_inc(m.ln_var, 1)
            dve.wait_ge(m.ln_std, k + 1)
            m.dve(dve.reciprocal(m.rstd[:, :], m.std[:, :]))
            m.dve.wait(dve)
            m.dve(dve.scalar_tensor_tensor(m.nmr[:, :], m.mv[:, :, 0], -1.0, m.rstd[:, :], ALU.mult, ALU.mult))
            m.dve.wait(dve)
            dve.sem_inc(m.ln_scale, 1)
            for i in DVE_TILES:
                dve.tensor_scalar(m.xn[:, i, :], m.x[:, i, :], m.rstd[:, i:i + 1], m.nmr[:, i:i + 1],
                                  ALU.mult, ALU.add).then_inc(m.ln_xn, 1)
            for q in (1, 3):
                dve.wait_ge(m.ln_turned, 4 * k + q + 1)
                dve.tensor_copy(m.xnT[:, q * BANK:(q + 1) * BANK], m.ps[q][:, :]).then_inc(m.ln_copied, 1)

        @block.scalar
        def _(act):
            act.wait_ge(m.ln_var, k + 1)
            act.activation(m.std[:, :], m.var[:, :], ACT.Sqrt).then_inc(m.ln_std, 1)
            act.wait_ge(m.ln_scale, k + 1)
            for i in ACT_TILES:
                act.activation(m.xn[:, i, :], m.x[:, i, :], ACT.Identity, bias=m.nmr[:, i:i + 1],
                               scale=m.rstd[:, i:i + 1]).then_inc(m.ln_xn_act, 1)
            act_work(act)
            for q in (0, 2):
                act.wait_ge(m.ln_turned, 4 * k + q + 1)
                act.copy(m.xnT[:, q * BANK:(q + 1) * BANK], m.ps[q][:, :]).then_inc(m.ln_copied_act, 1)

        @block.tensor
        def _(pe):
            if k == 0:
                pe.wait_ge(m.early_in, 16)
            pe_work(pe)
            if k > 0:
                keep_warm(pe, m, 3, LN_WARM)
            for i in range(NT):
                if i in DVE_TILES:
                    pe.wait_ge(m.ln_xn, len(DVE_TILES) * k + DVE_TILES.index(i) + 1)
                else:
                    pe.wait_ge(m.ln_xn_act, len(ACT_TILES) * k + ACT_TILES.index(i) + 1)
                ins = pe.transpose(m.ps[i // 4][:, i % 4 * P:i % 4 * P + P], m.xn[:, i, :], m.ident[:, :])
                if i % 4 == 3:
                    ins.then_inc(m.ln_turned, 1)
            for b in range(B) if pe_batch else ():
                if b % 2:
                    pe.wait_ge(m.ln_copied, 2 * k + b // 2 + 1)
                else:
                    pe.wait_ge(m.ln_copied_act, 2 * k + b // 2 + 1)
                pe_batch(pe, b)


def first_loads(nc, m, a, sem):
    zeroed = sem("zeroed")

    def loads(sp):
        x = a["x"].rearrange("b (i p) d -> p b i d", p=P)
        for b in range(B):
            sp.dma_start(m.x[:, b * TB:(b + 1) * TB, :], x[:, b, :, :]).then_inc(m.x_in[b], 16)
            if b == 0:
                sp.dma_start(m.packs["early"][:, :], a["early"]).then_inc(m.early_in, 16)
        m.a0_loads(sp)
        m.fetch(sp.dma_start(m.packs["later"][:, :], a["later"]))
        m.fetch(sp.dma_start(m.packs["narrow"][:, :], a["narrow"]))
        sp.wait_ge(zeroed, 1)
        m.fetch(sp.dma_start(a["m2_pairs_out"].rearrange("(q p) d -> p q d", p=P), m.zero[:, :].unsqueeze(1).broadcast_to([P, 2 * NT, D])))

    def pool_work(pool):
        pool.memset(m.zero[:, :], 0.0).then_inc(zeroed, 1)
        pool.memset(m.xnT[:, N:N + P], 0.0).then_inc(zeroed, 1)
        pool.wait_ge(zeroed, 2)

    return loads, pool_work


def attention0(nc, m, a, sem, sb):
    kT = sb("a0_kT", [P, B, J])
    ctxv = sb("a0_ctxv", [J, B, D + 1])
    madd = sb("a0_madd", [1, B * J])
    maski = sb("a0_maski", [1, B * J], I32)
    ones1 = sb("a0_ones1", [1, P])
    qT = sb("a0_qT", [P, N])
    pr = sb("a0_pr", [P, B, TB, J])
    prT = sb("a0_prT", [J, N])
    mx = sb("a0_mx", [P, B, TB])
    rden = sb("a0_rden", [P, NT])
    ctx_loaded, k_ready, k_done, bias_done, q_ready, q_done, s_ready, sub_done, exp_done, t_ready, t_done, o_ready, x_done, narrowed = (
        sem("a0_" + n) for n in ("ctx_loaded", "k_ready", "k_done", "bias_done", "q_ready", "q_done", "s_ready", "sub_done",
                                 "exp_done", "t_ready", "t_done", "o_ready", "x_done", "narrowed"))

    def loads(sp):
        sp.dma_start(ctxv[:, :, 0:D], a["ctx"].rearrange("b j d -> j b d")).then_inc(ctx_loaded, 16)
        sp.dma_start(maski[:, :], a["mask0"].rearrange("b j -> (b j)").unsqueeze(0)).then_inc(ctx_loaded, 16)

    m.a0_loads = loads
    loads, pool_work = first_loads(nc, m, a, sem)
    yield loads, nothing, nothing, pool_work

    with nc.Block() as block:
        @block.sync
        def _(sp):
            m.fetch.wait(sp)

        @block.gpsimd
        def _(pool):
            m.fetch.wait(pool)
            pool.tensor_copy(m.narrow[:, :], m.packs["narrow"][:, :]).then_inc(narrowed, 1)
            pool.wait_ge(narrowed, 1)

        @block.tensor
        def _(pe):
            pe.matmul(m.ps[7][:, 0:B * J], m.w0T[:, :], m.ctxT[:, :, :], start=True, stop=True).then_inc(k_ready, 1)
            for s in range(B + 3):
                if s < B:
                    ge(pe, q_done, s - 1)
                    pe.matmul(m.ps[s % 2][:, :], m.w0T[:, :], m.xnT[:, s * S:(s + 1) * S],
                              start=True, stop=True).then_inc(q_ready, 1)
                if 1 <= s <= B:
                    b = s - 1
                    pe.wait_ge(q_done, b + 1)
                    if b == 0:
                        pe.wait_ge(k_done, 1)
                        pe.wait_ge(bias_done, 1)
                    ge(pe, sub_done, b - 1)
                    for t in range(TB):
                        o = m.ps[2 + b % 2][:, t * J:(t + 1) * J]
                        pe.matmul(o, qT[:, (b * TB + t) * P:(b * TB + t + 1) * P], kT[:, b, :], start=True, stop=False)
                        ins = pe.matmul(o, ones1[0:1, :], madd[:, b * J:(b + 1) * J], start=False, stop=True)
                    ins.then_inc(s_ready, 1)
                if 2 <= s <= B + 1:
                    b = s - 2
                    pe.wait_ge(exp_done, b + 1)
                    ge(pe, t_done, b - 1)
                    for t in range(TB):
                        ins = pe.transpose(m.ps[(4, 7)[b % 2]][0:J, t * P:(t + 1) * P], pr[:, b, t, :], m.ident[:, :])
                    ins.then_inc(t_ready, 1)
                if 3 <= s:
                    b = s - 3
                    pe.wait_ge(t_done, b + 1)
                    ge(pe, x_done, b)
                    if b == 0:
                        pe.wait_ge(ctx_loaded, 32)
                    for t in range(TB):
                        i = b * TB + t
                        ins = pe.matmul(m.ps[5 + t // 2][:, t % 2 * 129:t % 2 * 129 + 129], prT[:, i * P:(i + 1) * P],
                                        ctxv[:, b, :], start=True, stop=True)
                    ins.then_inc(o_ready, 1)

        @block.vector
        def _(dve):
            m.dve(dve.memset(ones1[:, :], 1.0))
            m.dve(dve.memset(ctxv[:, :, D:D + 1], 1.0))
            m.dve.wait(dve)
            dve.wait_ge(k_ready, 1)
            dve.tensor_scalar(kT[:, :, :], m.ps[7][:, 0:B * J].rearrange("p (b j) -> p b j", b=B), 0.0, m.diag0[:, 0:1],
                              ALU.max, ALU.mult).then_inc(k_done, 1)
            dve.wait_ge(ctx_loaded, 32)
            dve.tensor_scalar(madd[:, :], maski[:, :], 10000.0, -10000.0, ALU.mult, ALU.add).then_inc(bias_done, 1)
            for s in range(B + 3):
                if s < B:
                    dve.wait_ge(q_ready, s + 1)
                    dve.tensor_scalar(qT[:, s * S:(s + 1) * S], m.ps[s % 2][:, :], 0.0, None, ALU.max).then_inc(q_done, 1)
                if 1 <= s <= B:
                    b = s - 1
                    dve.wait_ge(s_ready, b + 1)
                    sc = m.ps[2 + b % 2][:, 0:TB * J].rearrange("p (t j) -> p t j", t=TB)
                    m.dve(dve.tensor_reduce(mx[:, b, :], sc, AX.X, ALU.max))
                    m.dve.wait(dve)
                    dve.tensor_tensor(pr[:, b, :, :], sc, mx[:, b, :].unsqueeze(2).broadcast_to([P, TB, J]),
                                      ALU.subtract).then_inc(sub_done, 1)
                if 3 <= s:
                    b = s - 3
                    dve.wait_ge(o_ready, b + 1)
                    for t in range(TB):
                        i = b * TB + t
                        m.dve(dve.reciprocal(rden[:, i:i + 1], m.ps[5 + t // 2][:, t % 2 * 129 + 128:t % 2 * 129 + 129]))
                    m.dve.wait(dve)
                    for t in range(TB):
                        i = b * TB + t
                        ins = dve.scalar_tensor_tensor(m.x[:, i, :], m.ps[5 + t // 2][:, t % 2 * 129:t % 2 * 129 + 128],
                                                       rden[:, i:i + 1], m.x[:, i, :], ALU.mult, ALU.add)
                        m.dve(ins)
                    m.dve.wait(dve)
                    dve.sem_inc(x_done, 1)

        @block.scalar
        def _(act):
            for s in range(1, B + 2):
                if s <= B:
                    b = s - 1
                    act.wait_ge(sub_done, b + 1)
                    act.activation(pr[:, b, :, :], pr[:, b, :, :], ACT.Exp).then_inc(exp_done, 1)
                if s >= 2:
                    b = s - 2
                    act.wait_ge(t_ready, b + 1)
                    act.copy(prT[:, b * S:(b + 1) * S], m.ps[(4, 7)[b % 2]][0:J, :]).then_inc(t_done, 1)


def moe(nc, m, a, sem, sb, name, ahead, blocks, topk, cap, biased, gated, act_fn, x_stage, last):
    context = m.context8[ahead] if ahead else None
    G, k = blocks, topk
    Q = k * NT
    U = 8
    assert G % U == 0
    W = 2 if gated else 1
    w1 = sb(name + "_w1", [P, E, W, F])
    w2 = sb(name + "_w2", [P, E, FC, D])
    b1 = sb(name + "_b1", [P, E, FC]) if biased else None
    b2 = sb(name + "_b2", [P, E, D]) if biased else None
    weights = [("w1", w1[:, :, 0, :]), ("w2", w2[:, :, :, :].rearrange("p e c d -> p e (c d)"))]
    if gated:
        weights.append(("w3", w1[:, :, 1, :]))
    if biased:
        weights += [("b1", b1[:, :, :]), ("b2", b2[:, :, :])]

    def loads(sp):
        for n, t in weights:
            for half in (slice(0, E // 2), slice(E // 2, E)):
                m.fetch(sp.dma_start(t[:, half, :], a[f"{name}_{n}"][half, :, :].rearrange("e p f -> p e f")))

    (logits_ready, shifted, exped, sel_ready, rank_ready, slots_known, index_ready, index_done, table_ready, xn_out,
     xT_ready, xT_done, wnow_done, h_ready, h_act, h_done, y_ready, y_done, gnow_done, snow_done, pool_pass,
     blkhot_done, code_done, combined, combined_pool, stored) = (
        sem(f"{name}_{n}") for n in (
        "logits_ready", "shifted", "exped", "sel_ready", "rank_ready", "slots_known", "index_ready", "index_done",
        "table_ready", "xn_out", "xT_ready", "xT_done", "wnow_done", "h_ready", "h_act", "h_done",
        "y_ready", "y_done", "gnow_done", "snow_done", "pool_pass",
        "blkhot_done", "code_done", "combined", "combined_pool", "stored"))
    x_in, scattered = ([sem(f"{name}_{n}{sl}") for sl in range(U)] for n in ("x_in", "scattered"))
    back_in = [sem(f"{name}_back_in{q}") for q in range(B)]
    bt = lambda ap: ap.unsqueeze(1).broadcast_to([P, NT, E])
    be = lambda ap: ap.unsqueeze(2).broadcast_to([P, NT, E])
    weight = sb(name + "_weight", [P, k, NT])
    wt = [weight[:, j, :] for j in range(k)]
    btabi = sb(name + "_btabi", [1, G], I32)
    gidx = sb(name + "_gidx", [P, G], U32)
    sidx = sb(name + "_sidx", [P, G], U32)

    def pe_logits(pe, b):
        for i in range(b * TB, (b + 1) * TB):
            ins = pe.matmul(m.ps[4][:, i * E:(i + 1) * E], m.xnT[:, i * P:(i + 1) * P], m.small[name + "_router"][:, :],
                            start=True, stop=True)
        if b == B - 1:
            ins.then_inc(logits_ready, 1)

    yield loads, nothing, nothing, nothing, pe_logits
    fetched = m.fetch.n

    pairs_in, pairs_out = a["pairs_in"][0:Q * P, :], a[f"{name}_pairs_out"]

    with ExitStack() as inner:
        tp = lambda n, shape, dt=F32: inner.enter_context(nc.sbuf_tensor(f"{name}_{n}", shape, dt))
        lg, l2 = tp("lg", [P, NT, E]), tp("l2", [P, NT, E])
        tmp = [tp(f"tmp{i}", [P, NT, E]) for i in range(2)]
        picked, pick = tp("picked", [P, k, NT, E]), tp("pick", [P, k, NT, E])
        oh = [picked[:, j, :, :] for j in range(k)]
        top = [tp(f"top{i}", [P, NT]) for i in range(k)]
        low, den = tp("low", [P, NT]), tp("den", [P, NT])
        dif, ex = (tp(n, [P, NT, E] if k == 1 else [P, NT]) for n in ("dif", "ex"))
        sel = tp("sel", [P, E, NT], BF16)
        run, over = (tp(n, [P, E, NT]) for n in ("run", "over"))
        rank, keep = tp("rank", [P, NT, E]), tp("keep", [P, NT, E])
        cnt, nblk, bend, base = (tp(n, [P, E]) for n in ("cnt", "nblk", "bend", "base"))
        pos = tp("pos", [P, k, NT])
        kept = tp("kept", [P, k, NT])
        div, mod = tp("div", [P, Q]), tp("mod", [P, Q], BF16)
        rowhot = tp("rowhot", [P, Q, P], BF16)
        blkhot = tp("blkhot", [P, Q, G], BF16)
        code = tp("code", [P, Q, 2, G], BF16)
        found, ffree = tp("found", [P, G]), tp("ffree", [P, G])
        cmpt, btab = tp("cmpt", [1, G, E]), tp("btab", [1, G])

        with nc.Block() as block:
            @block.sync
            def _(sp):
                for j in range(k):
                    sp.dma_start(pairs_in[j * N:(j + 1) * N, :].rearrange("(i p) d -> p i d", p=P), m.xn[:, :, :]).then_inc(xn_out, 16)
                sp.wait_ge(xn_out, 16 * k)

            @block.gpsimd
            def _(pool):
                if context:
                    context.pool_keys(pool)
                for j in range(k):
                    own = slice(j * NT, (j + 1) * NT)
                    pool.wait_ge(blkhot_done, j + 1)
                    pool.tensor_tensor(code[:, own, 0, :], blkhot[:, own, :],
                                       m.small["tile1"][:, own].unsqueeze(2).broadcast_to([P, NT, G]), ALU.mult).then_inc(code_done, 1)
                    pool.tensor_scalar(code[:, own, 1, :], blkhot[:, own, :], m.small["part"][:, 0:1], 0.0, ALU.mult, ALU.add).then_inc(code_done, 1)

            @block.tensor
            def _(pe):
                if context:
                    context.pe_keys(pe)
                if context:
                    context.pe_values(pe, 0)
                pe.wait_ge(sel_ready, 1)
                pe.matmul(m.ps[1][:, 0:P], m.tri[:, :], sel[:, :, :], start=True, stop=True)
                pe.matmul(m.ps[2][:, 0:P], m.onesb[:, :], sel[:, :, :], start=True, stop=True).then_inc(rank_ready, 1)
                if context:
                    context.pe_values(pe, 1)
                    context.pe_values(pe, 2)
                for q in range(Q):
                    if q % NT == 0:
                        pe.wait_ge(slots_known, q // NT + 1)
                        pe.wait_ge(code_done, 2 * (q // NT + 1))
                    ins = pe.matmul(m.ps[3][:, 0:2 * G], rowhot[:, q, :], code[:, q, :, :], start=(q == 0), stop=(q == Q - 1))
                ins.then_inc(index_ready, 1)

            @block.scalar
            def _(act):
                if context:
                    context.act_keys(act)
                act.wait_ge(shifted, 1)
                sl = tuple([slice(None)] * len(dif.shape))
                act.activation(ex[sl], dif[sl], ACT.Exp).then_inc(exped, 1)
                if context:
                    for b in range(B - 1):
                        context.act_values(act, b)

            @block.vector
            def _(dve):
                c = m.dve

                def step(ins):
                    c(ins)
                    c.wait(dve)

                dve.wait_ge(logits_ready, 1)
                logits = m.ps[4][:, 0:NT * E].rearrange("p (i e) -> p i e", e=E)
                if biased:
                    step(dve.tensor_tensor(lg[:, :, :], logits, bt(m.small[name + "_rbias"][:, :]), ALU.add))
                src = score = lg[:, :, :] if biased else logits
                for j in range(k):
                    step(dve.tensor_reduce(top[j][:, :], src, AX.X, ALU.max))
                    step(dve.tensor_tensor(tmp[0][:, :, :], src, be(top[j][:, :]), ALU.is_equal))
                    step(dve.scalar_tensor_tensor(tmp[1][:, :, :], tmp[0][:, :, :], -float(E), bt(m.iota8[:, :]), ALU.mult, ALU.add))
                    step(dve.tensor_reduce(low[:, :], tmp[1][:, :, :], AX.X, ALU.min))
                    step(dve.scalar_tensor_tensor(oh[j], bt(m.iota8[:, :]), -float(E), be(low[:, :]), ALU.add, ALU.is_equal))
                    if j + 1 < k:
                        step(dve.scalar_tensor_tensor(l2[:, :, :], oh[j], -1e30, score, ALU.mult, ALU.add))
                        src = l2[:, :, :]
                if k == 1:
                    dve.tensor_tensor(dif[:, :, :], lg[:, :, :], be(top[0][:, :]), ALU.subtract).then_inc(shifted, 1)
                    dve.tensor_copy(sel[:, :, :].rearrange("p e i -> p i e"), oh[0]).then_inc(sel_ready, 1)
                    dve.wait_ge(exped, 1)
                    step(dve.tensor_reduce(den[:, :], ex[:, :, :], AX.X, ALU.add))
                    step(dve.reciprocal(wt[0], den[:, :]))
                else:
                    dve.tensor_tensor(dif[:, :], top[1][:, :], top[0][:, :], ALU.subtract).then_inc(shifted, 1)
                    dve.tensor_tensor(sel[:, :, :].rearrange("p e i -> p i e"), oh[0], oh[1], ALU.add).then_inc(sel_ready, 1)
                    dve.wait_ge(exped, 1)
                    step(dve.tensor_scalar(den[:, :], ex[:, :], 1.0, None, ALU.add))
                    step(dve.reciprocal(wt[0], den[:, :]))
                    step(dve.tensor_tensor(wt[1], ex[:, :], wt[0], ALU.mult))
                dve.wait_ge(rank_ready, 1)
                total = m.ps[2][:, 0:P]
                step(dve.tensor_tensor_scan(run[:, :, :].rearrange("p e i -> p (e i)"), m.restart[:, :], total, 0.0, ALU.mult, ALU.add))
                step(dve.tensor_tensor(over[:, :, :], run[:, :, :], total.rearrange("p (e i) -> p e i", e=E), ALU.subtract))
                step(dve.tensor_tensor(rank[:, :, :], m.ps[1][:, 0:P].rearrange("p (e i) -> p i e", e=E),
                                       over[:, :, :].rearrange("p e i -> p i e"), ALU.add))
                step(dve.tensor_scalar(cnt[:, :], run[:, :, NT - 1], float(cap if cap else N), None, ALU.min))
                step(dve.tensor_tensor(over[:, :, :], cnt[:, :].unsqueeze(2).broadcast_to([P, E, NT]),
                                       m.iota128[:, :].unsqueeze(1).broadcast_to([P, E, NT]), ALU.is_gt))
                step(dve.tensor_reduce(nblk[:, :], over[:, :, :], AX.X, ALU.add))
                step(dve.tensor_tensor_scan(bend[:, :], m.one8[:, :], nblk[:, :], 0.0, ALU.mult, ALU.add))
                step(dve.tensor_tensor(base[:, :], bend[:, :], nblk[:, :], ALU.subtract))
                if cap:
                    step(dve.tensor_scalar(keep[:, :, :], rank[:, :, :], float(cap), None, ALU.is_lt))
                step(dve.scalar_tensor_tensor(rank[:, :, :], bt(base[:, :]), float(P), rank[:, :, :], ALU.mult, ALU.add))
                of_pairs = lambda t: t[:, :, :].unsqueeze(1).broadcast_to([P, k, NT, E])
                step(dve.tensor_tensor(pick[:, :, :, :], picked[:, :, :, :], of_pairs(rank), ALU.mult))
                step(dve.tensor_reduce(pos[:, :, :], pick[:, :, :, :], AX.X, ALU.add))
                if cap:
                    step(dve.tensor_tensor(pick[:, :, :, :], picked[:, :, :, :], of_pairs(keep), ALU.mult))
                    step(dve.tensor_reduce(kept[:, :, :], pick[:, :, :, :], AX.X, ALU.add))
                    step(dve.tensor_tensor(weight[:, :, :], weight[:, :, :], kept[:, :, :], ALU.mult))
                    step(dve.tensor_scalar(kept[:, :, :], kept[:, :, :], -float(2 * G * P), float(2 * G * P), ALU.mult, ALU.add))
                    step(dve.tensor_tensor(pos[:, :, :], pos[:, :, :], kept[:, :, :], ALU.add))
                flat = pos[:, :, :].rearrange("p j i -> p (j i)")
                step(dve.tensor_scalar(div[:, :], flat, 1.0 / P, -63.5 / P, ALU.mult, ALU.add))
                step(dve.tensor_scalar(div[:, :], div[:, :], MAGIC, MAGIC, ALU.add, ALU.subtract))
                step(dve.scalar_tensor_tensor(mod[:, :], div[:, :], -float(P), flat, ALU.mult, ALU.add))
                each = lambda t, n: t.unsqueeze(2).broadcast_to([P, NT, n])
                row = lambda t, n: t.unsqueeze(1).broadcast_to([P, NT, n])
                own = [slice(j * NT, (j + 1) * NT) for j in range(k)]
                for j in range(k):
                    dve.tensor_tensor(blkhot[:, own[j], :], each(div[:, own[j]], G), row(m.small["iotag"][:, 0:G], G), ALU.is_equal).then_inc(blkhot_done, 1)
                for j in range(k):
                    dve.tensor_tensor(rowhot[:, own[j], :], each(mod[:, own[j]], P), row(m.small["iotar"][:, :], P), ALU.is_equal).then_inc(slots_known, 1)
                step(dve.tensor_tensor(cmpt[:, :, :], m.small["iotag"][0:1, 0:G].unsqueeze(2).broadcast_to([1, G, E]),
                                       bend[0:1, :].unsqueeze(1).broadcast_to([1, G, E]), ALU.is_ge))
                step(dve.tensor_reduce(btab[:, :], cmpt[:, :, :], AX.X, ALU.add))
                dve.tensor_scalar(btabi[:, :], btab[:, :], float(E - 1), None, ALU.min).then_inc(table_ready, 1)
                dve.wait_ge(index_ready, 1)
                step(dve.tensor_copy(ffree[:, :], m.ps[3][:, G:2 * G]))
                step(dve.scalar_tensor_tensor(found[:, :], m.ps[3][:, 0:G], float(P), ffree[:, :], ALU.mult, ALU.add))
                step(dve.tensor_scalar(found[:, :], found[:, :], -float(P), None, ALU.add))
                step(dve.tensor_scalar(ffree[:, :], found[:, :], 0.0, float(2 * Q * P), ALU.is_lt, ALU.mult))
                dve.tensor_scalar(gidx[:, :], found[:, :], 0.0, None, ALU.max).then_inc(index_done, 1)
                dve.tensor_tensor(sidx[:, :], found[:, :], ffree[:, :], ALU.add).then_inc(index_done, 1)
                dve.wait_ge(index_done, 2)

    xb = sb(name + "_xb", [P, U, D])
    xT = sb(name + "_xT", [P, 2, P])
    wnow = sb(name + "_wnow", [P, 2, W, F])
    hp = sb(name + "_hp", [P, 2, F]) if gated or biased else None
    h = sb(name + "_h", [P, 2, F])
    yb = sb(name + "_yb", [P, U, D])
    gnow, snow = (sb(f"{name}_{n}", [P, U], U32) for n in ("gnow", "snow"))
    IT = G // U
    LAG = U - 2

    def back(n, sl, by):
        if sl < by:
            n, sl = n - 1, sl + U
        if isinstance(n, int) and not 0 <= n < IT:
            return None
        return n, sl - by

    def loop(eng, body, tail):
        for sl in range(U):
            body(0, sl)
        with eng.Fori(1, IT) as n:
            for sl in range(U):
                body(n, sl)
        for sl in range(tail):
            body(IT, sl)

    with nc.Block() as block:
        @block.gpsimd
        def _(pool):
            def indices(nn, ss, table, now, done):
                g = nn * U + ss
                pool.sem_inc(pool_pass, 1)
                pool.tensor_copy(now[:, ss:ss + U // 2], table[:, bass.ds(g, U // 2)]).then_inc(done, 1)
                pool.wait_ge(done, 2 * nn + ss // (U // 2) + 1)
                pool.sem_inc(pool_pass, 1)

            def body(n, sl):
                if (at := back(n, sl, 0)):
                    g = at[0] * U + sl
                    if sl % (U // 2) == 0:
                        ge(pool, xT_ready, g - U // 2)
                        indices(n, sl, gidx, gnow, gnow_done)
                    else:
                        ge(pool, xT_ready, g + 1 - U)
                        pool.sem_inc(pool_pass, 1)
                    pool.indirect_dma_start(out=xb[:, sl, :], out_offset=None, in_=pairs_in,
                                            in_offset=bass.IndirectOffsetOnAxis(ap=gnow[:, sl:sl + 1], axis=0)).then_inc(x_in[sl], 16)
                if (at := back(n, sl, LAG)):
                    nn, ss = at
                    g = nn * U + ss
                    if ss % (U // 2) == 0:
                        for other in range(ss, ss + U // 2):
                            ge(pool, scattered[other], 16 * nn)
                        indices(nn, ss, sidx, snow, snow_done)
                    pool.wait_ge(y_done, g + 1)
                    pool.sem_inc(pool_pass, 1)
                    pool.indirect_dma_start(out=pairs_out, out_offset=bass.IndirectOffsetOnAxis(ap=snow[:, ss:ss + 1], axis=0),
                                            in_=yb[:, ss, :], in_offset=None, bounds_check=Q * P - 1,
                                            oob_is_err=False).then_inc(scattered[ss], 16)

            loop(pool, body, LAG)

        @block.tensor
        def _(pe):
            def body(n, sl):
                if (at := back(n, sl, 1)):
                    nn, ss = at
                    g = nn * U + ss
                    pe.wait_ge(xT_done, g + 1)
                    pe.wait_ge(wnow_done, g + 1)
                    for q in range(W):
                        for f in range(FC):
                            ins = pe.matmul(m.ps[1 + 2 * q + ss % 2][:, f * P:(f + 1) * P], wnow[:, ss % 2, q, f * P:(f + 1) * P],
                                            xT[:, ss % 2, :], start=True, stop=True)
                    ins.then_inc(h_ready, 1)
                if (at := back(n, sl, 0)):
                    pe.wait_ge(x_in[sl], 16 * (n + 1))
                    pe.transpose(m.ps[0][:, 0:P], xb[:, sl, :], m.ident[:, :]).then_inc(xT_ready, 1)
                if (at := back(n, sl, 2)):
                    nn, ss = at
                    g = nn * U + ss
                    e = pe.value_load(btabi[0:1, bass.ds(g, 1)], min_val=0, max_val=E - 1)
                    pe.wait_ge(h_done, g + 1)
                    ge(pe, y_done, g)
                    for f in range(FC):
                        ins = pe.matmul(m.ps[7][:, 0:D], h[:, ss % 2, f * P:(f + 1) * P],
                                        w2[:, bass.ds(e, 1), f, :].rearrange("p e d -> p (e d)"), start=(f == 0), stop=(f == FC - 1))
                    ins.then_inc(y_ready, 1)

            if context:
                context.pe_values(pe, B - 1)
                pe.wait_ge(context.v_copied, B)
            pe.wait_ge(m.fetch.sem, 16 * fetched)
            loop(pe, body, 2)

        @block.scalar
        def _(act):
            def body(n, sl):
                if (at := back(n, sl, 0)):
                    g = at[0] * U + sl
                    e = act.value_load(btabi[0:1, bass.ds(g, 1)], min_val=0, max_val=E - 1)
                    ge(act, h_ready, g - 1)
                    act.copy(wnow[:, sl % 2, :, :].rearrange("p q f -> p (q f)"),
                             w1[:, bass.ds(e, 1), :, :].rearrange("p e q f -> p (e q f)")).then_inc(wnow_done, 1)
                if (at := back(n, sl, 1)):
                    nn, ss = at
                    g = nn * U + ss
                    if gated:
                        act.wait_ge(h_ready, g + 1)
                        ge(act, h_done, g - 1)
                        act.activation(hp[:, ss % 2, :], m.ps[1 + ss % 2][:, :], act_fn).then_inc(h_act, 1)
                    else:
                        act.wait_ge(h_act if biased else h_ready, g + 1)
                        ge(act, y_ready, g - 1)
                        act.activation(h[:, ss % 2, :], hp[:, ss % 2, :] if biased else m.ps[1 + ss % 2][:, :], act_fn).then_inc(h_done, 1)

            if context:
                context.act_values(act, B - 1)
            act.wait_ge(m.fetch.sem, 16 * fetched)
            loop(act, body, 1)

        @block.vector
        def _(dve):
            def body(n, sl):
                if (at := back(n, sl, 0)):
                    g = at[0] * U + sl
                    dve.wait_ge(xT_ready, g + 1)
                    ge(dve, h_ready, g - 1)
                    dve.tensor_copy(xT[:, sl % 2, :], m.ps[0][:, 0:P]).then_inc(xT_done, 1)
                if (gated or biased) and (at := back(n, sl, 1)):
                    nn, ss = at
                    g = nn * U + ss
                    if gated:
                        dve.wait_ge(h_act, g + 1)
                        ge(dve, y_ready, g - 1)
                        dve.tensor_tensor(h[:, ss % 2, :], hp[:, ss % 2, :], m.ps[3 + ss % 2][:, :], ALU.mult).then_inc(h_done, 1)
                    else:
                        e = dve.value_load(btabi[0:1, bass.ds(g, 1)], min_val=0, max_val=E - 1)
                        dve.wait_ge(h_ready, g + 1)
                        ge(dve, h_done, g - 1)
                        chunks = lambda t: t.rearrange("p (f r) -> p f r", f=FC)
                        dve.tensor_tensor(chunks(hp[:, ss % 2, :]), chunks(m.ps[1 + ss % 2][:, :]),
                                          b1[:, bass.ds(e, 1), :].rearrange("p e f -> p (e f)").unsqueeze(2).broadcast_to([P, FC, P]),
                                          ALU.add).then_inc(h_act, 1)
                if (at := back(n, sl, 2)):
                    nn, ss = at
                    g = nn * U + ss
                    if biased:
                        e = dve.value_load(btabi[0:1, bass.ds(g, 1)], min_val=0, max_val=E - 1)
                    dve.wait_ge(y_ready, g + 1)
                    ge(dve, scattered[ss], 16 * nn)
                    if biased:
                        dve.tensor_tensor(yb[:, ss, :], m.ps[7][:, 0:D],
                                          b2[:, bass.ds(e, 1), :].rearrange("p e d -> p (e d)"), ALU.add).then_inc(y_done, 1)
                    else:
                        dve.tensor_copy(yb[:, ss, :], m.ps[7][:, 0:D]).then_inc(y_done, 1)

            if x_stage:
                m.dve(dve.tensor_tensor(m.x[:, :, :], m.x[:, :, :], m.xn[:, :, :], ALU.add))
            loop(dve, body, 2)
            m.dve.wait(dve)

    got = sb(name + "_got", [P, Q, D])
    with nc.Block() as block:
        @block.sync
        def _(sp):
            for q in scattered:
                sp.wait_ge(q, 16 * IT)
            rows = pairs_out.rearrange("(q p) d -> p q d", p=P)
            for b in range(B):
                for j in range(k):
                    tiles = slice(j * NT + b * TB, j * NT + (b + 1) * TB)
                    sp.dma_start(got[:, tiles, :], rows[:, tiles, :]).then_inc(back_in[b], 16)
            if last:
                out = a["out"].rearrange("b (i p) d -> p b i d", p=P)
                for b in (*range(1, B), 0):
                    if b:
                        sp.wait_ge(combined, b)
                    else:
                        sp.wait_ge(combined_pool, 2 * k)
                    sp.dma_start(out[:, b, :, :], m.x[:, b * TB:(b + 1) * TB, :]).then_inc(stored, 16)
                sp.wait_ge(stored, 16 * B)

        @block.gpsimd
        def _(pool):
            tiles = slice(0, TB)
            pool.wait_ge(back_in[0], 16 * k)
            for j in range(k):
                y = got[:, j * NT:j * NT + TB, :]
                pool.tensor_tensor(y, y, wt[j][:, tiles].unsqueeze(2).broadcast_to([P, TB, D]), ALU.mult).then_inc(combined_pool, 1)
                pool.wait_ge(combined_pool, 2 * j + 1)
                pool.tensor_tensor(m.x[:, tiles, :], m.x[:, tiles, :], y, ALU.add).then_inc(combined_pool, 1)
                pool.wait_ge(combined_pool, 2 * j + 2)

        @block.vector
        def _(dve):
            for b in range(1, B):
                dve.wait_ge(back_in[b], 16 * k)
                for j in range(k):
                    for i in range(b * TB, (b + 1) * TB):
                        m.dve(dve.scalar_tensor_tensor(m.x[:, i, :], got[:, j * NT + i, :], wt[j][:, i:i + 1], m.x[:, i, :],
                                                       ALU.mult, ALU.add))
                    m.dve.wait(dve)
                dve.sem_inc(combined, 1)


class Context8:

    def __init__(self, m, sem, name, keys, kbias, values, vbias):
        self.m, self.keys, self.kbias, self.values, self.vbias = m, keys, kbias, values, vbias
        self.k_ready, self.k_done, self.kb_done, self.v_ready, self.v_copied, self.v_biased, self.vf_done = (
            sem(f"{name}_{n}") for n in ("k_ready", "k_done", "kb_done", "v_ready", "v_copied", "v_biased", "vf_done"))

    def pe_keys(self, pe):
        if self.keys is not None:
            pe.matmul(self.m.ps[7][:, 0:B * J], self.keys[:, :], self.m.ctxT[:, :, :], start=True, stop=True).then_inc(self.k_ready, 1)

    def act_keys(self, act):
        if self.keys is not None:
            act.wait_ge(self.k_ready, 1)
            act.copy(self.m.kT[:, :, :], self.m.ps[7][:, 0:B * J].rearrange("p (b j) -> p b j", b=B)).then_inc(self.k_done, 1)

    def pool_keys(self, pool):
        kT = self.m.ctxT
        if self.keys is not None:
            kT = self.m.kT
            pool.wait_ge(self.k_done, 1)
            pool.tensor_scalar(kT[:, :, :], kT[:, :, :], self.kbias[:, 0:1], None, ALU.add).then_inc(self.k_done, 1)
            pool.wait_ge(self.k_done, 2)
        for b in range(B):
            pool.tensor_tensor(self.m.kb[:, b, :, :], kT[:, b, :].unsqueeze(1).broadcast_to([P, H, J]),
                               self.m.small["qmask"][:, :].unsqueeze(2).broadcast_to([P, H, J]), ALU.mult).then_inc(self.kb_done, 1)

    def pe_values(self, pe, b):
        ge(pe, self.v_copied, b - 1)
        for n, c in enumerate(CHUNKS):
            ins = pe.matmul(self.m.ps[5 + b % 2][:, n * CH * HD:(n + 1) * CH * HD], self.m.ctxT3[:, b, c.row:c.row + P],
                            self.values[:, c.h0 * HD:(c.h0 + CH) * HD], start=True, stop=True)
        ins.then_inc(self.v_ready, 1)

    def act_values(self, act, b):
        act.wait_ge(self.v_ready, b + 1)
        act.copy(self.m.vraw[:, b, :], self.m.ps[5 + b % 2][:, 0:NC * CH * HD]).then_inc(self.v_copied, 1)

    def pool_values(self, pool):
        mask, vraw = self.m.small["vmask"][:, :], self.m.vraw
        pool.wait_ge(self.kb_done, B)
        pool.wait_ge(self.v_copied, B)
        for b in range(B):
            out = self.m.vf[:, b, :, :].rearrange("p c (h e) -> p (c h) e", e=HD + 1)
            if self.vbias is not None:
                pool.tensor_tensor(vraw[:, b, :], vraw[:, b, :], self.vbias[:, :], ALU.add).then_inc(self.v_biased, 1)
                pool.wait_ge(self.v_biased, b + 1)
            pool.tensor_tensor(out[:, :, 0:HD], vraw[:, b, :].rearrange("p (c e) -> p c e", e=HD),
                               mask.unsqueeze(2).broadcast_to([P, NC * CH, HD]), ALU.mult).then_inc(self.vf_done, 1)
            pool.tensor_copy(out[:, :, HD], mask).then_inc(self.vf_done, 1)
        pool.wait_ge(self.vf_done, 2 * B)


LATE = NG - 1


def rotate(eng, body, lag):
    for t in range(TB):
        body(0, t)
    with eng.Fori(1, B) as b:
        for t in range(TB):
            body(b, t)
    for t in range(lag):
        body(B, t)


def due(b, t, by):
    while t < by:
        b, t = b - 1, t + TB
    if isinstance(b, int) and not 0 <= b < B:
        return None
    return b, t - by


def turn_queries(m, pool, b, t, qT, s_ready, q_done, pool_pass):
    ge(pool, s_ready, b * TB + t - 2)
    pool.sem_inc(pool_pass, 1)
    at = (t + 1) % TB * P
    pool.tensor_copy(qT[:, at:at + P], m.xnT[:, bass.ds(b * S + (t + 1) * P, P)]).then_inc(q_done, 1)


def tile_statistics(m, dve, at, x, x_done, stats_done):
    if at:
        i = at[0] * TB + at[1]
        dve.wait_ge(x_done, i + 1)
        row = lambda z: z[:, bass.ds(i, 1), :].rearrange("p i d -> p (i d)")
        dve.bn_stats(row(m.stats), row(x)).then_inc(stats_done, 1)


def attention8(nc, m, a, sem, sb, name, scale, projected, masked):
    kb, vf, context = m.kb, m.vf, m.context8[name]
    wo, bo = (m.small["woT"], m.small["bo"]) if projected else (m.small["woutT"], m.small["bout"])
    (q_ready, q_biased, q_done, s_ready, sub_done, exp_done, t_ready, t_done, pv_ready, o_done, oT_ready,
     oT_done, y_ready, x_biased, x_done, stats_done, max_done, rden_done, pool_pass, mask_done) = (
        sem(f"{name}_{n}") for n in (
        "q_ready", "q_biased", "q_done", "s_ready", "sub_done", "exp_done", "t_ready", "t_done", "pv_ready",
        "o_done", "oT_ready", "oT_done", "y_ready", "x_biased", "x_done", "stats_done", "max_done", "rden_done", "pool_pass", "mask_done"))
    qT = sb(name + "_qT", [P, S])
    pr = sb(name + "_pr", [P, 2, HJ])
    prT = sb(name + "_prT", [P, 2, NC * P])
    mx = sb(name + "_mx", [P, 2, H])
    rden = sb(name + "_rden", [P, 2, H])
    o = sb(name + "_o", [P, 2, D])
    oT = sb(name + "_oT", [P, 2, P])
    if masked:
        maski = sb(name + "_maski", [P, NT, J], I32)
        madd = sb(name + "_madd", [P, NT, J], BF16)
    scores = [m.ps[i][:, 0:QJ] for i in range(4)]
    PV, OB = m.ps[6], m.ps[7]

    def loads(sp):
        if masked:
            m.fetch(sp.dma_start(maski[:, :, :], a["mask3"].rearrange("b (i p) j -> p (b i) j", p=P)))

    def pool_part(pool):
        if masked:
            m.fetch.wait(pool)
            pool.tensor_scalar(madd[:, :, :], maski[:, :, :], 0.0, MASKED, ALU.is_equal, ALU.mult).then_inc(mask_done, 1)
            pool.wait_ge(mask_done, 1)
        context.pool_values(pool)

    yield loads, nothing, nothing, pool_part

    with nc.Block() as block:
        @block.gpsimd
        def _(pool):
            if projected:
                pool.wait_ge(q_biased, 1)
            pool.tensor_copy(qT[:, 0:P], m.xnT[:, 0:P]).then_inc(q_done, 1)
            if projected:
                pool.wait_ge(q_biased, 2)
            for t in range(TB):
                turn_queries(m, pool, 0, t, qT, s_ready, q_done, pool_pass)
                if t == 0:
                    pool.tensor_tensor(m.x[:, :, :], m.x[:, :, :], bo[:, :].unsqueeze(1).broadcast_to([P, NT, D]), ALU.add).then_inc(x_biased, 1)
            if projected:
                pool.wait_ge(q_biased, B)
            with pool.Fori(1, B) as b:
                for t in range(TB):
                    turn_queries(m, pool, b, t, qT, s_ready, q_done, pool_pass)

        @block.tensor
        def _(pe):
            def body(b, t):
                if (at := due(b, t, 0)):
                    i = at[0] * TB + at[1]
                    pe.wait_ge(q_done, i + 1)
                    ge(pe, sub_done, i)
                    for r in range(4):
                        ins = pe.matmul(scores[r], qT[:, t * P:(t + 1) * P],
                                        kb[:, bass.ds(at[0], 1), r * QH:(r + 1) * QH, :].rearrange("p b h j -> p (b h j)"),
                                        start=True, stop=not masked)
                    if masked:
                        for r in range(4):
                            ins = pe.matmul(scores[r], m.small["identb"][:, :],
                                            madd[:, bass.ds(i, 1), :].broadcast_to([P, QH, J]), start=False, stop=True)
                    ins.then_inc(s_ready, 1)
                    if isinstance(i, int) and i < 2:
                        keep_warm(pe, m, 7, TILE_WARM)

                def turn(groups):
                    if (at := due(b, t, 1)):
                        i = at[0] * TB + at[1]
                        if 0 in groups:
                            pe.wait_ge(exp_done, i + 1)
                        for g in groups:
                            ge(pe, t_done, NG * i + g - 1)
                            for n, ch in enumerate(GROUPS[g]):
                                c = CHUNKS[ch]
                                ins = pe.transpose(m.ps[4 + (NG * at[1] + g) % 2][0:c.width, n * P:(n + 1) * P],
                                                   pr[:, at[1] % 2, c.at:c.at + c.width], m.ident[:, :])
                            ins.then_inc(t_ready, 1)

                turn(range(LATE))
                if (at := due(b, t, 3)):
                    i = at[0] * TB + at[1]
                    pe.wait_ge(o_done, i + 1)
                    ge(pe, x_done, i)
                    pe.transpose(OB[:, 0:P], o[:, at[1] % 2, :], m.ident[:, :]).then_inc(oT_ready, 1)
                if (at := due(b, t, 2)):
                    i = at[0] * TB + at[1]
                    pe.wait_ge(t_done, NG * (i + 1))
                    ge(pe, o_done, i)
                    for n, c in enumerate(CHUNKS):
                        ins = pe.matmul(PV[:, c.h0 * 9:(c.h0 + CH) * 9], prT[0:c.width, at[1] % 2, n * P:(n + 1) * P],
                                        vf[0:c.width, bass.ds(at[0], 1), n, :].rearrange("p b e -> p (b e)"),
                                        start=(n == 0), stop=(n == NC - 1), skip_group_check=True)
                    ins.then_inc(pv_ready, 1)
                turn([LATE])
                if (at := due(b, t, 3)):
                    i = at[0] * TB + at[1]
                    pe.wait_ge(oT_done, i + 1)
                    pe.matmul(OB[:, P:P + D], oT[:, at[1] % 2, :], wo[:, :], start=True, stop=True).then_inc(y_ready, 1)

            if projected:
                for b in range(B):
                    pe.matmul(m.ps[b][:, :], m.small["wqT"][:, :], m.xnT[:, b * S:(b + 1) * S], start=True, stop=True).then_inc(q_ready, 1)
                pe.wait_ge(q_biased, B)
            rotate(pe, body, 3)

        @block.vector
        def _(dve):
            if projected:
                for b in range(B):
                    dve.wait_ge(q_ready, b + 1)
                    dve.tensor_scalar(m.xnT[:, b * S:(b + 1) * S], m.ps[b][:, :], m.small["bq"][:, 0:1], None, ALU.add).then_inc(q_biased, 1)
            bank4 = m.all_banks[:, 0:4, 0:QJ].rearrange("p r (h j) -> p r h j", h=QH)

            def body(b, t):
                tile_statistics(m, dve, due(b, t, 4), m.x, x_done, stats_done)
                if (at := due(b, t, 0)):
                    i = at[0] * TB + at[1]
                    dve.wait_ge(s_ready, i + 1)
                    dve.tensor_reduce(mx[:, t % 2, :], bank4, AX.X, ALU.max).then_inc(max_done, 1)
                    dve.wait_ge(max_done, i + 1)
                    ge(dve, t_ready, NG * (i - 1))
                    dve.tensor_tensor(pr[:, t % 2, :].rearrange("p (r h j) -> p r h j", r=4, h=QH), bank4,
                                      mx[:, t % 2, :].rearrange("p (r h) -> p r h", r=4).unsqueeze(3).broadcast_to([P, 4, QH, J]),
                                      ALU.subtract).then_inc(sub_done, 1)
                if (at := due(b, t, 3)):
                    i = at[0] * TB + at[1]
                    dve.wait_ge(oT_ready, i + 1)
                    dve.tensor_copy(oT[:, at[1] % 2, :], OB[:, 0:P]).then_inc(oT_done, 1)
                if (at := due(b, t, 2)):
                    i = at[0] * TB + at[1]
                    pv = PV[:, 0:H * 9].rearrange("p (h e) -> p h e", e=9)
                    dve.wait_ge(pv_ready, i + 1)
                    dve.reciprocal(rden[:, at[1] % 2, :], pv[:, :, HD]).then_inc(rden_done, 1)
                    dve.wait_ge(rden_done, i + 1)
                    dve.tensor_tensor(o[:, at[1] % 2, :].rearrange("p (h e) -> p h e", e=HD), pv[:, :, 0:HD],
                                      rden[:, at[1] % 2, :].unsqueeze(2).broadcast_to([P, H, HD]), ALU.mult).then_inc(o_done, 1)
                if (at := due(b, t, 3)):
                    i = at[0] * TB + at[1]
                    dve.wait_ge(y_ready, i + 1)
                    if isinstance(i, int) and i == 0:
                        dve.wait_ge(x_biased, 1)
                    xi = m.x[:, bass.ds(i, 1), :].rearrange("p i d -> p (i d)")
                    dve.tensor_tensor(xi, xi, OB[:, P:P + D], ALU.add).then_inc(x_done, 1)

            rotate(dve, body, 4)
            dve.wait_ge(stats_done, NT)

        @block.scalar
        def _(act):
            def body(b, t):
                def copy(groups):
                    if (at := due(b, t, 1)):
                        i = at[0] * TB + at[1]
                        for g in groups:
                            group = GROUPS[g]
                            act.wait_ge(t_ready, NG * i + g + 1)
                            if g == 0:
                                ge(act, pv_ready, i - 1)
                            bank, at0 = m.ps[4 + (NG * at[1] + g) % 2], P * group[0]
                            full = sum(CHUNKS[ch].width == P for ch in group)
                            ins = act.copy(prT[:, at[1] % 2, at0:at0 + full * P], bank[:, 0:full * P])
                            if full < len(group):
                                width = CHUNKS[group[-1]].width
                                ins = act.copy(prT[0:width, at[1] % 2, at0 + full * P:at0 + full * P + P],
                                               bank[0:width, full * P:full * P + P])
                            ins.then_inc(t_done, 1)

                copy(range(LATE))
                if (at := due(b, t, 0)):
                    i = at[0] * TB + at[1]
                    act.wait_ge(sub_done, i + 1)
                    act.activation(pr[:, t % 2, :], pr[:, t % 2, :], ACT.Exp, scale=scale).then_inc(exp_done, 1)
                copy([LATE])

            rotate(act, body, 1)


VW_PARTS = 4
assert H * D // VW_PARTS == BANK
EPS2 = 1e-6
KH = 64
PAIRS = H // 2


class Context64:

    def __init__(self, nc, a, sem, sb):
        self.a = a
        self.G = sb("a2_G", [P, B, H, J])
        self.vwf = sb("a2_vwf", [P, B, NC, D])
        self.names = ("w_in", "k_ready", "k_done", "g_ready", "g_done", "mm_ready", "mm_done", "vw_ready", "vw_done", "vw_back", "zeroed")
        self.s = {n: sem("a2_" + n) for n in self.names}
        self.vw_out = [sem(f"a2_vw_out{n}") for n in range(VW_PARTS)]

    def take(self, m, sb):
        room = m.kb[:, :, :, :].rearrange("p b h j -> p (b h j)")
        self.wk, self.wqT, self.wvT = (room[:, n * D * PAIRS:(n + 1) * D * PAIRS].rearrange("p (c d) -> p c d", c=PAIRS)
                                       for n in range(3))
        self.k2T = room[:, 3 * D * PAIRS:3 * D * PAIRS + 4 * B * J].rearrange("p (s j) -> p s j", s=4)
        self.w0 = sb("a2_w0", [P, H, D])
        self.M = m.xn[:, :, :].rearrange("p i d -> p (i d)")
        self.vw = sb("a2_vw", [J, VW_PARTS, BANK])

    def loads(self, sp):
        for t, n in ((self.wk, "wk"), (self.wqT, "wqT"), (self.wvT, "wvT"), (self.w0, "w0")):
            sp.dma_start(t[:, :, :], self.a["a2_" + n]).then_inc(self.s["w_in"], 16)

    def pool_zeros(self, pool):
        pool.memset(self.k2T[:, :, :], 0.0).then_inc(self.s["zeroed"], 1)
        pool.wait_ge(self.s["zeroed"], 1)

    def sp_work(self, sp):
        s, vw_in = self.s, self.a["vw"]
        rows, full = vw_in.rearrange("b h j d -> b (h j) d"), HJ // P

        def load(b):
            for q in self.vw_out:
                sp.wait_ge(q, 16 * (b + 1))
            sp.dma_start(self.vwf[:, b, 0:full, :], rows[b, 0:full * P, :].rearrange("(c p) d -> p c d", p=P)).then_inc(s["vw_back"], 16)
            sp.dma_start(self.vwf[0:HJ - full * P, b, full, :], rows[b, full * P:, :]).then_inc(s["vw_back"], 16)

        for b in range(B):
            for part in range(VW_PARTS):
                sp.wait_ge(s["vw_done"], b * VW_PARTS + part + 1)
                heads = slice(part * H // VW_PARTS, (part + 1) * H // VW_PARTS)
                sp.dma_start(vw_in[b, heads, :, :].rearrange("h j d -> j h d"),
                             self.vw[:, part, :].rearrange("j (h d) -> j h d", d=D)).then_inc(self.vw_out[part], 16)
            if b:
                load(b - 1)
        load(B - 1)
        sp.wait_ge(s["vw_back"], 16 * 2 * B)

    def pe_keys(self, pe, m, pairs):
        s = self.s

        def g_pair(c):
            pe.wait_ge(s["k_done"], 2 * (c + 1))
            for r in range(2):
                ge(pe, s["g_done"], 2 * c + r - 1)
                pe.matmul(m.ps[6 + r][:, 0:B * J], self.wqT[:, c, :], self.k2T[:, (2 * c + r) % 4, :], start=True, stop=True).then_inc(s["g_ready"], 1)

        pe.wait_ge(s["w_in"], 64)
        for c in pairs:
            ge(pe, s["k_done"], 2 * (c - 1))
            pe.matmul(m.ps[4 + c % 2][:, 0:B * J], self.wk[:, c, :], m.ctxT[:, :, :], start=True, stop=True).then_inc(s["k_ready"], 1)
            if c > pairs[0]:
                g_pair(c - 1)
        g_pair(pairs[-1])

    def pe_values(self, pe, m):
        s = self.s
        for h in range(H):
            if h == 0:
                pe.wait_ge(s["g_done"], H)
            ge(pe, s["mm_done"], h - 3)
            pe.matmul(m.ps[4 + h % 4][:, 0:D], self.wvT[:, h // 2, :], self.w0[:, h, :], start=True, stop=True).then_inc(s["mm_ready"], 1)
        pe.wait_ge(s["mm_done"], H)
        for n in range(B * VW_PARTS):
            b, q = n // VW_PARTS, n % VW_PARTS
            ge(pe, s["vw_done"], n - 3)
            pe.matmul(m.ps[4 + n % 4][0:J, :], m.ctxT[:, b, :], self.M[:, q * BANK:(q + 1) * BANK], start=True, stop=True).then_inc(s["vw_ready"], 1)

    def act_keys(self, act, m, pairs):
        s = self.s
        for c in (*pairs, pairs[-1] + 1):
            if c in pairs:
                act.wait_ge(s["k_ready"], c + 1)
                for r in range(2):
                    rows = slice(KH * r, KH * r + KH)
                    act.activation(self.k2T[rows, (2 * c + r) % 4, :], m.ps[4 + c % 2][rows, 0:B * J], ACT.Copy, scale=KH ** -0.5).then_inc(s["k_done"], 1)
            if c > pairs[0]:
                for h in (2 * c - 2, 2 * c - 1):
                    act.wait_ge(s["g_ready"], h + 1)
                    act.copy(self.G[:, :, h, :], m.ps[6 + h % 2][:, 0:B * J].rearrange("p (b j) -> p b j", b=B)).then_inc(s["g_done"], 1)

    def act_values(self, act, m):
        s = self.s
        for h in range(H):
            act.wait_ge(s["mm_ready"], h + 1)
            act.copy(self.M[:, h * D:(h + 1) * D], m.ps[4 + h % 4][:, 0:D]).then_inc(s["mm_done"], 1)
        act.wait_ge(s["mm_done"], H)
        for n in range(B * VW_PARTS):
            b, part = n // VW_PARTS, n % VW_PARTS
            act.wait_ge(s["vw_ready"], n + 1)
            ge(act, self.vw_out[part], 16 * b)
            act.copy(self.vw[:, part, :], m.ps[4 + n % 4][0:J, :]).then_inc(s["vw_done"], 1)


def attention64(nc, m, a, sem, sb):
    G, vwf = m.context64.G, m.context64.vwf
    gamma, beta = sb("a2_gamma", [P, D]), sb("a2_beta", [P, D])
    maski = sb("a2_maski", [P, NT, J], I32)
    m01 = sb("a2_m01", [P, NT, J])
    y = sb("a2_y", [P, NT, D])
    (q_done, s_ready, mask_applied, max_done, sub_done, exp_done, sum_done, rden_done, norm_done, t_ready,
     t_done, pv_ready, y_done, pool_pass, var_done, std_done, scale_done, scaled,
     x_biased, stats_done) = (
        sem("a2_" + n) for n in (
        "q_done", "s_ready", "mask_applied", "max_done", "sub_done", "exp_done", "sum_done",
        "rden_done", "norm_done", "t_ready", "t_done", "pv_ready", "y_done", "pool_pass", "var_done", "std_done", "scale_done",
        "scaled", "x_biased", "stats_done"))

    def loads(sp):
        m.fetch(sp.dma_start(maski[:, :, :], a["mask2"].rearrange("b (i p) j -> p (b i) j", p=P)))
        m.fetch(sp.dma_start(gamma[:, :], a["a2_gamma"]))
        m.fetch(sp.dma_start(beta[:, :], a["a2_beta"]))

    yield (loads,)

    qT = sb("a2_qT", [P, S])
    SLOTS = 4
    pr = sb("a2_pr", [P, SLOTS, HJ])
    prT = sb("a2_prT", [P, 2, NC * P])
    mx, sm, rden = (sb("a2_" + n, [P, SLOTS, H]) for n in ("mx", "sm", "rden"))
    scores = [m.ps[i][:, 0:QJ] for i in range(4)]
    PV = m.ps[6]
    hj = lambda ap: ap.rearrange("p (h j) -> p h j", h=H)
    wide = lambda ap: ap.unsqueeze(2).broadcast_to([P, H, J])

    with nc.Block() as block:
        @block.gpsimd
        def _(pool):
            def body(b, t):
                if (at := due(b, t, 2)):
                    i = at[0] * TB + at[1]
                    pool.wait_ge(rden_done, i + 1)
                    p = hj(pr[:, at[1], :])
                    pool.tensor_tensor(p, p, wide(rden[:, at[1], :]), ALU.mult).then_inc(norm_done, 1)
                if (at := due(b, t, 0)):
                    turn_queries(m, pool, b, t, qT, s_ready, q_done, pool_pass)
                    i = at[0] * TB + at[1]
                    p = hj(pr[:, at[1], :])
                    pool.wait_ge(max_done, i + 1)
                    pool.tensor_tensor(p, p, wide(mx[:, at[1], :]), ALU.subtract).then_inc(sub_done, 1)

            pool.tensor_copy(qT[:, 0:P], m.xnT[:, 0:P]).then_inc(q_done, 1)
            rotate(pool, body, 2)
            m.fetch.wait(pool)
            pool.tensor_tensor(m.x[:, :, :], m.x[:, :, :], beta[:, :].unsqueeze(1).broadcast_to([P, NT, D]), ALU.add).then_inc(x_biased, 1)
            pool.wait_ge(x_biased, 1)

        @block.tensor
        def _(pe):
            def turn(at, groups):
                i = at[0] * TB + at[1]
                if 0 in groups:
                    pe.wait_ge(norm_done, i + 1)
                for g in groups:
                    ge(pe, t_done, NG * i + g - 1)
                    for n, ch in enumerate(GROUPS[g]):
                        c = CHUNKS[ch]
                        ins = pe.transpose(m.ps[4 + (NG * at[1] + g) % 2][0:c.width, n * P:(n + 1) * P],
                                           pr[:, at[1], c.at:c.at + c.width], m.ident[:, :])
                    ins.then_inc(t_ready, 1)

            def body(b, t):
                if (at := due(b, t, 3)):
                    turn(at, [LATE])
                if (at := due(b, t, 0)):
                    i = at[0] * TB + at[1]
                    pe.wait_ge(q_done, i + 1)
                    ge(pe, mask_applied, i)
                    for r in range(4):
                        ins = pe.matmul(scores[r], qT[:, t * P:(t + 1) * P],
                                        G[:, bass.ds(b, 1), r * QH:(r + 1) * QH, :].rearrange("p b h j -> p (b h j)"), start=True, stop=True)
                    ins.then_inc(s_ready, 1)
                    if isinstance(i, int) and i < 2:
                        keep_warm(pe, m, 7, TILE_WARM)
                if (at := due(b, t, 3)):
                    i = at[0] * TB + at[1]
                    pe.wait_ge(t_done, NG * (i + 1))
                    ge(pe, y_done, i)
                    for n, c in enumerate(CHUNKS):
                        ins = pe.matmul(PV[:, 0:D], prT[0:c.width, at[1] % 2, n * P:(n + 1) * P],
                                        vwf[0:c.width, bass.ds(at[0], 1), n, :].rearrange("p b e -> p (b e)"),
                                        start=(n == 0), stop=(n == NC - 1))
                    ins.then_inc(pv_ready, 1)
                if (at := due(b, t, 2)):
                    turn(at, range(LATE))

            rotate(pe, body, 3)

        @block.vector
        def _(dve):
            m.fetch.wait(dve)
            m.dve(dve.tensor_scalar(m01[:, :, :], maski[:, :, :], 0.0, None, ALU.not_equal))
            m.dve.wait(dve)

            def body(b, t):
                tile_statistics(m, dve, due(b, t, 4), y, y_done, stats_done)
                if (at := due(b, t, 0)):
                    i = at[0] * TB + at[1]
                    p = hj(pr[:, t, :])
                    dve.wait_ge(s_ready, i + 1)
                    ge(dve, t_ready, NG * (i - 3))
                    for r in range(4):
                        ins = dve.scalar_tensor_tensor(p[:, r * QH:(r + 1) * QH, :], scores[r].rearrange("p (h j) -> p h j", h=QH),
                                                       -EPS2, m01[:, bass.ds(i, 1), :].broadcast_to([P, QH, J]), ALU.add, ALU.mult)
                    ins.then_inc(mask_applied, 1)
                    dve.wait_ge(mask_applied, i + 1)
                    dve.tensor_reduce(mx[:, t, :], p, AX.X, ALU.max).then_inc(max_done, 1)
                if (at := due(b, t, 1)):
                    i = at[0] * TB + at[1]
                    dve.wait_ge(exp_done, i + 1)
                    dve.tensor_reduce(sm[:, at[1], :], hj(pr[:, at[1], :]), AX.X, ALU.add).then_inc(sum_done, 1)
                    dve.wait_ge(sum_done, i + 1)
                    dve.reciprocal(rden[:, at[1], :], sm[:, at[1], :]).then_inc(rden_done, 1)
                if (at := due(b, t, 3)):
                    i = at[0] * TB + at[1]
                    dve.wait_ge(pv_ready, i + 1)
                    yi, xi = (z[:, bass.ds(i, 1), :].rearrange("p i d -> p (i d)") for z in (y, m.xn))
                    dve.tensor_tensor(yi, xi, PV[:, 0:D], ALU.add).then_inc(y_done, 1)

            rotate(dve, body, 4)
            dve.wait_ge(stats_done, NT)

        @block.scalar
        def _(act):
            def copy(at, groups):
                i = at[0] * TB + at[1]
                for g in groups:
                    group = GROUPS[g]
                    act.wait_ge(t_ready, NG * i + g + 1)
                    if g == 0:
                        ge(act, pv_ready, i - 1)
                    bank, at0 = m.ps[4 + (NG * at[1] + g) % 2], P * group[0]
                    full = sum(CHUNKS[ch].width == P for ch in group)
                    ins = act.copy(prT[:, at[1] % 2, at0:at0 + full * P], bank[:, 0:full * P])
                    if full < len(group):
                        width = CHUNKS[group[-1]].width
                        ins = act.copy(prT[0:width, at[1] % 2, at0 + full * P:at0 + full * P + P],
                                       bank[0:width, full * P:full * P + P])
                    ins.then_inc(t_done, 1)

            def body(b, t):
                if (at := due(b, t, 3)):
                    copy(at, [LATE])
                if (at := due(b, t, 1)):
                    i = at[0] * TB + at[1]
                    act.wait_ge(sub_done, i + 1)
                    act.activation(pr[:, at[1], :], pr[:, at[1], :], ACT.Exp).then_inc(exp_done, 1)
                if (at := due(b, t, 2)):
                    copy(at, range(LATE))

            rotate(act, body, 3)

    with nc.Block() as block:
        @block.vector
        def _(dve):
            for i in range(NT):
                m.dve(dve.bn_aggr(m.mv[:, i, :], m.stats[:, i, :]))
            m.dve.wait(dve)
            dve.tensor_scalar(m.var[:, :], m.mv[:, :, 1], D / (D - 1.0), None, ALU.mult).then_inc(var_done, 1)
            dve.wait_ge(std_done, 1)
            m.dve(dve.tensor_scalar(m.std[:, :], m.std[:, :], EPS2, None, ALU.add))
            m.dve.wait(dve)
            m.dve(dve.reciprocal(m.rstd[:, :], m.std[:, :]))
            m.dve.wait(dve)
            m.dve(dve.scalar_tensor_tensor(m.nmr[:, :], m.mv[:, :, 0], -1.0, m.rstd[:, :], ALU.mult, ALU.mult))
            m.dve.wait(dve)
            dve.sem_inc(scale_done, 1)
            for i in DVE_TILES:
                m.dve(dve.tensor_scalar(y[:, i, :], y[:, i, :], m.rstd[:, i:i + 1], m.nmr[:, i:i + 1], ALU.mult, ALU.add))
            m.dve.wait(dve)
            for b in range(B):
                dve.wait_ge(scaled, sum(i < (b + 1) * TB for i in ACT_TILES))
                yb, xb = (z[:, b * TB:(b + 1) * TB, :] for z in (y, m.x))
                m.dve(dve.tensor_tensor(yb, yb, gamma[:, :].unsqueeze(1).broadcast_to([P, TB, D]), ALU.mult))
                m.dve.wait(dve)
                m.dve(dve.tensor_tensor(xb, xb, yb, ALU.add))
                m.dve.wait(dve)
                for i in range(b * TB, (b + 1) * TB):
                    m.dve(dve.bn_stats(m.stats[:, i, :], m.x[:, i, :]))

        @block.scalar
        def _(act):
            act.wait_ge(var_done, 1)
            act.activation(m.std[:, :], m.var[:, :], ACT.Sqrt).then_inc(std_done, 1)
            act.wait_ge(scale_done, 1)
            for i in ACT_TILES:
                act.activation(y[:, i, :], y[:, i, :], ACT.Identity, bias=m.nmr[:, i:i + 1], scale=m.rstd[:, i:i + 1]).then_inc(scaled, 1)


HID = 384
HC = HID // P
QMAX = 2.0 ** 15 - 1
TINY = 1e-12


EARLY_PAIRS, LATE_PAIRS = range(0, 2), range(2, PAIRS)


def ffn1(nc, m, a, sem, sb):
    w = sb("f1_w", [P, 3 * HC, P])
    wT = sb("f1_wT", [P, 3 * HC, P])
    NBLK = 3 * HC * 4
    ws, winv = sb("f1_ws", [P, NBLK]), sb("f1_winv", [P, NBLK])
    up, gate, sig = (sb("f1_" + n, [P, HC, N]) for n in ("up", "gate", "sig"))
    (w_in, w_done, wT_ready, wT_done, most_ready, most_done, xq_done, mm_ready, mm_done, scaled, rounded, gate_done,
     sig_ready, sig_rounded, up_rounded, up_done, o_done, down_ready) = (
        sem("f1_" + n) for n in (
        "w_in", "w_done", "wT_ready", "wT_done", "most_ready", "most_done", "xq_done", "mm_ready", "mm_done",
        "scaled", "rounded", "gate_done", "sig_ready", "sig_rounded", "up_rounded", "up_done", "o_done", "down_ready"))
    XQ, UP, GATE, G2, OUT = range(5)
    part = sb("f1_part", [P, 5, 12])
    most, over, sc, inv = (sb("f1_" + n, [P, 5]) for n in ("most", "over", "sc", "inv"))
    scug = sb("f1_scug", [P, 1])
    col = lambda t, q: t[:, q:q + 1]
    m.context64.take(m, sb)

    def loads(sp):
        for n, part_name in enumerate(("f1_up", "f1_gate", "f1_down")):
            sp.dma_start(w[:, n * HC:(n + 1) * HC, :], a[part_name]).then_inc(w_in, 16)
        m.context64.loads(sp)

    yield loads, nothing, nothing, m.context64.pool_zeros

    with nc.Block() as block:
        @block.sync
        def _(sp):
            m.context64.sp_work(sp)

        @block.gpsimd
        def _(pool):
            for n, (q, count) in enumerate(((XQ, 1), (UP, 2), (G2, 1), (OUT, 1))):
                pool.wait_ge(most_ready, n + 1)
                pool.partition_all_reduce(over[:, q:q + count], most[:, q:q + count], P, RED.max).then_inc(most_done, 1)
                if n == 1:
                    pool.wait_ge(scaled, 1)
                    for c in range(HC):
                        pool.tensor_scalar(up[:, c, :], up[:, c, :], col(inv, UP), MAGIC, ALU.mult, ALU.add).then_inc(up_rounded, 1)
                    for c in range(HC):
                        pool.wait_ge(up_rounded, c + 1)
                        pool.tensor_scalar(up[:, c, :], up[:, c, :], 1.0, -MAGIC, ALU.mult, ALU.add).then_inc(up_rounded, 1)
                        pool.wait_ge(up_rounded, HC + c + 1)
                        pool.tensor_scalar(up[:, c, :], up[:, c, :], col(sc, UP), 0.0, ALU.mult, ALU.add).then_inc(up_done, 1)

        @block.tensor
        def _(pe):
            m.context64.pe_keys(pe, m, EARLY_PAIRS)
            pe.wait_ge(w_done, 1)
            for n in range(3 * HC):
                ins = pe.transpose(m.ps[n // 4][:, n % 4 * P:n % 4 * P + P], w[:, n, :], m.ident[:, :])
            ins.then_inc(wT_ready, 1)
            pe.wait_ge(m.context64.s["g_done"], 2 * (EARLY_PAIRS[-1] + 1))
            pe.wait_ge(wT_done, 3)
            for n in range(8 * HC):
                q, mat = n // (2 * HC), n % (2 * HC)
                pe.wait_ge(xq_done, q + 1)
                ge(pe, mm_done, n - 7)
                pe.matmul(m.ps[n % 8][:, :], wT[:, mat, :], m.xnT[:, q * BANK:(q + 1) * BANK], start=True, stop=True).then_inc(mm_ready, 1)
            pe.wait_ge(mm_done, 8 * HC)
            m.context64.pe_keys(pe, m, LATE_PAIRS)
            m.context64.pe_values(pe, m)
            for i in range(NT):
                if i % 4 == 0:
                    pe.wait_ge(o_done, i // 4 + 1)
                for c in range(HC):
                    ins = pe.matmul(m.ps[i // 4][:, i % 4 * P:i % 4 * P + P], sig[:, c, i * P:(i + 1) * P], wT[:, 2 * HC + c, :],
                                    start=(c == 0), stop=(c == HC - 1))
                if i % 4 == 3:
                    ins.then_inc(down_ready, 1)

        @block.scalar
        def _(act):
            m.context64.act_keys(act, m, EARLY_PAIRS)
            act.wait_ge(wT_ready, 1)
            for n in range(0, 3 * HC, 4):
                k = min(4, 3 * HC - n)
                act.copy(wT[:, n:n + k, :], m.ps[n // 4][:, 0:k * P].rearrange("p (n e) -> p n e", n=k)).then_inc(wT_done, 1)
            for n in range(8 * HC):
                q, mat = n // (2 * HC), n % (2 * HC)
                act.wait_ge(mm_ready, n + 1)
                act.copy((up, gate)[mat // HC][:, mat % HC, q * BANK:(q + 1) * BANK], m.ps[n % 8][:, :]).then_inc(mm_done, 1)
            act.wait_ge(scaled, 1)
            for c in range(HC):
                act.activation(gate[:, c, :], gate[:, c, :], ACT.Copy, scale=col(inv, GATE), bias=MAGIC).then_inc(rounded, 1)
            for c in range(HC):
                act.wait_ge(gate_done, c + 1)
                act.activation(sig[:, c, :], gate[:, c, :], ACT.Sigmoid).then_inc(sig_ready, 1)
                act.wait_ge(sig_ready, c + 1)
                act.activation(sig[:, c, :], sig[:, c, :], ACT.Copy, scale=65536.0, bias=MAGIC).then_inc(sig_rounded, 1)
            m.context64.act_keys(act, m, LATE_PAIRS)
            act.wait_ge(scaled, 2)
            for c in range(HC):
                act.activation(gate[:, c, :], gate[:, c, :], ACT.Copy, scale=col(inv, G2), bias=MAGIC).then_inc(rounded, 1)
            m.context64.act_values(act, m)
            act.wait_ge(scaled, 3)
            for q in range(4):
                o = sig[:, :, q * BANK:(q + 1) * BANK]
                act.activation(o, o, ACT.Copy, scale=col(inv, OUT), bias=MAGIC).then_inc(rounded, 1)

        @block.vector
        def _(dve):
            def step(ins):
                m.dve(ins)
                m.dve.wait(dve)

            def scale(q, n, count=1):
                at = slice(q, q + count)
                dve.wait_ge(most_done, n)
                step(dve.tensor_scalar(sc[:, at], over[:, at], 1.0 / QMAX, TINY, ALU.mult, ALU.max))
                step(dve.reciprocal(inv[:, at], sc[:, at]))

            dve.tensor_reduce(col(most, XQ), m.xnT[:, 0:N], AX.X, ALU.max, apply_absolute_value=True).then_inc(most_ready, 1)
            dve.wait_ge(w_in, 48)
            wb = w[:, :, :].rearrange("p n (k e) -> p (n k) e", e=32)
            wide = lambda t: t[:, :].unsqueeze(2).broadcast_to([P, NBLK, 32])
            step(dve.tensor_reduce(ws[:, :], wb, AX.X, ALU.max, apply_absolute_value=True))
            step(dve.tensor_scalar(ws[:, :], ws[:, :], 1.0 / 7, TINY, ALU.mult, ALU.max))
            step(dve.reciprocal(winv[:, :], ws[:, :]))
            step(dve.tensor_tensor(wb, wb, wide(winv), ALU.mult))
            step(dve.tensor_scalar(wb, wb, MAGIC, MAGIC, ALU.add, ALU.subtract))
            dve.tensor_tensor(wb, wb, wide(ws), ALU.mult).then_inc(w_done, 1)
            scale(XQ, 1)
            for q in range(4):
                xq = m.xnT[:, q * BANK:(q + 1) * BANK]
                step(dve.tensor_scalar(xq, xq, col(inv, XQ), MAGIC, ALU.mult, ALU.add))
                dve.tensor_scalar(xq, xq, MAGIC, col(sc, XQ), ALU.subtract, ALU.mult).then_inc(xq_done, 1)
            for n in range(8 * HC):
                q, mat = n // (2 * HC), n % (2 * HC)
                dve.wait_ge(mm_done, n + 1)
                m.dve(dve.tensor_reduce(part[:, UP + mat // HC, q * HC + mat % HC:q * HC + mat % HC + 1],
                                        (up, gate)[mat // HC][:, mat % HC, q * BANK:(q + 1) * BANK], AX.X, ALU.max,
                                        apply_absolute_value=True))
            m.dve.wait(dve)
            dve.tensor_reduce(most[:, UP:UP + 2], part[:, UP:UP + 2, :], AX.X, ALU.max).then_inc(most_ready, 1)
            scale(UP, 2, 2)
            dve.sem_inc(scaled, 1)
            for c in range(HC):
                dve.wait_ge(rounded, c + 1)
                dve.tensor_scalar(gate[:, c, :], gate[:, c, :], MAGIC, col(sc, GATE), ALU.subtract, ALU.mult).then_inc(gate_done, 1)
            for c in range(HC):
                dve.wait_ge(sig_rounded, c + 1)
                step(dve.tensor_scalar(sig[:, c, :], sig[:, c, :], MAGIC, 65535.0, ALU.subtract, ALU.min))
                step(dve.scalar_tensor_tensor(gate[:, c, :], sig[:, c, :], 1 / 65536.0, gate[:, c, :], ALU.mult, ALU.mult))
                step(dve.tensor_reduce(part[:, G2, c:c + 1], gate[:, c, :], AX.X, ALU.max, apply_absolute_value=True))
            dve.tensor_reduce(col(most, G2), part[:, G2, 0:HC], AX.X, ALU.max).then_inc(most_ready, 1)
            scale(G2, 3)
            dve.sem_inc(scaled, 1)
            for c in range(HC):
                dve.wait_ge(rounded, HC + c + 1)
                step(dve.tensor_scalar(gate[:, c, :], gate[:, c, :], MAGIC, col(sc, G2), ALU.subtract, ALU.mult))
                dve.wait_ge(up_done, c + 1)
                step(dve.tensor_tensor(sig[:, c, :], gate[:, c, :], up[:, c, :], ALU.mult))
                step(dve.tensor_reduce(part[:, OUT, c:c + 1], sig[:, c, :], AX.X, ALU.max, apply_absolute_value=True))
            dve.tensor_reduce(col(most, OUT), part[:, OUT, 0:HC], AX.X, ALU.max).then_inc(most_ready, 1)
            scale(OUT, 4)
            dve.sem_inc(scaled, 1)
            for q in range(4):
                o = sig[:, :, q * BANK:(q + 1) * BANK]
                dve.wait_ge(rounded, 2 * HC + q + 1)
                dve.tensor_scalar(o, o, MAGIC, col(sc, OUT), ALU.subtract, ALU.mult).then_inc(o_done, 1)
            for q in range(4):
                dve.wait_ge(down_ready, q + 1)
                xq = m.x[:, 4 * q:4 * q + 4, :]
                m.dve(dve.tensor_tensor(xq, xq, m.ps[q][:, :].rearrange("p (t d) -> p t d", t=4), ALU.add))
            m.dve.wait(dve)


def build(nc, a):
    with ExitStack() as ctx:
        def sem(name):
            return ctx.enter_context(nc.semaphore(name))

        def sb(name, shape, dt=F32):
            return ctx.enter_context(nc.sbuf_tensor(name, shape, dt))

        m = Machine()
        m.all_banks = ctx.enter_context(nc.psum_tensor("banks", [P, 8, BANK], F32))
        m.ps = [m.all_banks[:, i, :] for i in range(8)]
        m.x, m.xn = sb("x", [P, NT, D]), sb("xn", [P, NT, D])
        m.xnT = sb("xnT", [P, N + P])
        m.packs = {n: sb(n, [P, sum(width for _, width in parts)]) for n, parts in PACKS.items()}
        m.narrow = sb("narrow_b", [P, sum(width for _, width in PACKS["narrow"])], BF16)
        m.small = {}
        for pack, parts in PACKS.items():
            at = 0
            for n, width in parts:
                m.small[n] = (m.narrow if pack == "narrow" else m.packs[pack])[:, at:at + width]
                at += width
        m.ctxT = m.small["ctxT"].rearrange("p (b j) -> p b j", b=B)
        m.ctxT3 = m.small["ctxT3"].rearrange("p (b j) -> p b j", b=B)
        m.ident, m.w0T, m.diag0, m.tri, m.onesb, m.iota8, m.iota128, m.restart, m.one8 = (
            m.small[n] for n in ("ident", "w0T", "diag0", "tri", "onesb", "iota8", "iota128", "restart", "one8"))
        m.have_stats = False
        m.zero = sb("zero", [P, D])
        m.stats, m.mv = sb("stats", [P, NT, 6]), sb("mv", [P, NT, 2])
        m.var, m.std, m.rstd, m.nmr = (sb(n, [P, NT]) for n in ("var", "std", "rstd", "nmr"))
        m.dve = Chain(sem("dve_chain"))
        m.ln_var, m.ln_std, m.ln_xn, m.ln_turned, m.ln_copied, m.ln_copied_act = (
            sem("ln_" + n) for n in ("var", "std", "xn", "turned", "copied", "copied_act"))
        m.ln_scale, m.ln_xn_act = (sem("ln_" + n) for n in ("scale", "xn_act"))
        m.x_in, m.early_in = [sem(f"x_in{b}") for b in range(B)], sem("early_in")
        m.fetch = Fetch(sem("fetched"))
        m.kT = sb("kT", [P, B, J])
        m.kb = sb("kb", [P, B, H, J])
        m.vf = sb("vf", [P, B, NC, CH * (HD + 1)])
        m.vraw = sb("vraw", [P, B, NC * CH * HD])
        m.context8 = dict(a1=Context8(m, sem, "a1", m.small["wkT"], m.small["bk"], m.small["wvT"], m.small["bv"]),
                          a3=Context8(m, sem, "a3", None, None, m.ident, None))
        m.context64 = Context64(nc, a, sem, sb)

        used = []

        def stage(number, f, **kw):
            own = []

            def own_sem(name):
                own.append(nc.alloc_semaphore(name=name))
                return own[-1]

            with ExitStack() as inner:
                steps = f(nc, m, a, own_sem, lambda name, shape, dt=F32: inner.enter_context(nc.sbuf_tensor(name, shape, dt)), **kw)
                layer_norm(nc, m, number, *next(steps))
                if used:
                    nc.clear_and_free_semaphores(used)
                for _ in steps:
                    pass
            m.have_stats = f in (attention8, attention64)
            return own

        for number, (f, kw) in enumerate(STAGES):
            used = stage(number, f, **kw)


GMAX = 40
PACKS = dict(
    early=[("ident", P), ("w0T", P), ("diag0", 1), ("ctxT", B * J)],
    later=[("ctxT3", 3 * B * J), ("m0_router", E), ("m0_rbias", E), ("m2_router", E), ("m3_router", E), ("wqT", P), ("wkT", P),
           ("wvT", P), ("woT", P), ("bq", 1), ("bk", 1), ("bv", NC * CH * HD), ("bo", P), ("woutT", P), ("bout", P),
           ("vmask", NC * CH), ("qmask", H), ("iota8", E), ("iota128", NT), ("iotag", GMAX), ("tile1", 2 * NT),
           ("part", 1), ("restart", E * NT), ("one8", E)],
    narrow=[("identb", P), ("tri", P), ("onesb", P), ("iotar", P)],
)
STAGES = [
    (attention0, {}),
    (moe, dict(name="m0", ahead="a1", blocks=24, topk=1, cap=0, biased=True, gated=False, act_fn=ACT.Relu, x_stage=False, last=False)),
    (attention8, dict(name="a1", scale=HD ** -0.5, projected=True, masked=False)),
    (ffn1, {}),
    (attention64, {}),
    (moe, dict(name="m2", ahead="a3", blocks=GMAX, topk=2, cap=int(1.25 * N * 2 / E) + 1, biased=False, gated=False, act_fn=ACT.Silu, x_stage=True, last=False)),
    (attention8, dict(name="a3", scale=HD ** -0.5, projected=False, masked=True)),
    (moe, dict(name="m3", ahead=None, blocks=GMAX, topk=2, cap=0, biased=False, gated=True, act_fn=ACT.Silu, x_stage=False, last=True)),
]


def arrays(v):
    c = np.ascontiguousarray
    ctx = np.asarray(v["ctx_1024"])
    rows = lambda w, n: c(np.broadcast_to(w, (n,) + w.shape))
    chunked = lambda w: c(w.reshape(w.shape[0], FC, P, D).transpose(0, 2, 1, 3).reshape(w.shape[0], P, FC * D))
    pairs = lambda w: w.reshape(PAIRS, P, D).transpose(1, 0, 2)

    def apart(w):
        z = np.zeros((PAIRS, 2, KH, 2, D), w.dtype)
        for r in range(2):
            z[:, r, :, r, :] = w.reshape(PAIRS, 2, KH, D)[:, r]
        return z.reshape(PAIRS, P, 2, D).transpose(1, 0, 2, 3).reshape(P, H, D)

    def vmask():
        k = np.zeros((P, NC, CH), np.float32)
        for n, ch in enumerate(CHUNKS):
            r = np.arange(ch.width)
            k[r, n, (ch.at + r) // J - ch.h0] = 1
        return k.reshape(P, NC * CH)

    o = dict(
        x=v["x"], ctx=ctx, ctxT=ctx.transpose(2, 0, 1), ctxT3=np.tile(ctx.transpose(2, 0, 1), (1, 1, 3)), mask0=v["mask_BxS2_if1"],
        w0T=c(v["L0_xattn_W"].T), diag0=c(v["L0_xattn_diagonal"].reshape(P, 1)),
        m0_router=v["L0_ffn_w_gate"], m0_rbias=rows(v["L0_ffn_b_gate"], P),
        m0_w1=v["L0_ffn_W1"], m0_w2=chunked(v["L0_ffn_W2"]),
        m0_b1=v["L0_ffn_b1"].reshape(E, FC, P).transpose(0, 2, 1),
        m0_b2=c(np.broadcast_to(v["L0_ffn_b2"][:, None, :], (E, P, D))),
        m2_router=c(v["L2_ffn_router_w"].T), m3_router=c(v["L3_ffn_gate_w"].T),
        wqT=c(v["L1_xattn_wq"].T), wkT=c(v["L1_xattn_wk"].T), wvT=c(v["L1_xattn_wv"].T), woT=c(v["L1_xattn_wo"].T),
        bq=v["L1_xattn_bq"][:, None], bk=v["L1_xattn_bk"][:, None], bv=rows(np.concatenate([v["L1_xattn_bv"][c.h0 * HD:(c.h0 + CH) * HD] for c in CHUNKS]), P), bo=rows(v["L1_xattn_bo"], P),
        woutT=c(v["L3_xattn_W_out"].T), bout=rows(v["L3_xattn_b_out"], P), mask3=v["mask_Bx1xSxS2_ik1"][:, 0],
        mask2=v["mask_BxSxS2_ik1"], a2_wk=v["L2_xattn_w_k"].reshape(D, PAIRS, P),
        a2_wqT=pairs(v["L2_xattn_w_q"].T), a2_wvT=pairs(v["L2_xattn_w_v"].T), a2_w0=apart(v["L2_xattn_w_0"]),
        a2_gamma=rows(v["L2_xattn_gamma"], P), a2_beta=rows(v["L2_xattn_beta"], P),
        f1_up=v["L1_ffn_w_up"].reshape(HC, P, D).transpose(1, 0, 2), f1_gate=v["L1_ffn_w_gate"].reshape(HC, P, D).transpose(1, 0, 2),
        f1_down=v["L1_ffn_w_down"].reshape(P, HC, P),
        m2_w1=v["L2_ffn_w1"], m2_w2=chunked(v["L2_ffn_w2"]),
        m3_w1=c(v["L3_ffn_w1"].transpose(0, 2, 1)), m3_w3=c(v["L3_ffn_w3"].transpose(0, 2, 1)),
        m3_w2=chunked(v["L3_ffn_w2"].transpose(0, 2, 1)),
        vmask=vmask(), qmask=(np.arange(P)[:, None] // HD == np.arange(H)).astype(np.float32),
        identb=np.eye(P, dtype=np.float32),
        ident=np.eye(P, dtype=np.float32), tri=np.triu(np.ones((P, P), np.float32), 1), onesb=np.ones((P, P), np.float32),
        iota8=rows(np.arange(E, dtype=np.float32), P), iota128=rows(np.arange(NT, dtype=np.float32) * P, P),
        iotag=rows(np.arange(GMAX, dtype=np.float32), P), iotar=rows(np.arange(P, dtype=np.float32), P),
        tile1=rows(np.arange(1, 2 * NT + 1, dtype=np.float32), P), part=np.arange(P, dtype=np.float32)[:, None], restart=rows((np.arange(E * NT) % NT != 0).astype(np.float32), P),
        one8=np.ones((P, E), np.float32),
    )
    for pack, parts in PACKS.items():
        o[pack] = np.concatenate([np.asarray(o.pop(n)).reshape(P, width) for n, width in parts], axis=1)
    return {k: c(np.asarray(x)) for k, x in o.items()}


def kernel(**inputs):
    import concourse.bacc as bacc
    from concourse.bass_utils import run_bass_kernel_spmd

    nc = bacc.Bacc("TRN2", target_bir_lowering=False, num_devices=1)
    given = arrays({k: np.asarray(v) for k, v in inputs.items()})
    a = {k: nc.dram_tensor("in_" + k, v.shape, mybir.dt.from_np(v.dtype), kind="ExternalInput").ap() for k, v in given.items()}
    a["out"] = nc.dram_tensor("out", (B, S, D), F32, kind="ExternalOutput").ap()
    a["pairs_in"] = nc.dram_tensor("pairs_in", (2 * N, D), F32, kind="Internal").ap()
    a["vw"] = nc.dram_tensor("value_rows", (B, H, J, D), F32, kind="Internal").ap()
    for name, k in (("m0", 1), ("m2", 2), ("m3", 2)):
        a[name + "_pairs_out"] = nc.dram_tensor(name + "_pairs_out", (k * N, D), F32, kind="Internal").ap()
    build(nc, a)
    result = run_bass_kernel_spmd(nc, [{"in_" + k: v for k, v in given.items()}], core_ids=[0])
    return result.results[0]["out"]
```
